# Optimizing a Trainium2 kernel written in Bass

```python
import numpy as np
import jax
import jax.numpy as jnp

def _softmax(x, axis=-1):
    return jax.nn.softmax(x, axis=axis)

def _gelu(x):
    return jax.nn.gelu(x, approximate=True)

def _silu(x):
    return jax.nn.silu(x)

def _sigmoid(x):
    return jax.nn.sigmoid(x)

def _layernorm(x, axis=-1, eps=1e-05):
    m = jnp.mean(x, axis=axis, keepdims=True)
    v = jnp.var(x, axis=axis, keepdims=True)
    return (x - m) / jnp.sqrt(v + eps)

def _scatter_add(tgt, idx, src, axis=0):
    return tgt.at[idx].add(src)

def _segment_sum(src, seg, n):
    return jax.ops.segment_sum(src, seg, n)
kernel_name = 'mk_cond_seq_d2_seqx_r4_569138'

def setup_inputs(seed: int=0):
    np.random.seed(seed)
    _w = jnp.asarray

    def _rec_inputs():
        import jax
        import jax.numpy as jnp
        _rk = jax.random.key(seed)
        x = -0.0003482 + 1 * jax.random.normal(jax.random.fold_in(_rk, 1), (32, 256, 288), jnp.float32)
        _lenS = 256 - jax.random.randint(jax.random.fold_in(_rk, 7), (32,), 0, max(1, 256 // 4) + 1, jnp.int32)
        _lenS2 = 256 - jax.random.randint(jax.random.fold_in(_rk, 8), (32,), 0, max(1, 256 // 4) + 1, jnp.int32)
        cond_1152 = 0.00257642 + 1.0011 * jax.random.normal(jax.random.fold_in(_rk, 11), (32, 288), jnp.float32)
        return (x, cond_1152)
    x, cond_1152 = _rec_inputs()

    def _L0_cond_setup():
        import jax, jax.numpy as jnp
        import numpy as np
        from jax.scipy.linalg import expm
        N, D, COND_DIM = (288, 64, 288)
        B, T = (16, 256)

        def _rotation(cond, W, b):
            v = jax.nn.silu(cond) @ W.T + b
            iu, ju = jnp.triu_indices(D, k=1)
            A = jnp.zeros((cond.shape[0], D, D), dtype=v.dtype)
            A = A.at[:, iu, ju].set(v).at[:, ju, iu].set(-v)
            return expm(A)
        key = jax.random.key(seed)
        k1, k2, k3, k4, k5 = jax.random.split(key, 5)
        x = jax.random.normal(k1, (B, T, N), dtype=jnp.float32)
        cond = jax.random.normal(k2, (B, COND_DIM), dtype=jnp.float32)
        P = jax.random.normal(k3, (N, D), dtype=jnp.float32)
        n_skew = D * (D - 1) // 2
        bound = 1.0 / np.sqrt(COND_DIM)
        W = jax.random.uniform(k4, (n_skew, COND_DIM), minval=-bound, maxval=bound, dtype=jnp.float32)
        b = jax.random.uniform(k5, (n_skew,), minval=-bound, maxval=bound, dtype=jnp.float32)
        return {'x': x, 'cond': cond, 'P': P, 'W': W, 'b': b}
    _L0_cond_all = _L0_cond_setup()
    _L0_cond_in = {k: v for k, v in _L0_cond_all.items() if k in ('P', 'W', 'b')}
    del _L0_cond_all

    def _L1_cond_setup():
        import jax, jax.numpy as jnp
        import numpy as np
        DIM = 288
        HEADS = 16
        HEAD_DIM = DIM // HEADS
        HIDDEN = int(DIM * 4.0)
        EPS = 1e-12

        def rmsnorm(x, g, d):
            n = jnp.linalg.norm(x, axis=-1, keepdims=True)
            return x / jnp.maximum(n, EPS) * d ** 0.5 * g

        def modulate(x, scale, shift):
            return x * (1.0 + scale[:, None, :]) + shift[:, None, :]
        key = jax.random.key(seed)
        ks = jax.random.split(key, 12)
        B, N = (8, 256)
        s = 0.02
        return {'x': jax.random.normal(ks[0], (B, N, DIM), jnp.float32), 'c': jax.random.normal(ks[1], (B, DIM), jnp.float32), 'g1': jnp.ones((1,), jnp.float32), 'g2': jnp.ones((1,), jnp.float32), 'qkv_w': jax.random.normal(ks[2], (3 * DIM, DIM), jnp.float32) * s, 'qkv_b': jnp.zeros((3 * DIM,), jnp.float32), 'qg': jnp.ones((1,), jnp.float32), 'kg': jnp.ones((1,), jnp.float32), 'proj_w': jax.random.normal(ks[3], (DIM, DIM), jnp.float32) * s, 'proj_b': jnp.zeros((DIM,), jnp.float32), 'fc1_w': jax.random.normal(ks[4], (HIDDEN, DIM), jnp.float32) * s, 'fc1_b': jnp.zeros((HIDDEN,), jnp.float32), 'fc2_w': jax.random.normal(ks[5], (DIM, HIDDEN), jnp.float32) * s, 'fc2_b': jnp.zeros((DIM,), jnp.float32), 'ada_w': jax.random.normal(ks[6], (6 * DIM, DIM), jnp.float32) * s, 'ada_b': jnp.zeros((6 * DIM,), jnp.float32)}
    _L1_cond_all = _L1_cond_setup()
    _L1_cond_in = {k: v for k, v in _L1_cond_all.items() if k in ('g1', 'g2', 'qkv_w', 'qkv_b', 'qg', 'kg', 'proj_w', 'proj_b', 'fc1_w', 'fc1_b', 'fc2_w', 'fc2_b', 'ada_w', 'ada_b')}
    del _L1_cond_all
    return {'x': x, 'cond_1152': cond_1152, 'L0_cond_P': _L0_cond_in['P'], 'L0_cond_W': _L0_cond_in['W'], 'L0_cond_b': _L0_cond_in['b'], 'L1_cond_g1': _L1_cond_in['g1'], 'L1_cond_g2': _L1_cond_in['g2'], 'L1_cond_qkv_w': _L1_cond_in['qkv_w'], 'L1_cond_qkv_b': _L1_cond_in['qkv_b'], 'L1_cond_qg': _L1_cond_in['qg'], 'L1_cond_kg': _L1_cond_in['kg'], 'L1_cond_proj_w': _L1_cond_in['proj_w'], 'L1_cond_proj_b': _L1_cond_in['proj_b'], 'L1_cond_fc1_w': _L1_cond_in['fc1_w'], 'L1_cond_fc1_b': _L1_cond_in['fc1_b'], 'L1_cond_fc2_w': _L1_cond_in['fc2_w'], 'L1_cond_fc2_b': _L1_cond_in['fc2_b'], 'L1_cond_ada_w': _L1_cond_in['ada_w'], 'L1_cond_ada_b': _L1_cond_in['ada_b']}

def reference(x, cond_1152, L0_cond_P, L0_cond_W, L0_cond_b, L1_cond_g1, L1_cond_g2, L1_cond_qkv_w, L1_cond_qkv_b, L1_cond_qg, L1_cond_kg, L1_cond_proj_w, L1_cond_proj_b, L1_cond_fc1_w, L1_cond_fc1_b, L1_cond_fc2_w, L1_cond_fc2_b, L1_cond_ada_w, L1_cond_ada_b):
    import jax
    import jax.numpy as jnp

    def _L0_cond_ref(x, cond, P, W, b):
        import jax, jax.numpy as jnp
        import numpy as np
        from jax.scipy.linalg import expm
        N, D, COND_DIM = (288, 64, 288)
        B, T = (16, 256)

        def _rotation(cond, W, b):
            v = jax.nn.silu(cond) @ W.T + b
            iu, ju = jnp.triu_indices(D, k=1)
            A = jnp.zeros((cond.shape[0], D, D), dtype=v.dtype)
            A = A.at[:, iu, ju].set(v).at[:, ju, iu].set(-v)
            return expm(A)
        U, _ = jnp.linalg.qr(P)
        R = _rotation(cond, W, b)
        z = jnp.einsum('btn,nd->btd', x, U)
        z_rot = jnp.einsum('btd,bde->bte', z, R)
        x_rot = x + jnp.einsum('btd,nd->btn', z_rot - z, U)
        return x_rot

    def _L1_cond_ref(x, c, g1, g2, qkv_w, qkv_b, qg, kg, proj_w, proj_b, fc1_w, fc1_b, fc2_w, fc2_b, ada_w, ada_b):
        import jax, jax.numpy as jnp
        import numpy as np
        DIM = 288
        HEADS = 16
        HEAD_DIM = DIM // HEADS
        HIDDEN = int(DIM * 4.0)
        EPS = 1e-12

        def rmsnorm(x, g, d):
            n = jnp.linalg.norm(x, axis=-1, keepdims=True)
            return x / jnp.maximum(n, EPS) * d ** 0.5 * g

        def modulate(x, scale, shift):
            return x * (1.0 + scale[:, None, :]) + shift[:, None, :]
        B, N, D = x.shape
        mod = jax.nn.silu(c) @ ada_w.T + ada_b
        shift_msa, scale_msa, gate_msa, shift_mlp, scale_mlp, gate_mlp = jnp.split(mod, 6, axis=-1)
        gate_msa = jnp.tanh(gate_msa)
        gate_mlp = jnp.tanh(gate_mlp)
        h = modulate(rmsnorm(x, g1, D), scale_msa, shift_msa)
        qkv = h @ qkv_w.T + qkv_b
        qkv = qkv.reshape(B, N, 3, HEADS, HEAD_DIM).transpose(2, 0, 3, 1, 4)
        q, k, v = (qkv[0], qkv[1], qkv[2])
        q = rmsnorm(q, qg, HEAD_DIM)
        k = rmsnorm(k, kg, HEAD_DIM)
        q = q * HEAD_DIM ** (-0.5)
        attn = jax.nn.softmax(jnp.einsum('bhqd,bhkd->bhqk', q, k), axis=-1)
        o = jnp.einsum('bhqk,bhkd->bhqd', attn, v)
        o = o.transpose(0, 2, 1, 3).reshape(B, N, D)
        o = o @ proj_w.T + proj_b
        x = x + gate_msa[:, None, :] * o
        h2 = modulate(rmsnorm(x, g2, D), scale_mlp, shift_mlp)
        m = jax.nn.gelu(h2 @ fc1_w.T + fc1_b, approximate=True) @ fc2_w.T + fc2_b
        x = x + gate_mlp[:, None, :] * m
        return x
    x = _L0_cond_ref(x, cond_1152, L0_cond_P, L0_cond_W, L0_cond_b)
    x = _L1_cond_ref(x, cond_1152, L1_cond_g1, L1_cond_g2, L1_cond_qkv_w, L1_cond_qkv_b, L1_cond_qg, L1_cond_kg, L1_cond_proj_w, L1_cond_proj_b, L1_cond_fc1_w, L1_cond_fc1_b, L1_cond_fc2_w, L1_cond_fc2_b, L1_cond_ada_w, L1_cond_ada_b)
    return x

_drawn_inputs = setup_inputs


def setup_inputs(seed=0):
    import zlib

    import numpy as np

    out = dict(_drawn_inputs(seed))
    spreads = {'L1_cond_qkv_b': (0.0, 0.8),
     'L1_cond_proj_b': (0.0, 0.366),
     'L1_cond_fc1_b': (0.0, 0.8),
     'L1_cond_fc2_b': (0.0, 0.396),
     'L1_cond_ada_b': (0.0, 0.441)}
    factors = {'L1_cond_qkv_w': 8.0, 'L1_cond_proj_w': 5.928}
    for name, (base, spread) in spreads.items():
        noise = np.random.default_rng([zlib.crc32(name.encode()), seed]).standard_normal(out[name].shape)
        drawn = base * np.exp(spread * noise) if base else spread * noise
        out[name] = jnp.asarray(drawn.astype(out[name].dtype))
    for name, factor in factors.items():
        out[name] = (out[name] * factor).astype(out[name].dtype)
    return out
```

```python
from contextlib import ExitStack

import concourse.bass as bass
from concourse import mybir

F32 = mybir.dt.float32
F16 = mybir.dt.float16
ALU = mybir.AluOpType
ACT = mybir.ActivationFunctionType
AX = mybir.AxisListType

B, T, N, D = 32, 256, 288, 64
R, KT = 96, 3
H, HD = 16, 18
QKV = 3 * N
HID = 4 * N
MT = HID // 128
HP = H // 2
NP = B // 2
WS = 64.0
MODS = 6 * KT
AB, GT = 2 * KT, KT
DOUBLE = 13
RS = 256.0
GUARD = 1e-24
BIG_NORM = float(N) ** 0.5
HEAD_NORM = float(HD) ** 0.5
QR_PER = 4
ROUNDS = D // QR_PER
FIRST_PRODUCT = 3
CH = 4


def wait(eng, sem, value):
    if isinstance(value, int) and value <= 0:
        return
    eng.wait_ge(sem, value)


class Count:

    def __init__(self, sem, base=0):
        self.sem, self.base, self.n = sem, base, 0

    def inc(self, ins):
        ins.then_inc(self.sem, 1)
        self.n += 1
        return self.base + self.n


def prepare(nc, io, dram, keep):
    with ExitStack() as ctx:
        def sb(name, shape, dt=F32):
            return ctx.enter_context(nc.sbuf_tensor(name, shape, dt))

        def sem(name):
            return ctx.enter_context(nc.semaphore(name))

        At = sb("At", [128, N])
        prod = sb("prod", [128, N])
        sqv = sb("sqv", [128, N])
        ident = sb("ident", [128, 128])
        identd = sb("identd", [128, D])
        gtm = sb("gtm", [128, D])
        lem = sb("lem", [128, D])
        sel = sb("sel", [128, 2, 128])
        dots = sb("dots", [128, 1])
        ssq = sb("ssq", [128, 1])
        sgn = sb("sgn", [128, 1])
        sig = sb("sig", [128, 1])
        st = sb("st", [128, 2])
        tiny = sb("tiny", [128, 1])
        rsig = sb("rsig", [128, 1])
        sig2 = sb("sig2", [128, 1])
        nwt = sb("nwt", [128, 2])
        rt = sb("rt", [128, 1])
        wv = sb("wv", [128, 1])
        nw = sb("nw", [128, 1])
        stall = sb("stall", [128, D, 2])
        scol = sb("scol", [128, 2])
        junk = sb("junk", [128, D])
        rcol = sb("rcol", [128, 3])
        Vt = sb("Vt", [128, N])
        V = sb("V", [R, KT, D])
        XY = sb("XY", [D, 2, 2 * D])
        XT = sb("XT", [D, 2, D])
        Yd = sb("Yd", [D, 2, D])
        UT = sb("UT", [128, N])
        cT = sb("cT", [R, KT, B])
        cE = sb("cE", [R, KT, B])
        cR = sb("cR", [R, KT, B])
        sT = sb("sT", [R, KT, B])
        bfull = sb("bfull", [B, D * D])
        wfull = sb("wfull", [R, 2, KT, 512])
        vraw = sb("vraw", [B, 2, 512])
        vall = sb("vall", [B, D * D])
        Ald = sb("Ald", [128, 16, D])
        mask = sb("mask", [128, D])
        E = sb("E", [128, 16, 128])
        ET = sb("ET", [128, 16, 128])
        F = sb("F", [128, 16, 128])
        Q = sb("Q", [128, 16, 128])
        two = sb("two", [128, 128])
        half = sb("half", [128, 128])
        adaw = sb("adaw", [R, KT, 6 * N])
        adab = sb("adab", [R, MODS])
        mod = sb("mod", [R, MODS, B])
        moda = sb("moda", [R, B, 2, AB])
        modg = sb("modg", [R, B, 2, GT])
        modb = sb("modb", [R, B, GT])
        gs = sb("gs", [R, 2])
        b2 = sb("b2", [R, KT])
        Gs = sb("Gs", [128, 2, N])
        wraw = sb("wraw", [128, KT * QKV + 4 * N + KT * HID + MT * N])
        ps = [ctx.enter_context(nc.psum_tensor(f"prep{i}", [128, 512], F32)) for i in range(8)]
        VA, VB = ps[0], ps[1]
        EP, TP, MP = ps[2:4], ps[4:6], ps[6:8]

        p_in = sem("p_in")
        c_in = sem("c_in")
        bias_in = sem("bias_in")
        wf_in = [sem("wf_in0"), sem("wf_in1")]
        ada_in = sem("ada_in")
        small_in = sem("small_in")
        a_in = sem("a_in")
        raw_in = sem("raw_in")
        zeroed = sem("zeroed")
        masks = sem("masks")
        pool_step = sem("pool_step")
        dve_step = sem("dve_step")
        sel_ready = sem("sel_ready")
        row_bc = sem("row_bc")
        ssq_ready = sem("ssq_ready")
        sig_ready = sem("sig_ready")
        rcol_ready = sem("rcol_ready")
        st_ready = sem("st_ready")
        st_saved = sem("st_saved")
        at_updated = sem("at_updated")
        exp_c = sem("exp_c")
        silu_ready = sem("silu_ready")
        v_mm = sem("v_mm")
        v_raw = sem("v_raw")
        v_ready = sem("v_ready")
        v_out = sem("v_out")
        a_ready = sem("a_ready")
        at_neg = sem("at_neg")
        q_ready = sem("q_ready")
        prod_mm = sem("prod_mm")
        prod_sb = sem("prod_sb")
        tr_mm = sem("tr_mm")
        tr_sb = sem("tr_sb")
        f_ready = sem("f_ready")
        mod_mm = sem("mod_mm")
        mod_sb = sem("mod_sb")
        gate_t = sem("gate_t")
        mods_done = sem("mods_done")
        mods_out = sem("mods_out")
        vt_ready = sem("vt_ready")
        wy_pe = sem("wy_pe")
        wy_sb = sem("wy_sb")
        g_mm = sem("g_mm")
        g_sb = sem("g_sb")
        g_out = [sem("g_out0"), sem("g_out1")]
        w_used = sem("w_used")
        w_scaled = sem("w_scaled")
        w_high = sem("w_high")

        block = ctx.enter_context(nc.Block())
        NV = D * D // 512

        splits, at = [], 0
        for name, parts, w in (("wq", R, KT * QKV), ("wp", 128, 4 * N), ("w1", R, KT * HID), ("w2", 128, MT * N)):
            splits.append((keep[name + "h"], keep[name + "l"], io[name + "T"], parts, at, w))
            at += w

        @block.sync
        def _(sp):
            sp.dma_start(At[:], io["PT"]).then_inc(p_in, 16)
            sp.dma_start(cT[:], io["condT"]).then_inc(c_in, 16)
            for c in range(2):
                sp.dma_start(wfull[:, c], io["WT"][:, :, c * 512:(c + 1) * 512]).then_inc(wf_in[c], 16)
            sp.dma_start(bfull[:], io["bfull"].broadcast_to([B, D * D])).then_inc(bias_in, 16)
            sp.dma_start(adab[:], io["adab"]).then_inc(small_in, 16)
            sp.dma_start(b2[:], io["b2"]).then_inc(small_in, 16)
            sp.dma_start(gs[:, 0:1], io["g1"].broadcast_to([R, 1])).then_inc(small_in, 16)
            sp.dma_start(gs[:, 1:2], io["g2"].broadcast_to([R, 1])).then_inc(small_in, 16)
            for c in range(2, NV):
                sp.wait_ge(v_mm, c - 1)
                sp.dma_start(wfull[:, c % 2], io["WT"][:, :, c * 512:(c + 1) * 512]).then_inc(wf_in[c % 2], 16)
            sp.wait_ge(v_ready, NV)
            sp.dma_start(dram["A"], vall[:]).then_inc(v_out, 16)
            sp.wait_ge(v_out, 16)
            for p in range(2):
                sp.dma_start(Ald[64 * p:64 * p + 64], dram["A"].rearrange("(p q) (i j) -> p i q j", p=2, i=D)[p]).then_inc(a_in, 16)
            sp.wait_ge(mods_done, 1)
            for ph in range(2):
                sp.dma_start(dram["ab"][ph].rearrange("b r c -> r b c"), moda[:, :, ph]).then_inc(mods_out, 16)
                sp.dma_start(dram["gate"][ph].rearrange("b r c -> r b c"), modg[:, :, ph]).then_inc(mods_out, 16)
            sp.dma_start(dram["gb"].rearrange("b r c -> r b c"), modb[:]).then_inc(mods_out, 16)
            sp.wait_ge(mods_out, 80)
            for q in range(16):
                sp.wait_ge(g_sb, q + 1)
                for p in range(2):
                    sp.dma_start(dram["G"][16 * p + q], Gs[64 * p:64 * p + 64, q % 2]).then_inc(g_out[q % 2], 16)
            for p in range(2):
                sp.wait_ge(g_out[p], 32 * 8)

        @block.gpsimd
        def _(pool):
            pc = Count(pool_step)

            def link(ins):
                pool.wait_ge(pool_step, pc.inc(ins))

            for t, w in ((ident, 128), (two, 128), (half, 128), (identd, D)):
                ins = nc.gpsimd.memset(t[:], 0.0)
            for t in (gtm, lem, mask):
                ins = nc.gpsimd.memset(t[:], 0.0)
            link(ins)
            for t, v in ((ident, 1.0), (two, 2.0), (half, 0.5)):
                nc.gpsimd.affine_select(out=t[:], in_=t[:], compare_op=ALU.not_equal, fill=v, base=0,
                                        pattern=[[-1, 128]], channel_multiplier=1)
            for p in range(2):
                h = slice(64 * p, 64 * p + 64)
                sc = 2.0 ** -DOUBLE
                nc.gpsimd.affine_select(out=identd[h], in_=identd[h], compare_op=ALU.not_equal, fill=1.0, base=0,
                                        pattern=[[-1, D]], channel_multiplier=1)
                nc.gpsimd.affine_select(out=gtm[h], in_=gtm[h], compare_op=ALU.is_ge, fill=1.0, base=0,
                                        pattern=[[1, D]], channel_multiplier=-1)
                nc.gpsimd.affine_select(out=lem[h], in_=lem[h], compare_op=ALU.is_gt, fill=1.0, base=0,
                                        pattern=[[-1, D]], channel_multiplier=1)
                ins = nc.gpsimd.affine_select(out=mask[h], in_=mask[h], compare_op=ALU.is_ge, fill=sc, base=0,
                                              pattern=[[-1, D]], channel_multiplier=1)
                link(ins)
                ins = nc.gpsimd.affine_select(out=mask[h], in_=mask[h], compare_op=ALU.is_ge, fill=-sc, base=0,
                                        pattern=[[1, D]], channel_multiplier=-1)
            link(ins)
            nc.gpsimd.memset(E[:], 0.0).then_inc(masks, 1)

            def make_sel(j):
                if not (isinstance(j, int) and j < 2):
                    pool.wait_ge(row_bc, j * 2 - 2)
                nc.gpsimd.tensor_copy(sel[:, par(j)], ident[:, col(j)].broadcast_to([128, 128])).then_inc(sel_ready, 1)

            parity = [0]

            def par(j):
                return parity[0]

            def col(j):
                return bass.ds(j, 1)

            def sel_step(j, s):
                parity[0] = s % 2
                make_sel(j)

            sel_step(0, 0)

            def split(n):
                hi, lo, _src, parts, c0, w = splits[n]
                pool.wait_ge(w_high, n + 1)
                nc.gpsimd.tensor_tensor(lo[0:parts], wraw[0:parts, c0:c0 + w], hi[0:parts], ALU.subtract).then_inc(w_used, 1)

            def v_chunk(c):
                pool.wait_ge(v_raw, c + 1)
                if c == 0:
                    pool.wait_ge(bias_in, 16)
                nc.gpsimd.tensor_tensor(vall[:, c * 512:(c + 1) * 512], vraw[:, c % 2], bfull[:, c * 512:(c + 1) * 512],
                                        ALU.add).then_inc(v_ready, 1)

            def skew():
                pool.wait_ge(a_in, 32)
                pool.wait_ge(sel_ready, 2 * QR_PER + 2)
                for p in range(2):
                    h = slice(64 * p, 64 * p + 64)
                    nc.gpsimd.tensor_tensor(E[h, :, h], Ald[h], mask[h, None, :].broadcast_to([64, 16, D]), ALU.mult).then_inc(a_ready, 1)
                    pool.wait_ge(a_ready, p + 1)
                link(nc.gpsimd.tensor_scalar(Q[:], E[:], 1.0 / 6, None, ALU.mult))
                link(nc.gpsimd.tensor_tensor(Q[:], Q[:], half[:, None, :].broadcast_to([128, 16, 128]), ALU.add))

            def taylor(c):
                q = slice(CH * c, CH * c + CH)
                pool.wait_ge(prod_sb, c + 1)
                link(nc.gpsimd.tensor_scalar(E[:, q], F[:, q], 1.0 / 24, None, ALU.mult))
                nc.gpsimd.tensor_tensor(Q[:, q], Q[:, q], E[:, q], ALU.add).then_inc(q_ready, 1)

            def plus_two(c, k):
                q = slice(CH * c, CH * c + CH)
                pool.wait_ge(prod_sb, k + 1)
                nc.gpsimd.tensor_tensor(F[:, q], E[:, q], two[:, None, :].broadcast_to([128, CH, 128]),
                                        ALU.add).then_inc(f_ready, 1)

            def round_(r):
                for s in range(QR_PER):
                    j = QR_PER * r + s
                    if isinstance(r, int):
                        if j + 1 < D:
                            sel_step(j + 1, s + 1)
                        if r < 2:
                            v_chunk(j)
                        if r == 2 and s == 0:
                            skew()
                        if r == FIRST_PRODUCT:
                            taylor(s)
                        if r > FIRST_PRODUCT:
                            plus_two(s, (r - FIRST_PRODUCT) * CH + s)
                    else:
                        sel_step(r * QR_PER + s + 1, s + 1)
                        plus_two(s, r * CH + (s - FIRST_PRODUCT * CH))

            for r in range(FIRST_PRODUCT + 2):
                round_(r)
            with pool.Fori(FIRST_PRODUCT + 2, ROUNDS - 1) as r:
                round_(r)
            round_(ROUNDS - 1)
            for r in (ROUNDS, ROUNDS + 1)[:1]:
                for c in range(4):
                    plus_two(c, (r - FIRST_PRODUCT) * CH + c)
            pool.wait_ge(mod_sb, 2)
            pool.wait_ge(gate_t, 1)
            pool.wait_ge(small_in, 64)
            for ph, (sh, scl, gt) in enumerate(((0, 3, 6), (9, 12, 15))):
                v = mod[:, scl:scl + KT, :].rearrange("r c b -> r b c")
                link(nc.gpsimd.tensor_scalar(moda[:, :, ph, 0:KT], v, 1.0, BIG_NORM * RS, ALU.add, ALU.mult))
                link(nc.gpsimd.tensor_scalar(moda[:, :, ph, 0:KT], moda[:, :, ph, 0:KT], gs[:, ph:ph + 1], None, ALU.mult))
                link(nc.gpsimd.tensor_copy(moda[:, :, ph, KT:AB], mod[:, sh:sh + KT, :].rearrange("r c b -> r b c")))
                link(nc.gpsimd.tensor_scalar(modg[:, :, ph], mod[:, gt:gt + KT, :].rearrange("r c b -> r b c"),
                                             1.0 / WS, None, ALU.mult))
            nc.gpsimd.tensor_tensor(modb[:], mod[:, 15:18, :].rearrange("r c b -> r b c"),
                                    b2[:, None, :].broadcast_to([R, B, KT]), ALU.mult).then_inc(mods_done, 1)
            for n in range(len(splits)):
                split(n)

        @block.scalar
        def _(act):
            act.dma_start(adaw[:], io["adaT"]).then_inc(ada_in, 16)
            for _h, _l, src, parts, c0, w in splits:
                act.dma_start(wraw[0:parts, c0:c0 + w], src).then_inc(raw_in, 16)
            act.wait_ge(c_in, 16)
            nc.scalar.activation(cE[:], cT[:], ACT.Exp, scale=-1.0).then_inc(exp_c, 1)

            act.wait_ge(dve_step, 1)

            def square(j):
                act.wait_ge(row_bc, 2 * j + 1)
                nc.scalar.activation(sqv[:], VA[:, 0:N], ACT.Square, accum_out=ssq[:]).then_inc(ssq_ready, 1)
                act.wait_ge(ssq_ready, j + 1)
                nc.scalar.activation(sig[:], ssq[:], ACT.Sqrt, bias=tiny[:]).then_inc(sig_ready, 1)

            def save_st(j):
                act.wait_ge(st_ready, j + 1)
                nc.scalar.activation(stall[:, bass.ds(j, 1), :], st[:, None, :], ACT.Copy).then_inc(st_saved, 1)

            def evac_product(c, k):
                act.wait_ge(prod_mm, k + 1)
                q = slice(CH * c, CH * c + CH)
                dst = F if isinstance(k, int) and k < 4 else E
                nc.scalar.activation(dst[:, q], EP[c % 2][:].rearrange("p (q n) -> p q n", q=CH), ACT.Copy).then_inc(prod_sb, 1)

            def evac_turned(c, k):
                act.wait_ge(tr_mm, k - 3)
                q = slice(CH * c, CH * c + CH)
                nc.scalar.activation(ET[:, q], TP[c % 2][:].rearrange("p (q n) -> p q n", q=CH), ACT.Copy).then_inc(tr_sb, 1)

            def round_(r):
                for s in range(QR_PER):
                    j = r * QR_PER + s
                    square(j)
                    save_st(j)
                    if isinstance(r, int):
                        if r < 2:
                            act.wait_ge(v_mm, j + 1)
                            if j >= 2:
                                act.wait_ge(v_ready, j - 1)
                            nc.scalar.activation(vraw[:, j % 2], MP[j % 2][0:B, :], ACT.Copy).then_inc(v_raw, 1)
                        if r == 2 and s == 1:
                            act.wait_ge(a_ready, 2)
                            nc.scalar.activation(ET[:], E[:], ACT.Copy, scale=-1.0).then_inc(at_neg, 1)
                        if r == FIRST_PRODUCT and s < 2:
                            act.wait_ge(mod_mm, 1)
                        if r >= FIRST_PRODUCT:
                            k = (r - FIRST_PRODUCT) * CH + s
                            evac_product(s, k)
                            if k >= 5:
                                evac_turned((s - 1) % 4, k - 1)
                    else:
                        evac_product(s, r * CH + (s - FIRST_PRODUCT * CH))
                        evac_turned((s - 1) % 4, r * CH + (s - 1 - FIRST_PRODUCT * CH))

            for r in range(FIRST_PRODUCT + 2):
                round_(r)
            with act.Fori(FIRST_PRODUCT + 2, ROUNDS - 1) as r:
                round_(r)
            round_(ROUNDS - 1)
            act.wait_ge(rcol_ready, 1)
            nc.scalar.activation(rcol[:, 1:2], rcol[:, 0:1], ACT.Sqrt).then_inc(sig_ready, 1)
            for k in range((ROUNDS - FIRST_PRODUCT) * CH, (ROUNDS + 2 - FIRST_PRODUCT) * CH + 1):
                if k < (ROUNDS + 2 - FIRST_PRODUCT) * CH:
                    evac_product(k % 4, k)
                evac_turned((k - 1) % 4, k - 1)
            act.wait_ge(mod_sb, 2)
            nc.scalar.activation(mod[:, 6:9], mod[:, 6:9], ACT.Tanh)
            nc.scalar.activation(mod[:, 15:18], mod[:, 15:18], ACT.Tanh).then_inc(gate_t, 1)
            act.wait_ge(raw_in, 16 * len(splits))
            for n, (hi, _l, _s, parts, c0, w) in enumerate(splits):
                nc.scalar.activation(wraw[0:parts, c0:c0 + w], wraw[0:parts, c0:c0 + w], ACT.Copy, scale=WS).then_inc(w_scaled, 1)
                act.wait_ge(w_scaled, n + 1)
                nc.scalar.activation(hi[0:parts], wraw[0:parts, c0:c0 + w], ACT.Copy).then_inc(w_high, 1)
            for q in range(16):
                act.wait_ge(g_mm, q + 1)
                if q >= 2:
                    act.wait_ge(g_out[q % 2], 32 * (q // 2))
                nc.scalar.activation(Gs[:, q % 2], MP[q % 2][:, 0:N], ACT.Copy).then_inc(g_sb, 1)

        @block.vector
        def _(dve):
            dc = Count(dve_step)

            def link(ins):
                dve.wait_ge(dve_step, dc.inc(ins))

            nc.vector.memset(keep["ones"][:], 1.0)
            nc.vector.memset(st[:], 0.0)
            link(nc.vector.memset(tiny[:], 1e-30))
            dve.wait_ge(exp_c, 1)
            link(nc.vector.tensor_scalar(cE[:], cE[:], 1.0, None, ALU.add))
            link(nc.vector.reciprocal(cR[:], cE[:]))
            nc.vector.tensor_tensor(sT[:], cT[:], cR[:], ALU.mult).then_inc(silu_ready, 1)
            dve.wait_ge(masks, 1)
            dve.wait_ge(p_in, 16)

            def step(j):
                at = bass.ds(j, 1)
                dve.wait_ge(row_bc, 2 * j + 2)
                dots_at = dc.inc(nc.vector.tensor_tensor_reduce(prod[:], At[:], VB[:, 0:N], 1.0, 0.0, ALU.mult, ALU.add, dots[:]))
                sg_at = dc.inc(nc.vector.tensor_scalar(sgn[:], VB[:, at], 0.0, -1.0, ALU.is_ge, ALU.mult))
                dve.wait_ge(sig_ready, j + 1)
                link(nc.vector.reciprocal(rsig[:], sig[:]))
                link(nc.vector.scalar_tensor_tensor(sig2[:], ssq[:], rsig[:], sig[:], ALU.mult, ALU.add))
                if not (isinstance(j, int) and j == 0):
                    dve.wait_ge(st_saved, j)
                link(nc.vector.scalar_tensor_tensor(st[:, 0:1], sgn[:], 0.5, sig2[:], ALU.add, ALU.mult))
                nc.vector.scalar_tensor_tensor(st[:, 1:2], VB[:, at], st[:, 0:1], st[:, 0:1], ALU.subtract, ALU.mult).then_inc(st_ready, 1)
                dve.wait_ge(dve_step, dots_at)
                w_at = dc.inc(nc.vector.scalar_tensor_tensor(wv[:], At[:, at], st[:, 0:1], dots[:], ALU.mult, ALU.subtract))
                dve.wait_ge(st_ready, j + 1)
                link(nc.vector.reciprocal(rt[:], st[:, 1:2]))
                dve.wait_ge(dve_step, w_at)
                link(nc.vector.scalar_tensor_tensor(nw[:], wv[:], rt[:], gtm[:, at], ALU.mult, ALU.mult))
                link(nc.vector.scalar_tensor_tensor(At[:], VB[:, 0:N], nw[:], At[:], ALU.mult, ALU.add))
                ins = nc.vector.tensor_tensor(At[:, at], At[:, at], lem[:, at], ALU.mult)
                ins.then_inc(at_updated, 1)

            link(nc.vector.tensor_scalar(gtm[:], gtm[:], -1.0, None, ALU.mult))

            def round_(r):
                for s in range(QR_PER):
                    step(r * QR_PER + s)

            for r in range(FIRST_PRODUCT):
                round_(r)
            dve.wait_ge(mod_mm, 1)
            dve.wait_ge(small_in, 64)
            for c in range(2):
                nc.vector.tensor_tensor(mod[:, 9 * c:9 * c + 9], MP[c][0:R, 0:9 * B].rearrange("r (c b) -> r c b", b=B),
                                        adab[:, 9 * c:9 * c + 9, None].broadcast_to([R, 9, B]), ALU.add).then_inc(mod_sb, 1)
            per_round = None
            before = dc.n
            round_(FIRST_PRODUCT)
            per_round = dc.n - before
            start = dc.n
            with dve.Fori(FIRST_PRODUCT + 1, ROUNDS) as r:
                dc.base, dc.n = r * per_round, start - (FIRST_PRODUCT + 1) * per_round
                round_(r)
            dc.base, dc.n = 0, start + (ROUNDS - FIRST_PRODUCT - 1) * per_round
            dve.wait_ge(st_saved, D)
            dve.wait_ge(at_updated, D)
            for k in range(2):
                ins = nc.vector.tensor_tensor_reduce(junk[:], stall[:, :, k], identd[:], -1.0, 0.0, ALU.mult, ALU.add, scol[:, k:k + 1])
                link(ins)
            nc.vector.reciprocal(rcol[:, 0:1], scol[:, 1:2]).then_inc(rcol_ready, 1)
            dve.wait_ge(sig_ready, D + 1)
            link(nc.vector.tensor_tensor(nwt[:, 0:1], rcol[:, 1:2], rcol[:, 1:2], ALU.mult))
            link(nc.vector.scalar_tensor_tensor(nwt[:, 1:2], nwt[:, 0:1], -0.5, scol[:, 1:2], ALU.mult, ALU.mult))
            link(nc.vector.scalar_tensor_tensor(rcol[:, 2:3], nwt[:, 1:2], 1.5, rcol[:, 1:2], ALU.add, ALU.mult))
            link(nc.vector.scalar_tensor_tensor(At[:, 0:D], identd[:], scol[:, 0:1], At[:, 0:D], ALU.mult, ALU.add))
            nc.vector.tensor_scalar(Vt[:], At[:], rcol[:, 2:3], None, ALU.mult).then_inc(vt_ready, 1)
            wy = Count(wy_sb)
            dve.wait_ge(wy_pe, 1)
            wy.inc(nc.vector.tensor_copy(V[:], VA[0:R, 0:KT * D].rearrange("r (k d) -> r k d", k=KT)))
            dve.wait_ge(wy_pe, 2)
            link(nc.vector.tensor_tensor(junk[0:D], lem[0:D], identd[0:D], ALU.subtract))
            link(nc.vector.scalar_tensor_tensor(XY[:, 0, 0:D], VB[0:D, 0:D], -1.0, junk[0:D], ALU.mult, ALU.mult))
            link(nc.vector.tensor_tensor(XT[:, 0], VB[0:D, 0:D], gtm[0:D], ALU.mult))
            dve.wait_ge(vt_ready, 1)
            wy.inc(nc.vector.tensor_copy(XY[:, 0, D:2 * D], Vt[0:D, 0:D]))
            for k in range(6):
                a, b = k % 2, (k + 1) % 2
                dve.wait_ge(wy_pe, 3 + k)
                last = nc.vector.tensor_tensor(XY[:, b, D:2 * D], VA[0:D, D:2 * D], XY[:, a, D:2 * D], ALU.add)
                if k < 5:
                    nc.vector.tensor_copy(XY[:, b, 0:D], VA[0:D, 0:D])
                    last = nc.vector.tensor_copy(XT[:, b], VB[0:D, 0:D])
                wy.inc(last)
            dve.wait_ge(wy_sb, 8)
            wy.inc(nc.vector.tensor_copy(Yd[:], XY[:, 0, None, D:2 * D].broadcast_to([D, 2, D])))
            dve.wait_ge(wy_pe, 9)
            nc.vector.tensor_scalar(UT[:, D:N], VA[:, D:N], -1.0, None, ALU.mult)
            wy.inc(nc.vector.scalar_tensor_tensor(UT[:, 0:D], VA[:, 0:D], -1.0, identd[:], ALU.mult, ALU.add))
            dve.wait_ge(wy_pe, 10)
            nc.vector.memset(keep["U"][:], 0.0).then_inc(wy_sb, 1)
            dve.wait_ge(wy_sb, 11)
            wy.inc(nc.vector.tensor_copy(keep["U"][:, :, 0:D], VB[0:R, 0:KT * D].rearrange("r (k d) -> r k d", k=KT)))
            dve.wait_ge(wy_sb, 12)

        @block.tensor
        def _(pe):
            pe.wait_ge(p_in, 16)
            pe.wait_ge(masks, 1)

            def bcast(j, s):
                pe.wait_ge(sel_ready, j + 1)
                if not (isinstance(j, int) and j == 0):
                    pe.wait_ge(at_updated, j)
                for t in (VA, VB):
                    nc.tensor.matmul(t[:, 0:N], sel[:, s % 2], At[:], start=True, stop=True).then_inc(row_bc, 1)

            def product(c, k):
                if isinstance(k, int) and k < 4:
                    pe.wait_ge(at_neg, 1)
                elif isinstance(k, int) and k < 8:
                    pe.wait_ge(q_ready, k - 3)
                else:
                    pe.wait_ge(f_ready, k - 7)
                    pe.wait_ge(tr_sb, k - 7)
                if not (isinstance(k, int) and k < 2):
                    pe.wait_ge(prod_sb, k - 1)
                out = EP[c % 2]
                for n in range(CH):
                    q = CH * c + n
                    o = out[:, 128 * n:128 * n + 128]
                    if isinstance(k, int) and k < 4:
                        mm = nc.tensor.matmul(o, ET[:, q], E[:, q], start=True, stop=True)
                    elif isinstance(k, int) and k < 8:
                        nc.tensor.matmul(o, ET[:, q], ident[:], start=True, stop=False)
                        mm = nc.tensor.matmul(o, F[:, q], Q[:, q], start=False, stop=True)
                    else:
                        mm = nc.tensor.matmul(o, ET[:, q], F[:, q], start=True, stop=True)
                mm.then_inc(prod_mm, 1)

            def turn(c, k):
                pe.wait_ge(prod_sb, k + 1)
                if not (isinstance(k, int) and k < 6):
                    pe.wait_ge(tr_sb, k - 5)
                for n in range(CH):
                    mm = nc.tensor.transpose(TP[c % 2][:, 128 * n:128 * n + 128], E[:, CH * c + n], ident[:])
                mm.then_inc(tr_mm, 1)

            def round_(r):
                for s in range(QR_PER):
                    j = r * QR_PER + s
                    bcast(j, s)
                    if isinstance(r, int):
                        if r < 2:
                            if j == 0:
                                pe.wait_ge(silu_ready, 1)
                            pe.wait_ge(wf_in[j % 2], 16 * (j // 2 + 1))
                            if j >= 2:
                                pe.wait_ge(v_raw, j - 1)
                            for k in range(KT):
                                mm = nc.tensor.matmul(MP[j % 2][0:B, :], sT[:, k], wfull[:, j % 2, k], start=(k == 0), stop=(k == 2))
                            mm.then_inc(v_mm, 1)
                        if r == 2:
                            if s == 0:
                                pe.wait_ge(ada_in, 16)
                                pe.wait_ge(v_raw, 8)
                            lo, hi = (0, 5, 9, 14, 18)[s], (0, 5, 9, 14, 18)[s + 1]
                            for c in range(lo, hi):
                                o = MP[c // 9][0:R, (c % 9) * B:(c % 9 + 1) * B]
                                for k in range(KT):
                                    mm = nc.tensor.matmul(o, adaw[:, k, c * R:(c + 1) * R], sT[:, k], start=(k == 0), stop=(k == 2))
                            if s == 3:
                                mm.then_inc(mod_mm, 1)
                        if r >= FIRST_PRODUCT:
                            k = (r - FIRST_PRODUCT) * CH + s
                            product(s, k)
                            if k >= 5:
                                turn((s - 1) % 4, k - 1)
                    else:
                        product(s, r * CH + (s - FIRST_PRODUCT * CH))
                        turn((s - 1) % 4, r * CH + (s - 1 - FIRST_PRODUCT * CH))

            for r in range(FIRST_PRODUCT + 2):
                round_(r)
            with pe.Fori(FIRST_PRODUCT + 2, ROUNDS - 1) as r:
                round_(r)
            round_(ROUNDS - 1)
            KEND = (ROUNDS + 2 - FIRST_PRODUCT) * CH

            def tail(k):
                if k < KEND:
                    product(k % 4, k)
                turn((k - 1) % 4, k - 1)

            wy = Count(wy_pe)
            kk = (ROUNDS - FIRST_PRODUCT) * CH
            tail(kk)
            pe.wait_ge(vt_ready, 1)
            for k in range(KT):
                mm = nc.tensor.transpose(VA[0:R, D * k:D * k + D], Vt[0:D, R * k:R * k + R], ident[0:D, 0:D])
            wy.inc(mm)
            tail(kk + 1)
            pe.wait_ge(wy_sb, 1)
            for k in range(KT):
                mm = nc.tensor.matmul(VB[0:D, 0:D], V[:, k], V[:, k], start=(k == 0), stop=(k == 2))
            wy.inc(mm)
            for k in range(6):
                if k < 6 and kk + 2 + k <= KEND:
                    tail(kk + 2 + k)
                pe.wait_ge(wy_sb, 2 + k)
                mm = nc.tensor.matmul(VA[0:D, 0:2 * D], XT[:, k % 2], XY[:, k % 2], start=True, stop=True)
                if k < 5:
                    mm = nc.tensor.matmul(VB[0:D, 0:D], XY[:, k % 2, 0:D], XT[:, k % 2], start=True, stop=True)
                wy.inc(mm)
            for k in range(kk + 8, KEND + 1):
                tail(k)
            pe.wait_ge(wy_sb, 9)
            wy.inc(nc.tensor.matmul(VA[:, 0:N], Yd[:].rearrange("p a d -> p (a d)"), Vt[0:D, :], start=True, stop=True))
            pe.wait_ge(wy_sb, 10)
            for k in range(KT):
                mm = nc.tensor.transpose(VB[0:R, D * k:D * k + D], UT[0:D, R * k:R * k + R], ident[0:D, 0:D])
            wy.inc(mm)
            pe.wait_ge(mod_sb, 2)
            pe.wait_ge(tr_sb, KEND - 4)
            for q in range(16):
                if q >= 2:
                    pe.wait_ge(g_sb, q - 1)
                nc.tensor.matmul(MP[q % 2][:, 0:N], ET[:, q], UT[:], start=True, stop=True).then_inc(g_mm, 1)


def at(m, per, k=0):
    i, c = m
    return per * c + k if i is None else i * (2 * per) + (per * c + k)


def after(m, d):
    return (m[0], m[1] + d)


def number(m):
    return m[1] if m[0] is None else m[0] * 2 + m[1]


def uses(m, per, k=0):
    i, c = m
    return per * (c // 2) + k if i is None else i * per + (per * (c // 2) + k)


def valid(m, last):
    return None if m[0] is None and not 0 <= m[1] < last else m


def slots(eng, last, body):
    def one(i, c):
        body(*(valid((i, c + d), last) for d in (1, 0, -1)), (i, c))

    for c in (-1, 0, 1):
        one(None, c)
    with eng.Fori(1, last // 2 - 1) as i:
        one(i, 0)
        one(i, 1)
    for c in (last - 2, last - 1, last):
        one(None, c)


def attention(nc, io, dram, keep):
    with ExitStack() as ctx:
        def sb(name, shape, dt=F32):
            return ctx.enter_context(nc.sbuf_tensor(name, shape, dt))

        def sem(name):
            return ctx.enter_context(nc.semaphore(name))

        xs = [sb(f"xs{p}", [R, KT, T]) for p in range(2)]
        Gb = [sb(f"Gb{p}", [R, N]) for p in range(2)]
        ab = [sb(f"ab{p}", [R, AB]) for p in range(2)]
        gate = [sb(f"gate{p}", [R, GT]) for p in range(2)]
        zT = sb("zT", [R, T])
        x1 = [sb(f"x1{p}", [R, KT, T]) for p in range(2)]
        x1k = sb("x1k", [R, KT, T])
        x2s = [sb(f"x2s{p}", [R, KT, T]) for p in range(2)]
        sq = sb("sq", [R, KT, T])
        ms = sb("ms", [R, T])
        ln = sb("ln", [R, T])
        ry = sb("ry", [R, T])
        ru = sb("ru", [R, T])
        rv = sb("rv", [R, T])
        rs = sb("rs", [R, T])
        h = sb("h", [R, KT, T])
        hh = sb("hh", [R, KT, T], F16)
        hl = sb("hl", [R, KT, T], F16)
        bq = sb("bq", [128, QKV])
        qk = sb("qk", [128, 2, 2 * N])
        qks = sb("qks", [128, 2, 2 * N])
        hm = sb("hm", [128, 2 * 32])
        hln = sb("hln", [128, 2 * 32])
        hy = sb("hy", [128, 2 * 32])
        hu = sb("hu", [128, 2 * 32])
        hv = sb("hv", [128, 2 * 32])
        hr = sb("hr", [128, 2 * 32])
        gv = sb("gv", [128, 2, 2, H])
        gk = sb("gk", [128, 4])
        stk = sb("stk", [128, 2, 2 * H, 64], F16)
        va = [sb(f"va{p}", [128, 2, H, 32]) for p in range(2)]
        qT = sb("qT", [128, HP, T], F16)
        kT = sb("kT", [128, HP, T], F16)
        pt = [sb(f"pt{j}", [128, 2, 2, T]) for j in range(4)]
        OT = sb("OT", [128, 4, T])
        rec = sb("rec", [128, 4, T])
        oh = sb("oh", [128, 4, T], F16)
        ol = sb("ol", [128, 4, T], F16)
        id16 = sb("id16", [128, 128], F16)
        pick = sb("pick", [128, 128])
        wqh = keep["wqh"][:].rearrange("p (k n) -> p k n", k=KT)
        wql = keep["wql"][:].rearrange("p (k n) -> p k n", k=KT)
        wph = keep["wph"][:].rearrange("p (g n) -> p g n", g=4)
        wpl = keep["wpl"][:].rearrange("p (g n) -> p g n", g=4)

        SP = [ctx.enter_context(nc.psum_tensor(f"scores{j}", [128, 2, 512], F32)) for j in range(2)]
        OP = ctx.enter_context(nc.psum_tensor("heads_out", [128, 512], F32))
        RB = [ctx.enter_context(nc.psum_tensor(f"ring{j}", [128, 512], F32)) for j in range(3)]
        ORDER = ["z", "sb0", "sb1", "d0", "d1", "d2", "ss", "pj0", "pj1", "pj2",
                 "q0", "q1", "q2", "q3", "t0", "t1", "t2", "t3"]
        rb = {u: RB[k % 3] for k, u in enumerate(ORDER)}

        x_in = [sem("x_in0"), sem("x_in1")]
        gate_in = [sem("gate_in0"), sem("gate_in1")]
        keep_in = sem("keep_in")
        x2_out = [sem("x2_out0"), sem("x2_out1")]
        setup_in = sem("setup_in")
        setup_pool = sem("setup_pool")
        setup_dve = sem("setup_dve")
        names_pe = ("z_mm", "d_mm", "ss_mm", "qkv_mm", "tr_mm", "s_mm", "av_mm", "sb_mm", "pj_mm")
        (z_mm, d_mm, ss_mm, qkv_mm, tr_mm, s_mm, av_mm, sb_mm, pj_mm) = [sem(n) for n in names_pe]
        names_act = ("z_sb", "sq_sb", "ln_sb", "ry_sb", "hh_sb", "p_sb", "ot_sb", "oh_sb", "qks_sb", "hln_sb", "hy_sb", "qh_sb")
        (z_sb, sq_sb, ln_sb, ry_sb, hh_sb, p_sb, ot_sb, oh_sb, qks_sb, hln_sb, hy_sb, qh_sb) = [sem(n) for n in names_act]
        names_dve = ("rec_sb", "x1_sb", "ms_sb", "newton", "rs_sb", "h_sb", "ol_sb", "hl_sb", "x2_sb", "qkv_sb",
                     "hss_sb", "hm_sb", "hnewton", "hr_sb", "qkn_sb", "tr_sb")
        (rec_sb, x1_sb, ms_sb, newton, rs_sb, h_sb, ol_sb, hl_sb, x2_sb, qkv_sb,
         hss_sb, hm_sb, hnewton, hr_sb, qkn_sb, tr_sb) = [sem(n + "_a") for n in names_dve]
        READER = {"z": (z_sb, 1, 0), "sb": (rec_sb, 2, 2), "d": (x1_sb, 3, 0), "ss": (ms_sb, 1, 0),
                  "pj": (x2_sb, 3, 2), "q": (qkv_sb, 4, 0), "t": (tr_sb, 4, 0)}
        t_sb, om_sb, stk_sb = sem("t_sb"), sem("om_sb"), sem("stk_sb")

        block = ctx.enter_context(nc.Block())

        @block.sync
        def _(sp):
            sp.dma_start(bq[:], io["bq"].broadcast_to([128, QKV])).then_inc(setup_in, 16)
            sp.dma_start(gk[:, 0:1], io["qg"].broadcast_to([128, 1])).then_inc(setup_in, 16)
            sp.dma_start(gk[:, 1:2], io["kg"].broadcast_to([128, 1])).then_inc(setup_in, 16)

            def load(m):
                p, n = m[1] % 2, number(m)
                wait(sp, x1_sb, at(m, 3, -3))
                if m[0] is not None or m[1] >= 2:
                    wait(sp, h_sb, at(m, 3, -3))
                s = bass.ds(n, 1)
                sp.dma_start(xs[p][:], io["x"][s].rearrange("o r k t -> (o r) k t")).then_inc(x_in[p], 16)
                sp.dma_start(Gb[p][0:D], dram["G"][s].rearrange("o d n -> (o d) n")).then_inc(x_in[p], 16)
                sp.dma_start(ab[p][:], dram["ab"][0][s].rearrange("o r c -> (o r) c")).then_inc(x_in[p], 16)

            load((None, 0))
            load((None, 1))
            for p in range(2):
                sp.sem_inc(x2_out[p], 16)

            def body(fr, mid, back, _centre):
                if fr is not None and not (fr[0] is None and fr[1] + 1 >= B) and not (fr[0] is None and fr[1] < 1):
                    load(after(fr, 1))
                if mid is not None:
                    p, s = mid[1] % 2, bass.ds(number(mid), 1)
                    wait(sp, x2_sb, at(mid, 3, -3))
                    sp.dma_start(gate[p][:], dram["gate"][0][s].rearrange("o r c -> (o r) c")).then_inc(gate_in[p], 16)
                    wait(sp, x1_sb, at(mid, 3, 3))
                    wait(sp, x2_sb, at(mid, 3, 0))
                    sp.dma_start(x1k[:], x1[p][:]).then_inc(keep_in, 16)
                if back is not None:
                    p, s = back[1] % 2, bass.ds(number(back), 1)
                    wait(sp, x2_sb, at(back, 3, 3))
                    sp.dma_start(dram["x2"][s].rearrange("o r k t -> (o r) k t"), x2s[p][:]).then_inc(x2_out[p], 16)

            slots(sp, B, body)
            for p in range(2):
                sp.wait_ge(x2_out[p], 16 * NP + 16)

        @block.gpsimd
        def _(pool):
            sc = Count(setup_pool)

            def link(ins):
                pool.wait_ge(setup_pool, sc.inc(ins))

            nc.gpsimd.memset(Gb[0][D:R], 0.0)
            link(nc.gpsimd.memset(Gb[1][D:R], 0.0))
            nc.gpsimd.memset(id16[:], 0.0)
            nc.gpsimd.memset(pick[:], 0.0)
            nc.gpsimd.memset(stk[:], 0.0)
            nc.gpsimd.memset(va[0][:], 0.0)
            link(nc.gpsimd.memset(va[1][:], 0.0))

            def body(fr, mid, back, _centre):
                if back is not None:
                    for u in range(2):
                        pool.wait_ge(rec_sb, at(back, 2, u + 1))
                        o = OT[:, 2 * u:2 * u + 2]
                        nc.gpsimd.tensor_tensor(o, o, rec[:, 2 * u:2 * u + 2], ALU.mult).then_inc(om_sb, 1)
                if fr is not None:
                    pool.wait_ge(rs_sb, at(fr, 1, 1))
                    p = fr[1] % 2
                    nc.gpsimd.tensor_tensor(h[:], x1[p][:], rs[:, None, :].broadcast_to([R, KT, T]), ALU.mult).then_inc(t_sb, 1)
                    for t in range(2):
                        pool.wait_ge(qh_sb, at(fr, 2, t + 1))
                        v = qk[:, t].rearrange("p (h d) -> p h d", d=HD)
                        nc.gpsimd.tensor_tensor(stk[:, t, 0:H, HD:2 * HD], v[:, 0:H], stk[:, t, 0:H, 0:HD], ALU.subtract)
                        nc.gpsimd.tensor_tensor(stk[:, t, H:2 * H, 2 * HD:3 * HD], v[:, H:2 * H], stk[:, t, H:2 * H, 0:HD],
                                                ALU.subtract)
                        nc.gpsimd.tensor_copy(stk[:, t, 0:H, 2 * HD:3 * HD], stk[:, t, 0:H, 0:HD])
                        nc.gpsimd.tensor_copy(stk[:, t, H:2 * H, HD:2 * HD], stk[:, t, H:2 * H, 0:HD]).then_inc(stk_sb, 1)

            nc.gpsimd.affine_select(out=id16[:], in_=id16[:], compare_op=ALU.not_equal, fill=1.0, base=0,
                                    pattern=[[-1, 128]], channel_multiplier=1)
            nc.gpsimd.affine_select(out=pick[:].rearrange("p (j r) -> p j r", j=4), in_=pick[:].rearrange("p (j r) -> p j r", j=4),
                                    compare_op=ALU.not_equal, fill=1.0, base=-HD, pattern=[[-32, 4], [0, 32]],
                                    channel_multiplier=1)
            nc.gpsimd.memset(va[0][:, :, :, HD:HD + 1], 1.0)
            nc.gpsimd.memset(va[1][:, :, :, HD:HD + 1], 1.0)
            nc.gpsimd.memset(stk[:, :, 0:H, 3 * HD:3 * HD + 2], 1.0)
            pool.wait_ge(setup_dve, 3)
            nc.gpsimd.tensor_copy(stk[:, 0, H:2 * H, 3 * HD], gk[:, 2:3].broadcast_to([128, H]))
            link(nc.gpsimd.tensor_copy(stk[:, 1, H:2 * H, 3 * HD], gk[:, 2:3].broadcast_to([128, H])))
            for t in range(2):
                ins = nc.gpsimd.tensor_tensor(stk[:, t, H:2 * H, 3 * HD + 1], gk[:, 2:3].broadcast_to([128, H]),
                                              stk[:, t, H:2 * H, 3 * HD], ALU.subtract)
            link(ins)
            slots(pool, B, body)

        @block.scalar
        def _(act):
            def ex(mid, hp):
                act.wait_ge(s_mm, at(mid, 8, hp + 1))
                wait(act, av_mm, at(mid, 8, hp - 3))
                nc.scalar.activation(pt[hp % 4][:].rearrange("p e k t -> p (e k t)"), SP[hp % 2][:].rearrange("p e n -> p (e n)"),
                                     ACT.Exp).then_inc(p_sb, 1)

            def heads_out(mid, g):
                act.wait_ge(av_mm, at(mid, 8, 2 * g + 2))
                wait(act, ol_sb, at(mid, 1, 0))
                nc.scalar.activation(OT[:, g], OP[:, 0:T], ACT.Copy).then_inc(ot_sb, 1)

            def body(fr, mid, back, _centre):
                if fr is not None:
                    act.wait_ge(z_mm, at(fr, 1, 1))
                    nc.scalar.activation(zT[:], rb["z"][0:R, 0:T], ACT.Copy).then_inc(z_sb, 1)
                if mid is not None:
                    ex(mid, 0)
                    ex(mid, 1)
                if fr is not None:
                    act.wait_ge(x1_sb, at(fr, 3, 3))
                    nc.scalar.activation(sq[:], x1[fr[1] % 2][:], ACT.Square).then_inc(sq_sb, 1)
                if mid is not None:
                    ex(mid, 2)
                if back is not None:
                    act.wait_ge(om_sb, at(back, 2, 2))
                    wait(act, pj_mm, at(back, 3, 0))
                    nc.scalar.activation(oh[:], OT[:], ACT.Copy).then_inc(oh_sb, 1)
                if fr is not None:
                    act.wait_ge(ms_sb, at(fr, 1, 1))
                    nc.scalar.activation(ln[:], ms[:], ACT.Ln, scale=RS * RS).then_inc(ln_sb, 1)
                    act.wait_ge(ln_sb, at(fr, 1, 1))
                    nc.scalar.activation(ry[:], ln[:], ACT.Exp, scale=-0.5).then_inc(ry_sb, 1)
                if mid is not None:
                    ex(mid, 3)
                    heads_out(mid, 0)
                if fr is not None:
                    act.wait_ge(h_sb, at(fr, 3, 3))
                    wait(act, qkv_mm, at(fr, 4, 0))
                    nc.scalar.activation(hh[:], h[:], ACT.Copy).then_inc(hh_sb, 1)
                    for t in range(2):
                        act.wait_ge(qkv_sb, at(fr, 4, 2 * t + 2))
                        nc.scalar.activation(qks[:, t], qk[:, t], ACT.Square).then_inc(qks_sb, 1)
                if mid is not None:
                    ex(mid, 4)
                    heads_out(mid, 1)
                if fr is not None:
                    act.wait_ge(hm_sb, at(fr, 1, 1))
                    nc.scalar.activation(hln[:], hm[:], ACT.Ln, scale=RS * RS).then_inc(hln_sb, 1)
                    act.wait_ge(hln_sb, at(fr, 1, 1))
                    nc.scalar.activation(hy[:], hln[:], ACT.Exp, scale=-0.5).then_inc(hy_sb, 1)
                if mid is not None:
                    ex(mid, 5)
                    ex(mid, 6)
                    heads_out(mid, 2)
                if fr is not None:
                    for t in range(2):
                        act.wait_ge(qkn_sb, at(fr, 2, t + 1))
                        wait(act, tr_mm, at(fr, 4, 0))
                        nc.scalar.activation(stk[:, t, :, 0:HD], qk[:, t].rearrange("p (h d) -> p h d", d=HD),
                                             ACT.Copy).then_inc(qh_sb, 1)
                if mid is not None:
                    ex(mid, 7)
                    heads_out(mid, 3)

            act.wait_ge(setup_pool, 4)
            slots(act, B, body)

        @block.vector
        def _(dve):
            dve.wait_ge(setup_in, 48)
            nc.vector.tensor_scalar(gv[:, :, 0, :], gk[:, None, 0:1].broadcast_to([128, 2, H]), RS, None, ALU.mult)
            nc.vector.tensor_scalar(gv[:, :, 1, :], gk[:, None, 1:2].broadcast_to([128, 2, H]), RS * HEAD_NORM, None, ALU.mult)
            nc.vector.tensor_tensor(gk[:, 2:3], gk[:, 0:1], gk[:, 1:2], ALU.mult).then_inc(setup_dve, 1)
            dve.wait_ge(setup_dve, 1)
            nc.vector.tensor_scalar(gk[:, 3:4], gk[:, 2:3], -1.0, None, ALU.mult).then_inc(setup_dve, 1)
            dve.wait_ge(setup_dve, 2)
            nc.vector.tensor_scalar(gk[:, 2:3], gk[:, 3:4], gk[:, 2:3], -HEAD_NORM, ALU.max, ALU.mult).then_inc(setup_dve, 1)
            dve.wait_ge(setup_pool, 4)

            def body(fr, mid, back, _centre):
                if back is not None:
                    for u in range(2):
                        dve.wait_ge(sb_mm, at(back, 2, u + 1))
                        nc.vector.reciprocal(rec[:, 2 * u:2 * u + 2], rb[f"sb{u}"][:].rearrange("p (g t) -> p g t", g=2)).then_inc(rec_sb, 1)
                if fr is not None:
                    p = fr[1] % 2
                    dve.wait_ge(x_in[p], uses(fr, 48, 48))
                    wait(dve, keep_in, at(fr, 16, -16))
                    for k in range(KT):
                        dve.wait_ge(d_mm, at(fr, 3, k + 1))
                        nc.vector.tensor_tensor(x1[p][:, k], rb[f"d{k}"][0:R, 0:T], xs[p][:, k], ALU.add).then_inc(x1_sb, 1)
                    dve.wait_ge(ss_mm, at(fr, 1, 1))
                    nc.vector.tensor_scalar(ms[:], rb["ss"][0:R, 0:T], GUARD, None, ALU.max).then_inc(ms_sb, 1)
                    dve.wait_ge(ry_sb, at(fr, 1, 1))
                    dve.wait_ge(ms_sb, at(fr, 1, 1))
                    nc.vector.scalar_tensor_tensor(ru[:], ms[:], -0.5 * RS * RS, ry[:], ALU.mult, ALU.mult).then_inc(newton, 1)
                    dve.wait_ge(newton, at(fr, 2, 1))
                    nc.vector.tensor_tensor(rv[:], ru[:], ry[:], ALU.mult).then_inc(newton, 1)
                    dve.wait_ge(newton, at(fr, 2, 2))
                    nc.vector.scalar_tensor_tensor(rs[:], rv[:], 1.5, ry[:], ALU.add, ALU.mult).then_inc(rs_sb, 1)
                if back is not None:
                    dve.wait_ge(oh_sb, at(back, 1, 1))
                    nc.vector.tensor_tensor(ol[:], OT[:], oh[:], ALU.subtract).then_inc(ol_sb, 1)
                if fr is not None:
                    dve.wait_ge(t_sb, at(fr, 1, 1))
                    for k in range(KT):
                        nc.vector.tensor_scalar(h[:, k], h[:, k], ab[p][:, k:k + 1], ab[p][:, KT + k:KT + k + 1],
                                                ALU.mult, ALU.add).then_inc(h_sb, 1)
                    dve.wait_ge(hh_sb, at(fr, 1, 1))
                    nc.vector.tensor_tensor(hl[:], h[:], hh[:], ALU.subtract).then_inc(hl_sb, 1)
                if back is not None:
                    q = back[1] % 2
                    dve.wait_ge(gate_in[q], uses(back, 16, 16))
                    dve.wait_ge(keep_in, at(back, 16, 16))
                    dve.wait_ge(x2_out[q], uses(back, 16, 16))
                    for k in range(KT):
                        dve.wait_ge(pj_mm, at(back, 3, k + 1))
                        nc.vector.scalar_tensor_tensor(x2s[q][:, k], rb[f"pj{k}"][0:R, 0:T], gate[q][:, k:k + 1], x1k[:, k],
                                                       ALU.mult, ALU.add).then_inc(x2_sb, 1)
                if fr is not None:
                    va_p = va[p]
                    for t in range(2):
                        dve.wait_ge(qkv_mm, at(fr, 4, 2 * t + 1))
                        a = rb[f"q{2 * t}"][:, 0:432]
                        nc.vector.scalar_tensor_tensor(qk[:, t, 0:432], a, 1.0 / WS, bq[:, 0:432], ALU.mult, ALU.add).then_inc(qkv_sb, 1)
                        dve.wait_ge(qkv_mm, at(fr, 4, 2 * t + 2))
                        a = rb[f"q{2 * t + 1}"]
                        nc.vector.scalar_tensor_tensor(qk[:, t, 432:576], a[:, 0:144], 1.0 / WS, bq[:, 432:576], ALU.mult, ALU.add)
                        nc.vector.scalar_tensor_tensor(va_p[:, t, :, 0:HD], a[:, 144:432].rearrange("p (h d) -> p h d", d=HD), 1.0 / WS,
                                                       bq[:, 576:864].rearrange("p (h d) -> p h d", d=HD), ALU.mult, ALU.add).then_inc(qkv_sb, 1)
                    for t in range(2):
                        dve.wait_ge(qks_sb, at(fr, 2, t + 1))
                        nc.vector.tensor_reduce(hm[:, 32 * t:32 * t + 32], qks[:, t].rearrange("p (h d) -> p h d", d=HD), AX.X, ALU.add).then_inc(hss_sb, 1)
                    dve.wait_ge(hss_sb, at(fr, 2, 2))
                    nc.vector.tensor_scalar(hm[:], hm[:], GUARD, None, ALU.max).then_inc(hm_sb, 1)
                    dve.wait_ge(hy_sb, at(fr, 1, 1))
                    dve.wait_ge(hm_sb, at(fr, 1, 1))
                    nc.vector.scalar_tensor_tensor(hu[:], hm[:], -0.5 * RS * RS, hy[:], ALU.mult, ALU.mult).then_inc(hnewton, 1)
                    dve.wait_ge(hnewton, at(fr, 3, 1))
                    nc.vector.tensor_tensor(hv[:], hu[:], hy[:], ALU.mult).then_inc(hnewton, 1)
                    dve.wait_ge(hnewton, at(fr, 3, 2))
                    nc.vector.scalar_tensor_tensor(hr[:], hv[:], 1.5, hy[:], ALU.add, ALU.mult).then_inc(hnewton, 1)
                    dve.wait_ge(hnewton, at(fr, 3, 3))
                    nc.vector.tensor_tensor(hr[:], hr[:], gv[:].rearrange("p t a h -> p (t a h)"), ALU.mult).then_inc(hr_sb, 1)
                    dve.wait_ge(hr_sb, at(fr, 1, 1))
                    for t in range(2):
                        v = qk[:, t].rearrange("p (h d) -> p h d", d=HD)
                        nc.vector.tensor_tensor(v, v, hr[:, 32 * t:32 * t + 32, None].broadcast_to([128, 32, HD]), ALU.mult).then_inc(qkn_sb, 1)
                    for u in range(4):
                        dve.wait_ge(tr_mm, at(fr, 4, u + 1))
                        dst = (qT, kT)[u // 2]
                        nc.vector.tensor_copy(dst[:, 4 * (u % 2):4 * (u % 2) + 4].rearrange("p a t -> p (a t)"),
                                              rb[f"t{u}"][:].bitcast(F16)).then_inc(tr_sb, 1)

            slots(dve, B, body)

        @block.tensor
        def _(pe):
            pe.wait_ge(setup_pool, 4)

            def take(use, centre):
                k, (i, c) = ORDER.index(use), centre
                while True:
                    k -= 3
                    if k < 0:
                        k, c = k + len(ORDER), c - 1
                    if i is None and c < -1:
                        return rb[use]
                    kind = ORDER[k].rstrip("0123456789")
                    reader, per, place = READER[kind]
                    m = valid((i, c + 1 - place), B)
                    if m is not None:
                        pe.wait_ge(reader, at(m, per, int(ORDER[k][len(kind):] or 0) + 1))
                        return rb[use]

            def scores(mid, hp):
                if hp == 0:
                    pe.wait_ge(tr_sb, at(mid, 4, 4))
                wait(pe, p_sb, at(mid, 8, hp - 1))
                for kt in range(2):
                    for e in range(2):
                        r = slice(64 * e, 64 * e + 64)
                        mm = nc.tensor.matmul(SP[hp % 2][:, e, kt * T:kt * T + T], kT[r, hp, kt * 128:kt * 128 + 128],
                                              qT[r, hp, :], start=True, stop=True)
                mm.then_inc(s_mm, 1)

            def values(mid, hp):
                pe.wait_ge(p_sb, at(mid, 8, hp + 1))
                if hp % 2 == 0:
                    wait(pe, ot_sb, at(mid, 4, hp // 2))
                for kt in range(2):
                    for e in range(2):
                        hd = 2 * hp + e
                        j = 32 * (hd % 4)
                        mm = nc.tensor.matmul(OP[j:j + 32, 0:T], va[mid[1] % 2][:, kt, hd, :], pt[hp % 4][:, e, kt, :],
                                              start=(kt == 0), stop=(kt == 1), skip_group_check=True)
                mm.then_inc(av_mm, 1)

            def body(fr, mid, back, centre):
                if fr is not None:
                    p = fr[1] % 2
                    pe.wait_ge(x_in[p], uses(fr, 48, 48))
                    o = take("z", centre)
                    for k in range(KT):
                        mm = nc.tensor.matmul(o[0:R, 0:T], keep["U"][:, k], xs[p][:, k], start=(k == 0), stop=(k == 2))
                    mm.then_inc(z_mm, 1)
                if mid is not None:
                    scores(mid, 0)
                    scores(mid, 1)
                if back is not None:
                    for u in range(2):
                        o = take(f"sb{u}", centre)
                        pe.wait_ge(ot_sb, at(back, 4, 2 * u + 2))
                        nc.tensor.matmul(o[:], pick[:], OT[:, 2 * u:2 * u + 2].rearrange("p g t -> p (g t)"),
                                         start=True, stop=True).then_inc(sb_mm, 1)
                if fr is not None:
                    pe.wait_ge(z_sb, at(fr, 1, 1))
                    for m in range(KT):
                        o = take(f"d{m}", centre)
                        nc.tensor.matmul(o[0:R, 0:T], Gb[p][:, m * R:m * R + R], zT[:], start=True, stop=True).then_inc(d_mm, 1)
                if mid is not None:
                    values(mid, 0)
                    scores(mid, 2)
                if fr is not None:
                    pe.wait_ge(sq_sb, at(fr, 1, 1))
                    o = take("ss", centre)
                    for k in range(KT):
                        mm = nc.tensor.matmul(o[0:R, 0:T], keep["ones"][:], sq[:, k], start=(k == 0), stop=(k == 2))
                    mm.then_inc(ss_mm, 1)
                if mid is not None:
                    values(mid, 1)
                    scores(mid, 3)
                if back is not None:
                    pe.wait_ge(ol_sb, at(back, 1, 1))
                    for m in range(KT):
                        o = take(f"pj{m}", centre)
                        c = slice(m * R, m * R + R)
                        terms = [(w, x, g) for g in range(4) for w, x in ((wph, oh), (wph, ol), (wpl, oh))]
                        for n, (w, x, g) in enumerate(terms):
                            mm = nc.tensor.matmul(o[0:R, 0:T], w[:, g, c], x[:, g], start=(n == 0), stop=(n == 11))
                        mm.then_inc(pj_mm, 1)
                if fr is not None:
                    pe.wait_ge(hl_sb, at(fr, 1, 1))
                    for t in range(2):
                        for half in range(2):
                            o = take(f"q{2 * t + half}", centre)
                            c = slice(432 * half, 432 * half + 432)
                            terms = [(x, w, k) for k in range(KT) for x, w in ((hh, wqh), (hh, wql), (hl, wqh))]
                            for n, (x, w, k) in enumerate(terms):
                                mm = nc.tensor.matmul(o[:, 0:432], x[:, k, 128 * t:128 * t + 128], w[:, k, c],
                                                      start=(n == 0), stop=(n == 8))
                            mm.then_inc(qkv_mm, 1)
                if mid is not None:
                    for hp in range(2, 8):
                        values(mid, hp)
                        if hp + 2 < 8:
                            scores(mid, hp + 2)
                if fr is not None:
                    pe.wait_ge(stk_sb, at(fr, 2, 2))
                    for u in range(4):
                        o = take(f"t{u}", centre)[:].bitcast(F16)
                        for n in range(4):
                            hd = H * (u // 2) + 8 * (u % 2) + 2 * n
                            for t in range(2):
                                mm = nc.tensor.transpose(o[:, n * T + 128 * t:n * T + 128 * t + 128],
                                                         stk[:, t, hd:hd + 2, :].rearrange("p h d -> p (h d)"), id16[:])
                        mm.then_inc(tr_mm, 1)

            slots(pe, B, body)


def mlp(nc, io, dram, keep, out):
    W = 2 * T
    with ExitStack() as ctx:
        def sb(name, shape, dt=F32):
            return ctx.enter_context(nc.sbuf_tensor(name, shape, dt))

        def sem(name):
            return ctx.enter_context(nc.semaphore(name))

        xp = [sb(f"xp{p}", [R, KT, 2, T]) for p in range(2)]
        mb = [sb(f"mb{p}", [R, 2, AB]) for p in range(2)]
        gt = [sb(f"gt{p}", [R, 2, 2 * GT]) for p in range(2)]
        sq = sb("sqm", [R, KT, W])
        ms = sb("msm", [R, W])
        ln = sb("lnm", [R, W])
        ry = sb("rym", [R, W])
        ru = sb("rum", [R, W])
        rv = sb("rvm", [R, W])
        rs = sb("rsm", [R, W])
        h = sb("hm2", [R, KT, 2, T])
        hh = [sb(f"hh{p}", [R, KT, W], F16) for p in range(2)]
        hl = [sb(f"hl{p}", [R, KT, W], F16) for p in range(2)]
        b1 = sb("b1s", [128, MT])
        g = [sb(f"g{j}", [128, W]) for j in range(3)]
        gh = sb("gh", [128, MT, W], F16)
        gl = sb("gl", [128, MT, W], F16)
        yt = sb("yt", [R, KT, 2, T])
        ys = [sb(f"ys{p}", [R, KT, 2, T]) for p in range(2)]
        w1h = keep["w1h"][:].rearrange("p (k n) -> p k n", k=KT)
        w1l = keep["w1l"][:].rearrange("p (k n) -> p k n", k=KT)
        w2h = keep["w2h"][:].rearrange("p (j n) -> p j n", j=MT)
        w2l = keep["w2l"][:].rearrange("p (j n) -> p j n", j=MT)
        SS = ctx.enter_context(nc.psum_tensor("squares", [128, 512], F32))
        H1 = [ctx.enter_context(nc.psum_tensor(f"hidden{j}", [128, 512], F32)) for j in range(3)]
        Y = [ctx.enter_context(nc.psum_tensor(f"down{j}", [128, 512], F32)) for j in range(KT)]

        x_in = [sem("xp_in0"), sem("xp_in1")]
        b1_in = sem("b1_in")
        y_out = [sem("y_out0"), sem("y_out1")]
        ss_mm, fc1_mm, fc2_mm, down_mm = sem("ss_mm2"), sem("fc1_mm"), sem("fc2_mm"), sem("down_mm")
        sq_sb, ln_sb, ry_sb, hh_sb, g_sb, yt_sb = [sem(n + "_m") for n in ("sq_sb", "ln_sb", "ry_sb", "hh_sb", "g_sb", "yt_sb")]
        ms_sb, newton, rs_sb, h_sb, hl_sb, gh_sb, gl_sb = [sem(n + "_m") for n in ("ms_sb", "newton", "rs_sb", "h_sb", "hl_sb", "gh_sb", "gl_sb")]
        t_sb, y_sb = sem("t_sb_m"), sem("y_sb_m")

        block = ctx.enter_context(nc.Block())

        @block.sync
        def _(sp):
            sp.dma_start(b1[:], io["b1"]).then_inc(b1_in, 16)

            def load(m):
                p, s = m[1] % 2, bass.ds(number(m) * 2, 2)
                wait(sp, y_sb, at(m, 1, -1))
                sp.dma_start(xp[p][:], dram["x2"][s].rearrange("b r k t -> r k b t")).then_inc(x_in[p], 16)
                sp.dma_start(mb[p][:], dram["ab"][1][s].rearrange("b r c -> r b c")).then_inc(x_in[p], 16)
                sp.dma_start(gt[p][:, :, 0:GT], dram["gate"][1][s].rearrange("b r c -> r b c")).then_inc(x_in[p], 16)
                sp.dma_start(gt[p][:, :, GT:2 * GT], dram["gb"][s].rearrange("b r c -> r b c")).then_inc(x_in[p], 16)

            def body(fr, mid, back, _centre):
                if fr is not None:
                    load(fr)
                if back is not None:
                    p, s = back[1] % 2, bass.ds(number(back) * 2, 2)
                    sp.wait_ge(y_sb, at(back, 1, 1))
                    sp.dma_start(out[s].rearrange("b r k t -> r k b t"), ys[p][:]).then_inc(y_out[p], 16)

            slots(sp, NP, body)
            for p in range(2):
                sp.wait_ge(y_out[p], 16 * NP // 2)

        @block.gpsimd
        def _(pool):
            def body(fr, mid, back, _centre):
                if fr is not None:
                    pool.wait_ge(rs_sb, at(fr, 1, 1))
                    nc.gpsimd.tensor_tensor(h[:].rearrange("r k b t -> r k (b t)"), xp[fr[1] % 2][:].rearrange("r k b t -> r k (b t)"),
                                            rs[:, None, :].broadcast_to([R, KT, W]), ALU.mult).then_inc(t_sb, 1)
                if mid is not None:
                    p = mid[1] % 2
                    pool.wait_ge(yt_sb, at(mid, 6, 6))
                    wait(pool, y_out[p], uses(mid, 16, 0))
                    nc.gpsimd.tensor_tensor(ys[p][:], yt[:], xp[p][:], ALU.add).then_inc(y_sb, 1)

            slots(pool, NP, body)

        @block.scalar
        def _(act):
            def hidden(mid, j):
                act.wait_ge(fc1_mm, at(mid, MT, j + 1))
                wait(act, gl_sb, at(mid, MT, j - 2))
                nc.scalar.activation(g[j % 3][:], H1[j % 3][:], ACT.Gelu_apprx_tanh, bias=b1[:, j:j + 1],
                                     scale=1.0 / WS).then_inc(g_sb, 1)

            def body(fr, mid, back, _centre):
                if fr is not None:
                    act.wait_ge(x_in[fr[1] % 2], uses(fr, 64, 64))
                    nc.scalar.activation(sq[:].rearrange("r k (b t) -> r k b t", b=2), xp[fr[1] % 2][:], ACT.Square).then_inc(sq_sb, 1)
                if mid is not None:
                    hidden(mid, 0)
                    hidden(mid, 1)
                    hidden(mid, 2)
                if fr is not None:
                    act.wait_ge(ms_sb, at(fr, 1, 1))
                    nc.scalar.activation(ln[:], ms[:], ACT.Ln, scale=RS * RS).then_inc(ln_sb, 1)
                    act.wait_ge(ln_sb, at(fr, 1, 1))
                    nc.scalar.activation(ry[:], ln[:], ACT.Exp, scale=-0.5).then_inc(ry_sb, 1)
                if mid is not None:
                    hidden(mid, 3)
                    hidden(mid, 4)
                    hidden(mid, 5)
                if fr is not None:
                    act.wait_ge(h_sb, at(fr, 6, 6))
                    nc.scalar.activation(hh[fr[1] % 2][:].rearrange("r k (b t) -> r k b t", b=2), h[:], ACT.Copy).then_inc(hh_sb, 1)
                if mid is not None:
                    hidden(mid, 6)
                    hidden(mid, 7)
                    hidden(mid, 8)
                    p = mid[1] % 2
                    act.wait_ge(x_in[p], uses(mid, 64, 64))
                    wait(act, y_sb, at(mid, 1, 0))
                    for k in range(KT):
                        act.wait_ge(down_mm, at(mid, KT, k + 1))
                        for b in range(2):
                            nc.scalar.activation(yt[:, k, b], Y[k][0:R, b * T:b * T + T], ACT.Identity,
                                                 bias=gt[p][:, b, GT + k:GT + k + 1], scale=gt[p][:, b, k:k + 1]).then_inc(yt_sb, 1)

            act.wait_ge(b1_in, 16)
            slots(act, NP, body)

        @block.vector
        def _(dve):
            def halves(mid, j):
                dve.wait_ge(g_sb, at(mid, MT, j + 1))
                nc.vector.tensor_copy(gh[:, j], g[j % 3][:]).then_inc(gh_sb, 1)
                dve.wait_ge(gh_sb, at(mid, MT, j + 1))
                nc.vector.tensor_tensor(gl[:, j], g[j % 3][:], gh[:, j], ALU.subtract).then_inc(gl_sb, 1)

            def body(fr, mid, back, _centre):
                if mid is not None:
                    halves(mid, 0)
                if fr is not None:
                    dve.wait_ge(ss_mm, at(fr, 1, 1))
                    nc.vector.tensor_scalar(ms[:], SS[0:R], GUARD, None, ALU.max).then_inc(ms_sb, 1)
                if mid is not None:
                    halves(mid, 1)
                    halves(mid, 2)
                    halves(mid, 3)
                if fr is not None:
                    p = fr[1] % 2
                    dve.wait_ge(ry_sb, at(fr, 1, 1))
                    dve.wait_ge(ms_sb, at(fr, 1, 1))
                    nc.vector.scalar_tensor_tensor(ru[:], ms[:], -0.5 * RS * RS, ry[:], ALU.mult, ALU.mult).then_inc(newton, 1)
                    dve.wait_ge(newton, at(fr, 2, 1))
                    nc.vector.tensor_tensor(rv[:], ru[:], ry[:], ALU.mult).then_inc(newton, 1)
                    dve.wait_ge(newton, at(fr, 2, 2))
                    nc.vector.scalar_tensor_tensor(rs[:], rv[:], 1.5, ry[:], ALU.add, ALU.mult).then_inc(rs_sb, 1)
                if mid is not None:
                    halves(mid, 4)
                if fr is not None:
                    dve.wait_ge(x_in[p], uses(fr, 64, 64))
                    dve.wait_ge(t_sb, at(fr, 1, 1))
                    for k in range(KT):
                        for b in range(2):
                            nc.vector.tensor_scalar(h[:, k, b], h[:, k, b], mb[p][:, b, k:k + 1], mb[p][:, b, KT + k:KT + k + 1],
                                                    ALU.mult, ALU.add).then_inc(h_sb, 1)
                if mid is not None:
                    halves(mid, 5)
                    halves(mid, 6)
                if fr is not None:
                    dve.wait_ge(hh_sb, at(fr, 1, 1))
                    nc.vector.tensor_tensor(hl[p][:], h[:].rearrange("r k b t -> r k (b t)"), hh[p][:], ALU.subtract).then_inc(hl_sb, 1)
                if mid is not None:
                    halves(mid, 7)
                    halves(mid, 8)

            slots(dve, NP, body)

        @block.tensor
        def _(pe):
            def up(mid, j):
                p = mid[1] % 2
                if j == 0:
                    pe.wait_ge(hl_sb, at(mid, 1, 1))
                wait(pe, g_sb, at(mid, MT, j - 2))
                c = slice(128 * j, 128 * j + 128)
                terms = [(w, x, k) for k in range(KT) for w, x in ((w1h, hh[p]), (w1h, hl[p]), (w1l, hh[p]))]
                for n, (w, x, k) in enumerate(terms):
                    mm = nc.tensor.matmul(H1[j % 3][:], w[:, k, c], x[:, k], start=(n == 0), stop=(n == 8))
                mm.then_inc(fc1_mm, 1)

            def down(mid, j):
                pe.wait_ge(gl_sb, at(mid, MT, j + 1))
                if j == 0:
                    wait(pe, yt_sb, at(mid, 6, 0))
                for k in range(KT):
                    c = slice(k * R, k * R + R)
                    for n, (w, x) in enumerate(((w2h, gh), (w2h, gl), (w2l, gh))):
                        mm = nc.tensor.matmul(Y[k][0:R], w[:, j, c], x[:, j], start=(j == 0 and n == 0), stop=(j == MT - 1 and n == 2))
                    if j == MT - 1:
                        mm.then_inc(down_mm, 1)

            def body(fr, mid, back, _centre):
                if mid is not None:
                    up(mid, 0)
                if fr is not None:
                    pe.wait_ge(sq_sb, at(fr, 1, 1))
                    wait(pe, ms_sb, at(fr, 1, 0))
                    for k in range(KT):
                        mm = nc.tensor.matmul(SS[0:R], keep["ones"][:], sq[:, k], start=(k == 0), stop=(k == 2))
                    mm.then_inc(ss_mm, 1)
                if mid is not None:
                    for j in range(1, MT):
                        up(mid, j)
                        if j >= 2:
                            down(mid, j - 2)
                    down(mid, MT - 2)
                    down(mid, MT - 1)

            slots(pe, NP, body)


def build(nc, io, out):
    dram = {
        "A": nc.dram_tensor("skew_d", (B, D * D), F32, kind="Internal").ap(),
        "G": nc.dram_tensor("G_d", (B, D, N), F32, kind="Internal").ap(),
        "ab": [nc.dram_tensor(f"ab{p}_d", (B, R, AB), F32, kind="Internal").ap() for p in range(2)],
        "gate": [nc.dram_tensor(f"gate{p}_d", (B, R, GT), F32, kind="Internal").ap() for p in range(2)],
        "gb": nc.dram_tensor("gb_d", (B, R, GT), F32, kind="Internal").ap(),
        "x2": nc.dram_tensor("x2_d", (B, R, KT, T), F32, kind="Internal").ap(),
    }
    with ExitStack() as ctx:
        def sb(name, shape, dt=F32):
            return ctx.enter_context(nc.sbuf_tensor(name, shape, dt))

        keep = {"U": sb("U", [R, KT, R]), "ones": sb("ones", [R, R])}
        for name, parts, w in (("wq", R, KT * QKV), ("wp", 128, 4 * N), ("w1", R, KT * HID), ("w2", 128, MT * N)):
            keep[name + "h"] = sb(name + "h", [parts, w], F16)
            keep[name + "l"] = sb(name + "l", [parts, w], F16)
        prepare(nc, io, dram, keep)
        attention(nc, io, dram, keep)
        mlp(nc, io, dram, keep, out)


def kernel(**inputs):
    import numpy as np
    import concourse.bacc as bacc
    from concourse.bass_utils import run_bass_kernel_spmd

    a = {k: np.asarray(v) for k, v in inputs.items()}

    def rows(w):
        return np.ascontiguousarray(w.T.reshape(KT, R, -1).transpose(1, 0, 2))

    def grid(w):
        iu, ju = np.triu_indices(D, k=1)
        at = np.zeros((D, D), np.int64)
        at[iu, ju] = at[ju, iu] = np.arange(len(iu))
        return w[at.reshape(-1)]

    wp = np.zeros((4, 32, 4, N), np.float32)
    heads = a["L1_cond_proj_w"].T.reshape(4, 4, HD, N)
    wp[:, 0:HD] = heads.transpose(1, 2, 0, 3)
    wp[0, HD, 0] = a["L1_cond_proj_b"]
    arrays = {
        "x": np.ascontiguousarray(a["x"].reshape(B, T, KT, R).transpose(0, 3, 2, 1)),
        "condT": rows(a["cond_1152"]),
        "PT": np.ascontiguousarray(np.concatenate([a["L0_cond_P"].T] * 2)),
        "WT": rows(grid(a["L0_cond_W"])),
        "bfull": grid(a["L0_cond_b"])[None],
        "adaT": rows(a["L1_cond_ada_w"]),
        "adab": np.ascontiguousarray(a["L1_cond_ada_b"].reshape(MODS, R).T),
        "wqT": rows(a["L1_cond_qkv_w"]).reshape(R, -1),
        "bq": a["L1_cond_qkv_b"][None],
        "wpT": np.ascontiguousarray(wp.reshape(128, -1)),
        "w1T": rows(a["L1_cond_fc1_w"]).reshape(R, -1),
        "b1": np.ascontiguousarray(a["L1_cond_fc1_b"].reshape(MT, 128).T),
        "w2T": np.ascontiguousarray(a["L1_cond_fc2_w"].T.reshape(MT, 128, N).transpose(1, 0, 2)).reshape(128, -1),
        "b2": np.ascontiguousarray(a["L1_cond_fc2_b"].reshape(KT, R).T),
    }
    for n in ("g1", "g2", "qg", "kg"):
        arrays[n] = a["L1_cond_" + n][None]
    nc = bacc.Bacc("TRN2", target_bir_lowering=False, num_devices=1)
    io = {k: nc.dram_tensor(k + "_in", v.shape, F32, kind="ExternalInput").ap() for k, v in arrays.items()}
    out = nc.dram_tensor("y_out", (B, R, KT, T), F32, kind="ExternalOutput").ap()
    build(nc, io, out)
    r = run_bass_kernel_spmd(nc, [{k + "_in": v for k, v in arrays.items()}], core_ids=[0])
    y = r.results[0]["y_out"]
    return np.ascontiguousarray(y.transpose(0, 3, 2, 1)).reshape(B, T, N)
```

```python
from contextlib import ExitStack

import concourse.bass as bass
from concourse import mybir

F32 = mybir.dt.float32
F16 = mybir.dt.float16
ALU = mybir.AluOpType
ACT = mybir.ActivationFunctionType
AX = mybir.AxisListType

B, T, N, D = 32, 256, 288, 64
R, KT = 96, 3
H, HD = 16, 18
QKV = 3 * N
HID = 4 * N
MT = HID // 128
HP = H // 2
NP = B // 2
WS = 64.0
MODS = 6 * KT
AB, GT = 2 * KT, KT
DOUBLE = 13
RS = 256.0
GUARD = 1e-24
BIG_NORM = float(N) ** 0.5
HEAD_NORM = float(HD) ** 0.5
QR_PER = 4
ROUNDS = D // QR_PER
FIRST_PRODUCT = 3
CH = 4


def wait(eng, sem, value):
    if isinstance(value, int) and value <= 0:
        return
    eng.wait_ge(sem, value)


class Count:

    def __init__(self, sem, base=0):
        self.sem, self.base, self.n = sem, base, 0

    def inc(self, ins):
        ins.then_inc(self.sem, 1)
        self.n += 1
        return self.base + self.n


def prepare(nc, io, dram, keep):
    with ExitStack() as ctx:
        def sb(name, shape, dt=F32):
            return ctx.enter_context(nc.sbuf_tensor(name, shape, dt))

        def sem(name):
            return ctx.enter_context(nc.semaphore(name))

        At = sb("At", [128, N])
        prod = sb("prod", [128, N])
        sqv = sb("sqv", [128, N])
        ident = sb("ident", [128, 128])
        identd = sb("identd", [128, D])
        gtm = sb("gtm", [128, D])
        lem = sb("lem", [128, D])
        sel = sb("sel", [128, 2, 128])
        dots = sb("dots", [128, 1])
        ssq = sb("ssq", [128, 1])
        sgn = sb("sgn", [128, 1])
        sig = sb("sig", [128, 1])
        st = sb("st", [128, 2])
        tiny = sb("tiny", [128, 1])
        rsig = sb("rsig", [128, 1])
        sig2 = sb("sig2", [128, 1])
        nwt = sb("nwt", [128, 2])
        rt = sb("rt", [128, 1])
        wv = sb("wv", [128, 1])
        nw = sb("nw", [128, 1])
        stall = sb("stall", [128, D, 2])
        scol = sb("scol", [128, 2])
        junk = sb("junk", [128, D])
        rcol = sb("rcol", [128, 3])
        Vt = sb("Vt", [128, N])
        V = sb("V", [R, KT, D])
        XY = sb("XY", [D, 2, 2 * D])
        XT = sb("XT", [D, 2, D])
        Yd = sb("Yd", [D, 2, D])
        UT = sb("UT", [128, N])
        cT = sb("cT", [R, KT, B])
        cE = sb("cE", [R, KT, B])
        cR = sb("cR", [R, KT, B])
        sT = sb("sT", [R, KT, B])
        bfull = sb("bfull", [B, D * D])
        wfull = sb("wfull", [R, 2, KT, 512])
        vraw = sb("vraw", [B, 2, 512])
        vall = sb("vall", [B, D * D])
        Ald = sb("Ald", [128, 16, D])
        mask = sb("mask", [128, D])
        E = sb("E", [128, 16, 128])
        ET = sb("ET", [128, 16, 128])
        F = sb("F", [128, 16, 128])
        Q = sb("Q", [128, 16, 128])
        two = sb("two", [128, 128])
        half = sb("half", [128, 128])
        adaw = sb("adaw", [R, KT, 6 * N])
        adab = sb("adab", [R, MODS])
        mod = sb("mod", [R, MODS, B])
        moda = sb("moda", [R, B, 2, AB])
        modg = sb("modg", [R, B, 2, GT])
        modb = sb("modb", [R, B, GT])
        gs = sb("gs", [R, 2])
        b2 = sb("b2", [R, KT])
        Gs = sb("Gs", [128, 2, N])
        wraw = sb("wraw", [128, KT * QKV + 4 * N + KT * HID + MT * N])
        ps = [ctx.enter_context(nc.psum_tensor(f"prep{i}", [128, 512], F32)) for i in range(8)]
        VA, VB = ps[0], ps[1]
        EP, TP, MP = ps[2:4], ps[4:6], ps[6:8]

        p_in = sem("p_in")
        c_in = sem("c_in")
        bias_in = sem("bias_in")
        wf_in = [sem("wf_in0"), sem("wf_in1")]
        ada_in = sem("ada_in")
        small_in = sem("small_in")
        a_in = sem("a_in")
        raw_in = sem("raw_in")
        zeroed = sem("zeroed")
        masks = sem("masks")
        pool_step = sem("pool_step")
        dve_step = sem("dve_step")
        sel_ready = sem("sel_ready")
        row_bc = sem("row_bc")
        ssq_ready = sem("ssq_ready")
        sig_ready = sem("sig_ready")
        rcol_ready = sem("rcol_ready")
        st_ready = sem("st_ready")
        st_saved = sem("st_saved")
        at_updated = sem("at_updated")
        exp_c = sem("exp_c")
        silu_ready = sem("silu_ready")
        v_mm = sem("v_mm")
        v_raw = sem("v_raw")
        v_ready = sem("v_ready")
        v_out = sem("v_out")
        a_ready = sem("a_ready")
        at_neg = sem("at_neg")
        q_ready = sem("q_ready")
        prod_mm = sem("prod_mm")
        prod_sb = sem("prod_sb")
        tr_mm = sem("tr_mm")
        tr_sb = sem("tr_sb")
        f_ready = sem("f_ready")
        mod_mm = sem("mod_mm")
        mod_sb = sem("mod_sb")
        gate_t = sem("gate_t")
        mods_done = sem("mods_done")
        mods_out = sem("mods_out")
        vt_ready = sem("vt_ready")
        wy_pe = sem("wy_pe")
        wy_sb = sem("wy_sb")
        g_mm = sem("g_mm")
        g_sb = sem("g_sb")
        g_out = [sem("g_out0"), sem("g_out1")]
        w_used = sem("w_used")
        w_scaled = sem("w_scaled")
        w_high = sem("w_high")

        block = ctx.enter_context(nc.Block())
        NV = D * D // 512

        splits, at = [], 0
        for name, parts, w in (("wq", R, KT * QKV), ("wp", 128, 4 * N), ("w1", R, KT * HID), ("w2", 128, MT * N)):
            splits.append((keep[name + "h"], keep[name + "l"], io[name + "T"], parts, at, w))
            at += w

        @block.sync
        def _(sp):
            sp.dma_start(At[:], io["PT"]).then_inc(p_in, 16)
            sp.dma_start(cT[:], io["condT"]).then_inc(c_in, 16)
            for c in range(2):
                sp.dma_start(wfull[:, c], io["WT"][:, :, c * 512:(c + 1) * 512]).then_inc(wf_in[c], 16)
            sp.dma_start(bfull[:], io["bfull"].broadcast_to([B, D * D])).then_inc(bias_in, 16)
            sp.dma_start(adab[:], io["adab"]).then_inc(small_in, 16)
            sp.dma_start(b2[:], io["b2"]).then_inc(small_in, 16)
            sp.dma_start(gs[:, 0:1], io["g1"].broadcast_to([R, 1])).then_inc(small_in, 16)
            sp.dma_start(gs[:, 1:2], io["g2"].broadcast_to([R, 1])).then_inc(small_in, 16)
            for c in range(2, NV):
                sp.wait_ge(v_mm, c - 1)
                sp.dma_start(wfull[:, c % 2], io["WT"][:, :, c * 512:(c + 1) * 512]).then_inc(wf_in[c % 2], 16)
            sp.wait_ge(v_ready, NV)
            sp.dma_start(dram["A"], vall[:]).then_inc(v_out, 16)
            sp.wait_ge(v_out, 16)
            for p in range(2):
                sp.dma_start(Ald[64 * p:64 * p + 64], dram["A"].rearrange("(p q) (i j) -> p i q j", p=2, i=D)[p]).then_inc(a_in, 16)
            sp.wait_ge(mods_done, 1)
            for ph in range(2):
                sp.dma_start(dram["ab"][ph].rearrange("b r c -> r b c"), moda[:, :, ph]).then_inc(mods_out, 16)
                sp.dma_start(dram["gate"][ph].rearrange("b r c -> r b c"), modg[:, :, ph]).then_inc(mods_out, 16)
            sp.dma_start(dram["gb"].rearrange("b r c -> r b c"), modb[:]).then_inc(mods_out, 16)
            sp.wait_ge(mods_out, 80)
            for q in range(16):
                sp.wait_ge(g_sb, q + 1)
                for p in range(2):
                    sp.dma_start(dram["G"][16 * p + q], Gs[64 * p:64 * p + 64, q % 2]).then_inc(g_out[q % 2], 16)
            for p in range(2):
                sp.wait_ge(g_out[p], 32 * 8)

        @block.gpsimd
        def _(pool):
            pc = Count(pool_step)

            def link(ins):
                pool.wait_ge(pool_step, pc.inc(ins))

            for t, w in ((ident, 128), (two, 128), (half, 128), (identd, D)):
                ins = nc.gpsimd.memset(t[:], 0.0)
            for t in (gtm, lem, mask):
                ins = nc.gpsimd.memset(t[:], 0.0)
            link(ins)
            for t, v in ((ident, 1.0), (two, 2.0), (half, 0.5)):
                nc.gpsimd.affine_select(out=t[:], in_=t[:], compare_op=ALU.not_equal, fill=v, base=0,
                                        pattern=[[-1, 128]], channel_multiplier=1)
            for p in range(2):
                h = slice(64 * p, 64 * p + 64)
                sc = 2.0 ** -DOUBLE
                nc.gpsimd.affine_select(out=identd[h], in_=identd[h], compare_op=ALU.not_equal, fill=1.0, base=0,
                                        pattern=[[-1, D]], channel_multiplier=1)
                nc.gpsimd.affine_select(out=gtm[h], in_=gtm[h], compare_op=ALU.is_ge, fill=1.0, base=0,
                                        pattern=[[1, D]], channel_multiplier=-1)
                nc.gpsimd.affine_select(out=lem[h], in_=lem[h], compare_op=ALU.is_gt, fill=1.0, base=0,
                                        pattern=[[-1, D]], channel_multiplier=1)
                ins = nc.gpsimd.affine_select(out=mask[h], in_=mask[h], compare_op=ALU.is_ge, fill=sc, base=0,
                                              pattern=[[-1, D]], channel_multiplier=1)
                link(ins)
                ins = nc.gpsimd.affine_select(out=mask[h], in_=mask[h], compare_op=ALU.is_ge, fill=-sc, base=0,
                                        pattern=[[1, D]], channel_multiplier=-1)
            link(ins)
            nc.gpsimd.memset(E[:], 0.0).then_inc(masks, 1)

            def make_sel(j):
                if not (isinstance(j, int) and j < 2):
                    pool.wait_ge(row_bc, j * 2 - 2)
                nc.gpsimd.tensor_copy(sel[:, par(j)], ident[:, col(j)].broadcast_to([128, 128])).then_inc(sel_ready, 1)

            parity = [0]

            def par(j):
                return parity[0]

            def col(j):
                return bass.ds(j, 1)

            def sel_step(j, s):
                parity[0] = s % 2
                make_sel(j)

            sel_step(0, 0)

            def split(n):
                hi, lo, _src, parts, c0, w = splits[n]
                pool.wait_ge(w_high, n + 1)
                nc.gpsimd.tensor_tensor(lo[0:parts], wraw[0:parts, c0:c0 + w], hi[0:parts], ALU.subtract).then_inc(w_used, 1)

            def v_chunk(c):
                pool.wait_ge(v_raw, c + 1)
                if c == 0:
                    pool.wait_ge(bias_in, 16)
                nc.gpsimd.tensor_tensor(vall[:, c * 512:(c + 1) * 512], vraw[:, c % 2], bfull[:, c * 512:(c + 1) * 512],
                                        ALU.add).then_inc(v_ready, 1)

            def skew():
                pool.wait_ge(a_in, 32)
                pool.wait_ge(sel_ready, 2 * QR_PER + 2)
                for p in range(2):
                    h = slice(64 * p, 64 * p + 64)
                    nc.gpsimd.tensor_tensor(E[h, :, h], Ald[h], mask[h, None, :].broadcast_to([64, 16, D]), ALU.mult).then_inc(a_ready, 1)
                    pool.wait_ge(a_ready, p + 1)
                link(nc.gpsimd.tensor_scalar(Q[:], E[:], 1.0 / 6, None, ALU.mult))
                link(nc.gpsimd.tensor_tensor(Q[:], Q[:], half[:, None, :].broadcast_to([128, 16, 128]), ALU.add))

            def taylor(c):
                q = slice(CH * c, CH * c + CH)
                pool.wait_ge(prod_sb, c + 1)
                link(nc.gpsimd.tensor_scalar(E[:, q], F[:, q], 1.0 / 24, None, ALU.mult))
                nc.gpsimd.tensor_tensor(Q[:, q], Q[:, q], E[:, q], ALU.add).then_inc(q_ready, 1)

            def plus_two(c, k):
                q = slice(CH * c, CH * c + CH)
                pool.wait_ge(prod_sb, k + 1)
                nc.gpsimd.tensor_tensor(F[:, q], E[:, q], two[:, None, :].broadcast_to([128, CH, 128]),
                                        ALU.add).then_inc(f_ready, 1)

            def round_(r):
                for s in range(QR_PER):
                    j = QR_PER * r + s
                    if isinstance(r, int):
                        if j + 1 < D:
                            sel_step(j + 1, s + 1)
                        if r < 2:
                            v_chunk(j)
                        if r == 2 and s == 0:
                            skew()
                        if r == FIRST_PRODUCT:
                            taylor(s)
                        if r > FIRST_PRODUCT:
                            plus_two(s, (r - FIRST_PRODUCT) * CH + s)
                    else:
                        sel_step(r * QR_PER + s + 1, s + 1)
                        plus_two(s, r * CH + (s - FIRST_PRODUCT * CH))

            for r in range(FIRST_PRODUCT + 2):
                round_(r)
            with pool.Fori(FIRST_PRODUCT + 2, ROUNDS - 1) as r:
                round_(r)
            round_(ROUNDS - 1)
            for r in (ROUNDS, ROUNDS + 1)[:1]:
                for c in range(4):
                    plus_two(c, (r - FIRST_PRODUCT) * CH + c)
            pool.wait_ge(mod_sb, 2)
            pool.wait_ge(gate_t, 1)
            pool.wait_ge(small_in, 64)
            for ph, (sh, scl, gt) in enumerate(((0, 3, 6), (9, 12, 15))):
                v = mod[:, scl:scl + KT, :].rearrange("r c b -> r b c")
                link(nc.gpsimd.tensor_scalar(moda[:, :, ph, 0:KT], v, 1.0, BIG_NORM * RS, ALU.add, ALU.mult))
                link(nc.gpsimd.tensor_scalar(moda[:, :, ph, 0:KT], moda[:, :, ph, 0:KT], gs[:, ph:ph + 1], None, ALU.mult))
                link(nc.gpsimd.tensor_copy(moda[:, :, ph, KT:AB], mod[:, sh:sh + KT, :].rearrange("r c b -> r b c")))
                link(nc.gpsimd.tensor_scalar(modg[:, :, ph], mod[:, gt:gt + KT, :].rearrange("r c b -> r b c"),
                                             1.0 / WS, None, ALU.mult))
            nc.gpsimd.tensor_tensor(modb[:], mod[:, 15:18, :].rearrange("r c b -> r b c"),
                                    b2[:, None, :].broadcast_to([R, B, KT]), ALU.mult).then_inc(mods_done, 1)
            for n in range(len(splits)):
                split(n)

        @block.scalar
        def _(act):
            act.dma_start(adaw[:], io["adaT"]).then_inc(ada_in, 16)
            for _h, _l, src, parts, c0, w in splits:
                act.dma_start(wraw[0:parts, c0:c0 + w], src).then_inc(raw_in, 16)
            act.wait_ge(c_in, 16)
            nc.scalar.activation(cE[:], cT[:], ACT.Exp, scale=-1.0).then_inc(exp_c, 1)

            act.wait_ge(dve_step, 1)

            def square(j):
                act.wait_ge(row_bc, 2 * j + 1)
                nc.scalar.activation(sqv[:], VA[:, 0:N], ACT.Square, accum_out=ssq[:]).then_inc(ssq_ready, 1)
                act.wait_ge(ssq_ready, j + 1)
                nc.scalar.activation(sig[:], ssq[:], ACT.Sqrt, bias=tiny[:]).then_inc(sig_ready, 1)

            def save_st(j):
                act.wait_ge(st_ready, j + 1)
                nc.scalar.activation(stall[:, bass.ds(j, 1), :], st[:, None, :], ACT.Copy).then_inc(st_saved, 1)

            def evac_product(c, k):
                act.wait_ge(prod_mm, k + 1)
                q = slice(CH * c, CH * c + CH)
                dst = F if isinstance(k, int) and k < 4 else E
                nc.scalar.activation(dst[:, q], EP[c % 2][:].rearrange("p (q n) -> p q n", q=CH), ACT.Copy).then_inc(prod_sb, 1)

            def evac_turned(c, k):
                act.wait_ge(tr_mm, k - 3)
                q = slice(CH * c, CH * c + CH)
                nc.scalar.activation(ET[:, q], TP[c % 2][:].rearrange("p (q n) -> p q n", q=CH), ACT.Copy).then_inc(tr_sb, 1)

            def round_(r):
                for s in range(QR_PER):
                    j = r * QR_PER + s
                    square(j)
                    save_st(j)
                    if isinstance(r, int):
                        if r < 2:
                            act.wait_ge(v_mm, j + 1)
                            if j >= 2:
                                act.wait_ge(v_ready, j - 1)
                            nc.scalar.activation(vraw[:, j % 2], MP[j % 2][0:B, :], ACT.Copy).then_inc(v_raw, 1)
                        if r == 2 and s == 1:
                            act.wait_ge(a_ready, 2)
                            nc.scalar.activation(ET[:], E[:], ACT.Copy, scale=-1.0).then_inc(at_neg, 1)
                        if r == FIRST_PRODUCT and s < 2:
                            act.wait_ge(mod_mm, 1)
                        if r >= FIRST_PRODUCT:
                            k = (r - FIRST_PRODUCT) * CH + s
                            evac_product(s, k)
                            if k >= 5:
                                evac_turned((s - 1) % 4, k - 1)
                    else:
                        evac_product(s, r * CH + (s - FIRST_PRODUCT * CH))
                        evac_turned((s - 1) % 4, r * CH + (s - 1 - FIRST_PRODUCT * CH))

            for r in range(FIRST_PRODUCT + 2):
                round_(r)
            with act.Fori(FIRST_PRODUCT + 2, ROUNDS - 1) as r:
                round_(r)
            round_(ROUNDS - 1)
            act.wait_ge(rcol_ready, 1)
            nc.scalar.activation(rcol[:, 1:2], rcol[:, 0:1], ACT.Sqrt).then_inc(sig_ready, 1)
            for k in range((ROUNDS - FIRST_PRODUCT) * CH, (ROUNDS + 2 - FIRST_PRODUCT) * CH + 1):
                if k < (ROUNDS + 2 - FIRST_PRODUCT) * CH:
                    evac_product(k % 4, k)
                evac_turned((k - 1) % 4, k - 1)
            act.wait_ge(mod_sb, 2)
            nc.scalar.activation(mod[:, 6:9], mod[:, 6:9], ACT.Tanh)
            nc.scalar.activation(mod[:, 15:18], mod[:, 15:18], ACT.Tanh).then_inc(gate_t, 1)
            act.wait_ge(raw_in, 16 * len(splits))
            for n, (hi, _l, _s, parts, c0, w) in enumerate(splits):
                nc.scalar.activation(wraw[0:parts, c0:c0 + w], wraw[0:parts, c0:c0 + w], ACT.Copy, scale=WS).then_inc(w_scaled, 1)
                act.wait_ge(w_scaled, n + 1)
                nc.scalar.activation(hi[0:parts], wraw[0:parts, c0:c0 + w], ACT.Copy).then_inc(w_high, 1)
            for q in range(16):
                act.wait_ge(g_mm, q + 1)
                if q >= 2:
                    act.wait_ge(g_out[q % 2], 32 * (q // 2))
                nc.scalar.activation(Gs[:, q % 2], MP[q % 2][:, 0:N], ACT.Copy).then_inc(g_sb, 1)

        @block.vector
        def _(dve):
            dc = Count(dve_step)

            def link(ins):
                dve.wait_ge(dve_step, dc.inc(ins))

            nc.vector.memset(keep["ones"][:], 1.0)
            nc.vector.memset(st[:], 0.0)
            link(nc.vector.memset(tiny[:], 1e-30))
            dve.wait_ge(exp_c, 1)
            link(nc.vector.tensor_scalar(cE[:], cE[:], 1.0, None, ALU.add))
            link(nc.vector.reciprocal(cR[:], cE[:]))
            nc.vector.tensor_tensor(sT[:], cT[:], cR[:], ALU.mult).then_inc(silu_ready, 1)
            dve.wait_ge(masks, 1)
            dve.wait_ge(p_in, 16)

            def step(j):
                at = bass.ds(j, 1)
                dve.wait_ge(row_bc, 2 * j + 2)
                dots_at = dc.inc(nc.vector.tensor_tensor_reduce(prod[:], At[:], VB[:, 0:N], 1.0, 0.0, ALU.mult, ALU.add, dots[:]))
                sg_at = dc.inc(nc.vector.tensor_scalar(sgn[:], VB[:, at], 0.0, -1.0, ALU.is_ge, ALU.mult))
                dve.wait_ge(sig_ready, j + 1)
                link(nc.vector.reciprocal(rsig[:], sig[:]))
                link(nc.vector.scalar_tensor_tensor(sig2[:], ssq[:], rsig[:], sig[:], ALU.mult, ALU.add))
                if not (isinstance(j, int) and j == 0):
                    dve.wait_ge(st_saved, j)
                link(nc.vector.scalar_tensor_tensor(st[:, 0:1], sgn[:], 0.5, sig2[:], ALU.add, ALU.mult))
                nc.vector.scalar_tensor_tensor(st[:, 1:2], VB[:, at], st[:, 0:1], st[:, 0:1], ALU.subtract, ALU.mult).then_inc(st_ready, 1)
                dve.wait_ge(dve_step, dots_at)
                w_at = dc.inc(nc.vector.scalar_tensor_tensor(wv[:], At[:, at], st[:, 0:1], dots[:], ALU.mult, ALU.subtract))
                dve.wait_ge(st_ready, j + 1)
                link(nc.vector.reciprocal(rt[:], st[:, 1:2]))
                dve.wait_ge(dve_step, w_at)
                link(nc.vector.scalar_tensor_tensor(nw[:], wv[:], rt[:], gtm[:, at], ALU.mult, ALU.mult))
                link(nc.vector.scalar_tensor_tensor(At[:], VB[:, 0:N], nw[:], At[:], ALU.mult, ALU.add))
                ins = nc.vector.tensor_tensor(At[:, at], At[:, at], lem[:, at], ALU.mult)
                ins.then_inc(at_updated, 1)

            link(nc.vector.tensor_scalar(gtm[:], gtm[:], -1.0, None, ALU.mult))

            def round_(r):
                for s in range(QR_PER):
                    step(r * QR_PER + s)

            for r in range(FIRST_PRODUCT):
                round_(r)
            dve.wait_ge(mod_mm, 1)
            dve.wait_ge(small_in, 64)
            for c in range(2):
                nc.vector.tensor_tensor(mod[:, 9 * c:9 * c + 9], MP[c][0:R, 0:9 * B].rearrange("r (c b) -> r c b", b=B),
                                        adab[:, 9 * c:9 * c + 9, None].broadcast_to([R, 9, B]), ALU.add).then_inc(mod_sb, 1)
            per_round = None
            before = dc.n
            round_(FIRST_PRODUCT)
            per_round = dc.n - before
            start = dc.n
            with dve.Fori(FIRST_PRODUCT + 1, ROUNDS) as r:
                dc.base, dc.n = r * per_round, start - (FIRST_PRODUCT + 1) * per_round
                round_(r)
            dc.base, dc.n = 0, start + (ROUNDS - FIRST_PRODUCT - 1) * per_round
            dve.wait_ge(st_saved, D)
            dve.wait_ge(at_updated, D)
            for k in range(2):
                ins = nc.vector.tensor_tensor_reduce(junk[:], stall[:, :, k], identd[:], -1.0, 0.0, ALU.mult, ALU.add, scol[:, k:k + 1])
                link(ins)
            nc.vector.reciprocal(rcol[:, 0:1], scol[:, 1:2]).then_inc(rcol_ready, 1)
            dve.wait_ge(sig_ready, D + 1)
            link(nc.vector.tensor_tensor(nwt[:, 0:1], rcol[:, 1:2], rcol[:, 1:2], ALU.mult))
            link(nc.vector.scalar_tensor_tensor(nwt[:, 1:2], nwt[:, 0:1], -0.5, scol[:, 1:2], ALU.mult, ALU.mult))
            link(nc.vector.scalar_tensor_tensor(rcol[:, 2:3], nwt[:, 1:2], 1.5, rcol[:, 1:2], ALU.add, ALU.mult))
            link(nc.vector.scalar_tensor_tensor(At[:, 0:D], identd[:], scol[:, 0:1], At[:, 0:D], ALU.mult, ALU.add))
            nc.vector.tensor_scalar(Vt[:], At[:], rcol[:, 2:3], None, ALU.mult).then_inc(vt_ready, 1)
            wy = Count(wy_sb)
            dve.wait_ge(wy_pe, 1)
            wy.inc(nc.vector.tensor_copy(V[:], VA[0:R, 0:KT * D].rearrange("r (k d) -> r k d", k=KT)))
            dve.wait_ge(wy_pe, 2)
            link(nc.vector.tensor_tensor(junk[0:D], lem[0:D], identd[0:D], ALU.subtract))
            link(nc.vector.scalar_tensor_tensor(XY[:, 0, 0:D], VB[0:D, 0:D], -1.0, junk[0:D], ALU.mult, ALU.mult))
            link(nc.vector.tensor_tensor(XT[:, 0], VB[0:D, 0:D], gtm[0:D], ALU.mult))
            dve.wait_ge(vt_ready, 1)
            wy.inc(nc.vector.tensor_copy(XY[:, 0, D:2 * D], Vt[0:D, 0:D]))
            for k in range(6):
                a, b = k % 2, (k + 1) % 2
                dve.wait_ge(wy_pe, 3 + k)
                last = nc.vector.tensor_tensor(XY[:, b, D:2 * D], VA[0:D, D:2 * D], XY[:, a, D:2 * D], ALU.add)
                if k < 5:
                    nc.vector.tensor_copy(XY[:, b, 0:D], VA[0:D, 0:D])
                    last = nc.vector.tensor_copy(XT[:, b], VB[0:D, 0:D])
                wy.inc(last)
            dve.wait_ge(wy_sb, 8)
            wy.inc(nc.vector.tensor_copy(Yd[:], XY[:, 0, None, D:2 * D].broadcast_to([D, 2, D])))
            dve.wait_ge(wy_pe, 9)
            nc.vector.tensor_scalar(UT[:, D:N], VA[:, D:N], -1.0, None, ALU.mult)
            wy.inc(nc.vector.scalar_tensor_tensor(UT[:, 0:D], VA[:, 0:D], -1.0, identd[:], ALU.mult, ALU.add))
            dve.wait_ge(wy_pe, 10)
            nc.vector.memset(keep["U"][:], 0.0).then_inc(wy_sb, 1)
            dve.wait_ge(wy_sb, 11)
            wy.inc(nc.vector.tensor_copy(keep["U"][:, :, 0:D], VB[0:R, 0:KT * D].rearrange("r (k d) -> r k d", k=KT)))
            dve.wait_ge(wy_sb, 12)

        @block.tensor
        def _(pe):
            pe.wait_ge(p_in, 16)
            pe.wait_ge(masks, 1)

            def bcast(j, s):
                pe.wait_ge(sel_ready, j + 1)
                if not (isinstance(j, int) and j == 0):
                    pe.wait_ge(at_updated, j)
                for t in (VA, VB):
                    nc.tensor.matmul(t[:, 0:N], sel[:, s % 2], At[:], start=True, stop=True).then_inc(row_bc, 1)

            def product(c, k):
                if isinstance(k, int) and k < 4:
                    pe.wait_ge(at_neg, 1)
                elif isinstance(k, int) and k < 8:
                    pe.wait_ge(q_ready, k - 3)
                else:
                    pe.wait_ge(f_ready, k - 7)
                    pe.wait_ge(tr_sb, k - 7)
                if not (isinstance(k, int) and k < 2):
                    pe.wait_ge(prod_sb, k - 1)
                out = EP[c % 2]
                for n in range(CH):
                    q = CH * c + n
                    o = out[:, 128 * n:128 * n + 128]
                    if isinstance(k, int) and k < 4:
                        mm = nc.tensor.matmul(o, ET[:, q], E[:, q], start=True, stop=True)
                    elif isinstance(k, int) and k < 8:
                        nc.tensor.matmul(o, ET[:, q], ident[:], start=True, stop=False)
                        mm = nc.tensor.matmul(o, F[:, q], Q[:, q], start=False, stop=True)
                    else:
                        mm = nc.tensor.matmul(o, ET[:, q], F[:, q], start=True, stop=True)
                mm.then_inc(prod_mm, 1)

            def turn(c, k):
                pe.wait_ge(prod_sb, k + 1)
                if not (isinstance(k, int) and k < 6):
                    pe.wait_ge(tr_sb, k - 5)
                for n in range(CH):
                    mm = nc.tensor.transpose(TP[c % 2][:, 128 * n:128 * n + 128], E[:, CH * c + n], ident[:])
                mm.then_inc(tr_mm, 1)

            def round_(r):
                for s in range(QR_PER):
                    j = r * QR_PER + s
                    bcast(j, s)
                    if isinstance(r, int):
                        if r < 2:
                            if j == 0:
                                pe.wait_ge(silu_ready, 1)
                            pe.wait_ge(wf_in[j % 2], 16 * (j // 2 + 1))
                            if j >= 2:
                                pe.wait_ge(v_raw, j - 1)
                            for k in range(KT):
                                mm = nc.tensor.matmul(MP[j % 2][0:B, :], sT[:, k], wfull[:, j % 2, k], start=(k == 0), stop=(k == 2))
                            mm.then_inc(v_mm, 1)
                        if r == 2:
                            if s == 0:
                                pe.wait_ge(ada_in, 16)
                                pe.wait_ge(v_raw, 8)
                            lo, hi = (0, 5, 9, 14, 18)[s], (0, 5, 9, 14, 18)[s + 1]
                            for c in range(lo, hi):
                                o = MP[c // 9][0:R, (c % 9) * B:(c % 9 + 1) * B]
                                for k in range(KT):
                                    mm = nc.tensor.matmul(o, adaw[:, k, c * R:(c + 1) * R], sT[:, k], start=(k == 0), stop=(k == 2))
                            if s == 3:
                                mm.then_inc(mod_mm, 1)
                        if r >= FIRST_PRODUCT:
                            k = (r - FIRST_PRODUCT) * CH + s
                            product(s, k)
                            if k >= 5:
                                turn((s - 1) % 4, k - 1)
                    else:
                        product(s, r * CH + (s - FIRST_PRODUCT * CH))
                        turn((s - 1) % 4, r * CH + (s - 1 - FIRST_PRODUCT * CH))

            for r in range(FIRST_PRODUCT + 2):
                round_(r)
            with pe.Fori(FIRST_PRODUCT + 2, ROUNDS - 1) as r:
                round_(r)
            round_(ROUNDS - 1)
            KEND = (ROUNDS + 2 - FIRST_PRODUCT) * CH

            def tail(k):
                if k < KEND:
                    product(k % 4, k)
                turn((k - 1) % 4, k - 1)

            wy = Count(wy_pe)
            kk = (ROUNDS - FIRST_PRODUCT) * CH
            tail(kk)
            pe.wait_ge(vt_ready, 1)
            for k in range(KT):
                mm = nc.tensor.transpose(VA[0:R, D * k:D * k + D], Vt[0:D, R * k:R * k + R], ident[0:D, 0:D])
            wy.inc(mm)
            tail(kk + 1)
            pe.wait_ge(wy_sb, 1)
            for k in range(KT):
                mm = nc.tensor.matmul(VB[0:D, 0:D], V[:, k], V[:, k], start=(k == 0), stop=(k == 2))
            wy.inc(mm)
            for k in range(6):
                if k < 6 and kk + 2 + k <= KEND:
                    tail(kk + 2 + k)
                pe.wait_ge(wy_sb, 2 + k)
                mm = nc.tensor.matmul(VA[0:D, 0:2 * D], XT[:, k % 2], XY[:, k % 2], start=True, stop=True)
                if k < 5:
                    mm = nc.tensor.matmul(VB[0:D, 0:D], XY[:, k % 2, 0:D], XT[:, k % 2], start=True, stop=True)
                wy.inc(mm)
            for k in range(kk + 8, KEND + 1):
                tail(k)
            pe.wait_ge(wy_sb, 9)
            wy.inc(nc.tensor.matmul(VA[:, 0:N], Yd[:].rearrange("p a d -> p (a d)"), Vt[0:D, :], start=True, stop=True))
            pe.wait_ge(wy_sb, 10)
            for k in range(KT):
                mm = nc.tensor.transpose(VB[0:R, D * k:D * k + D], UT[0:D, R * k:R * k + R], ident[0:D, 0:D])
            wy.inc(mm)
            pe.wait_ge(mod_sb, 2)
            pe.wait_ge(tr_sb, KEND - 4)
            for q in range(16):
                if q >= 2:
                    pe.wait_ge(g_sb, q - 1)
                nc.tensor.matmul(MP[q % 2][:, 0:N], ET[:, q], UT[:], start=True, stop=True).then_inc(g_mm, 1)


def at(m, per, k=0):
    i, c = m
    return per * c + k if i is None else i * (2 * per) + (per * c + k)


def after(m, d):
    return (m[0], m[1] + d)


def number(m):
    return m[1] if m[0] is None else m[0] * 2 + m[1]


def uses(m, per, k=0):
    i, c = m
    return per * (c // 2) + k if i is None else i * per + (per * (c // 2) + k)


def valid(m, last):
    return None if m[0] is None and not 0 <= m[1] < last else m


def slots(eng, last, ahead, body):
    def one(i, c):
        body(lambda d: valid((i, c + d), last), (i, c))

    for c in range(-ahead, 2):
        one(None, c)
    with eng.Fori(1, last // 2 - 1) as i:
        one(i, 0)
        one(i, 1)
    for c in (last - 2, last - 1, last):
        one(None, c)


def attention(nc, io, dram, keep):
    with ExitStack() as ctx:
        def sb(name, shape, dt=F32):
            return ctx.enter_context(nc.sbuf_tensor(name, shape, dt))

        def sem(name):
            return ctx.enter_context(nc.semaphore(name))

        xs = [sb(f"xs{p}", [R, KT, T]) for p in range(2)]
        Gb = [sb(f"Gb{p}", [R, N]) for p in range(2)]
        ab = [sb(f"ab{p}", [R, AB]) for p in range(2)]
        gate = [sb(f"gate{p}", [R, GT]) for p in range(2)]
        zT = sb("zT", [R, T])
        x1 = [sb(f"x1{p}", [R, KT, T]) for p in range(2)]
        x1k = [sb(f"x1k{p}", [R, KT, T]) for p in range(2)]
        x2s = [sb(f"x2s{p}", [R, KT, T]) for p in range(2)]
        sq = sb("sq", [R, KT, T])
        ms = sb("ms", [R, T])
        ln = sb("ln", [R, T])
        ry = sb("ry", [R, T])
        ru = sb("ru", [R, T])
        rv = sb("rv", [R, T])
        rs = sb("rs", [R, T])
        h = sb("h", [R, KT, T])
        hh = sb("hh", [R, KT, T], F16)
        hl = sb("hl", [R, KT, T], F16)
        bq = sb("bq", [128, QKV])
        qk = sb("qk", [128, 2, 2 * N])
        qks = sb("qks", [128, 2, 2 * N])
        hss = sb("hss", [128, 2 * 32])
        hm = sb("hm", [128, 2 * 32])
        hr2 = sb("hr2", [128, 2 * 32])
        hln = sb("hln", [128, 2 * 32])
        hy = sb("hy", [128, 2 * 32])
        hu = sb("hu", [128, 2 * 32])
        hv = sb("hv", [128, 2 * 32])
        hr = sb("hr", [128, 2 * 32])
        gv = sb("gv", [128, 2, 2, H])
        gk = sb("gk", [128, 4])
        stk = sb("stk", [128, 2, 2 * H, 64], F16)
        va = [sb(f"va{p}", [128, 2, H, 32]) for p in range(2)]
        qT = sb("qT", [128, HP, T], F16)
        kT = sb("kT", [128, HP, T], F16)
        pt = [sb(f"pt{j}", [128, 2, 2, T]) for j in range(4)]
        OT = [sb(f"OT{p}", [128, 4, T]) for p in range(2)]
        sums = sb("sums", [128, 32])
        rsums = sb("rsums", [128, 32])
        recs = sb("recs", [128, 4, T])
        OT2 = sb("OT2", [128, 4, T])
        oh = sb("oh", [128, 4, T], F16)
        ol = sb("ol", [128, 4, T], F16)
        id16 = sb("id16", [128, 128], F16)
        pick = sb("pick", [128, 128])
        wqh = keep["wqh"][:].rearrange("p (k n) -> p k n", k=KT)
        wql = keep["wql"][:].rearrange("p (k n) -> p k n", k=KT)
        wph = keep["wph"][:].rearrange("p (g n) -> p g n", g=4)
        wpl = keep["wpl"][:].rearrange("p (g n) -> p g n", g=4)

        SP = [ctx.enter_context(nc.psum_tensor(f"scores{j}", [128, 2, 512], F32)) for j in range(2)]
        OP = ctx.enter_context(nc.psum_tensor("heads_out", [128, 512], F32))
        RB = [ctx.enter_context(nc.psum_tensor(f"ring{j}", [128, 512], F32)) for j in range(3)]
        ORDER = ["q0", "q1", "q2", "q3", "sb0", "sb1", "z", "d0", "d1", "d2", "pj0", "pj1", "pj2",
                 "ss", "t0", "t1", "t2", "t3"]
        rb = {u: RB[k % 3] for k, u in enumerate(ORDER)}

        x_in = [sem("x_in0"), sem("x_in1")]
        gate_in = [sem("gate_in0"), sem("gate_in1")]
        keep_in = [sem("keep_in0"), sem("keep_in1")]
        x2_out = [sem("x2_out0"), sem("x2_out1")]
        setup_in = sem("setup_in")
        setup_pool = sem("setup_pool")
        setup_dve = sem("setup_dve")
        names_pe = ("z_mm", "d_mm", "ss_mm", "qkv_mm", "tr_mm", "s_mm", "av_mm", "sb_mm", "pj_mm")
        (z_mm, d_mm, ss_mm, qkv_mm, tr_mm, s_mm, av_mm, sb_mm, pj_mm) = [sem(n) for n in names_pe]
        names_act = ("z_sb", "sq_sb", "ln_sb", "ry_sb", "hh_sb", "p_sb", "ot_sb", "oh_sb", "qks_sb", "hln_sb", "hy_sb", "qh_sb")
        (z_sb, sq_sb, ln_sb, ry_sb, hh_sb, p_sb, ot_sb, oh_sb, qks_sb, hln_sb, hy_sb, qh_sb) = [sem(n) for n in names_act]
        names_dve = ("rec_sb", "x1_sb", "ms_sb", "newton", "rs_sb", "h_sb", "ol_sb", "hl_sb", "x2_sb", "qkv_sb",
                     "hss_sb", "hm_sb", "hnewton", "hr_sb", "qkn_sb", "tr_sb")
        (rec_sb, x1_sb, ms_sb, newton, rs_sb, h_sb, ol_sb, hl_sb, x2_sb, qkv_sb,
         hss_sb, hm_sb, hnewton, hr_sb, qkn_sb, tr_sb) = [sem(n + "_a") for n in names_dve]
        om_sb = sem("om_sb")
        sums_in = sem("sums_in")
        recs_in = sem("recs_in")
        READER = {"z": (z_sb, 1, 2), "sb": (om_sb, 2, -1), "d": (x1_sb, 3, 2), "ss": (ms_sb, 1, 2),
                  "pj": (x2_sb, 3, -1), "q": (qkv_sb, 4, 1), "t": (tr_sb, 4, 1)}
        t_sb, stk_sb = sem("t_sb"), sem("stk_sb")

        block = ctx.enter_context(nc.Block())

        @block.sync
        def _(sp):
            sp.dma_start(bq[:], io["bq"].broadcast_to([128, QKV])).then_inc(setup_in, 16)
            sp.dma_start(gk[:, 0:1], io["qg"].broadcast_to([128, 1])).then_inc(setup_in, 16)
            sp.dma_start(gk[:, 1:2], io["kg"].broadcast_to([128, 1])).then_inc(setup_in, 16)

            def load(m):
                p, n = m[1] % 2, number(m)
                wait(sp, x1_sb, at(m, 3, -3))
                wait(sp, h_sb, at(m, 3, -3))
                s = bass.ds(n, 1)
                sp.dma_start(xs[p][:], io["x"][s].rearrange("o r k t -> (o r) k t")).then_inc(x_in[p], 16)
                sp.dma_start(Gb[p][0:D], dram["G"][s].rearrange("o d n -> (o d) n")).then_inc(x_in[p], 16)
                sp.dma_start(ab[p][:], dram["ab"][0][s].rearrange("o r c -> (o r) c")).then_inc(x_in[p], 16)

            load((None, 0))
            load((None, 1))
            for p in range(2):
                sp.sem_inc(x2_out[p], 16)

            def body(batch, _centre):
                mid, back, f2 = batch(0), batch(-1), batch(2)
                if f2 is not None and not (f2[0] is None and f2[1] < 2):
                    load(f2)
                if back is not None:
                    sp.wait_ge(ot_sb, at(back, 4, 4))
                    for j in range(4):
                        r = 32 * j + HD
                        sp.dma_start(sums[32 * j:32 * j + 32], OT[back[1] % 2][r:r + 1].rearrange("o g t -> o (g t)")
                                     .rearrange("o (r c) -> o r c", r=32)).then_inc(sums_in, 16)
                    sp.wait_ge(rec_sb, at(back, 1, 1))
                    for j in range(4):
                        r = 32 * j + HD
                        sp.dma_start(recs[r:r + 1].rearrange("o g t -> o (g t)").rearrange("o (r c) -> o r c", r=32),
                                     rsums[32 * j:32 * j + 32]).then_inc(recs_in, 16)
                if mid is not None:
                    p, s = mid[1] % 2, bass.ds(number(mid), 1)
                    wait(sp, x2_sb, at(mid, 3, -3))
                    sp.wait_ge(x1_sb, at(mid, 3, 3))
                    sp.dma_start(x1k[p][:], x1[p][:]).then_inc(keep_in[p], 16)
                    sp.dma_start(gate[p][:], dram["gate"][0][s].rearrange("o r c -> (o r) c")).then_inc(gate_in[p], 16)
                if back is not None:
                    p, s = back[1] % 2, bass.ds(number(back), 1)
                    sp.wait_ge(x2_sb, at(back, 3, 3))
                    sp.dma_start(dram["x2"][s].rearrange("o r k t -> (o r) k t"), x2s[p][:]).then_inc(x2_out[p], 16)

            slots(sp, B, 2, body)
            for p in range(2):
                sp.wait_ge(x2_out[p], 16 * NP + 16)

        @block.gpsimd
        def _(pool):
            sc = Count(setup_pool)

            def link(ins):
                pool.wait_ge(setup_pool, sc.inc(ins))

            nc.gpsimd.memset(Gb[0][D:R], 0.0)
            link(nc.gpsimd.memset(Gb[1][D:R], 0.0))
            nc.gpsimd.memset(id16[:], 0.0)
            nc.gpsimd.memset(pick[:], 0.0)
            nc.gpsimd.memset(stk[:], 0.0)
            nc.gpsimd.memset(va[0][:], 0.0)
            nc.gpsimd.memset(recs[:], 0.0)
            link(nc.gpsimd.memset(va[1][:], 0.0))

            def body(batch, _centre):
                nx, f2 = batch(1), batch(2)
                if nx is not None:
                    for t in range(2):
                        pool.wait_ge(qh_sb, at(nx, 2, t + 1))
                        v = qk[:, t].rearrange("p (h d) -> p h d", d=HD)
                        nc.gpsimd.tensor_tensor(stk[:, t, 0:H, HD:2 * HD], v[:, 0:H], stk[:, t, 0:H, 0:HD], ALU.subtract)
                        nc.gpsimd.tensor_tensor(stk[:, t, H:2 * H, 2 * HD:3 * HD], v[:, H:2 * H], stk[:, t, H:2 * H, 0:HD],
                                                ALU.subtract)
                        nc.gpsimd.tensor_copy(stk[:, t, 0:H, 2 * HD:3 * HD], stk[:, t, 0:H, 0:HD])
                        nc.gpsimd.tensor_copy(stk[:, t, H:2 * H, HD:2 * HD], stk[:, t, H:2 * H, 0:HD]).then_inc(stk_sb, 1)
                if f2 is not None:
                    if nx is not None:
                        pool.wait_ge(stk_sb, at(nx, 2, 2))
                    pool.wait_ge(rs_sb, at(f2, 1, 1))
                    nc.gpsimd.tensor_tensor(h[:], x1[f2[1] % 2][:], rs[:, None, :].broadcast_to([R, KT, T]), ALU.mult).then_inc(t_sb, 1)

            nc.gpsimd.affine_select(out=id16[:], in_=id16[:], compare_op=ALU.not_equal, fill=1.0, base=0,
                                    pattern=[[-1, 128]], channel_multiplier=1)
            nc.gpsimd.affine_select(out=pick[:].rearrange("p (j r) -> p j r", j=4), in_=pick[:].rearrange("p (j r) -> p j r", j=4),
                                    compare_op=ALU.not_equal, fill=1.0, base=-HD, pattern=[[-32, 4], [0, 32]],
                                    channel_multiplier=1)
            nc.gpsimd.memset(va[0][:, :, :, HD:HD + 1], 1.0)
            nc.gpsimd.memset(va[1][:, :, :, HD:HD + 1], 1.0)
            nc.gpsimd.memset(stk[:, :, 0:H, 3 * HD:3 * HD + 2], 1.0)
            pool.wait_ge(setup_dve, 3)
            nc.gpsimd.tensor_copy(stk[:, 0, H:2 * H, 3 * HD], gk[:, 2:3].broadcast_to([128, H]))
            link(nc.gpsimd.tensor_copy(stk[:, 1, H:2 * H, 3 * HD], gk[:, 2:3].broadcast_to([128, H])))
            for t in range(2):
                ins = nc.gpsimd.tensor_tensor(stk[:, t, H:2 * H, 3 * HD + 1], gk[:, 2:3].broadcast_to([128, H]),
                                              stk[:, t, H:2 * H, 3 * HD], ALU.subtract)
            link(ins)
            slots(pool, B, 2, body)

        @block.scalar
        def _(act):
            def ex(mid, hp):
                act.wait_ge(s_mm, at(mid, 8, hp + 1))
                wait(act, av_mm, at(mid, 8, hp - 3))
                nc.scalar.activation(pt[hp % 4][:].rearrange("p e k t -> p (e k t)"), SP[hp % 2][:].rearrange("p e n -> p (e n)"),
                                     ACT.Exp).then_inc(p_sb, 1)

            def heads_out(mid, g):
                act.wait_ge(av_mm, at(mid, 8, 2 * g + 2))
                wait(act, om_sb, at(mid, 2, -2))
                nc.scalar.activation(OT[mid[1] % 2][:, g], OP[:, 0:T], ACT.Copy).then_inc(ot_sb, 1)

            def squares(nx, t):
                act.wait_ge(qkv_sb, at(nx, 4, 2 * t + 2))
                nc.scalar.activation(qks[:, t], qk[:, t], ACT.Square).then_inc(qks_sb, 1)

            def body(batch, _centre):
                mid, nx, f2, back = batch(0), batch(1), batch(2), batch(-1)
                if mid is not None:
                    ex(mid, 0)
                    ex(mid, 1)
                    ex(mid, 2)
                if nx is not None:
                    squares(nx, 0)
                if mid is not None:
                    heads_out(mid, 0)
                if nx is not None:
                    squares(nx, 1)
                if mid is not None:
                    ex(mid, 3)
                if nx is not None:
                    act.wait_ge(hm_sb, at(nx, 1, 1))
                    nc.scalar.activation(hln[:], hm[:], ACT.Ln, scale=RS * RS).then_inc(hln_sb, 1)
                    act.wait_ge(hln_sb, at(nx, 1, 1))
                    nc.scalar.activation(hy[:], hln[:], ACT.Exp, scale=-0.5).then_inc(hy_sb, 1)
                if f2 is not None:
                    act.wait_ge(z_mm, at(f2, 1, 1))
                    nc.scalar.activation(zT[:], rb["z"][0:R, 0:T], ACT.Copy).then_inc(z_sb, 1)
                if back is not None:
                    act.wait_ge(om_sb, at(back, 2, 2))
                    nc.scalar.activation(oh[:], OT2[:], ACT.Copy).then_inc(oh_sb, 1)
                if mid is not None:
                    ex(mid, 4)
                if f2 is not None:
                    act.wait_ge(x1_sb, at(f2, 3, 3))
                    nc.scalar.activation(sq[:], x1[f2[1] % 2][:], ACT.Square).then_inc(sq_sb, 1)
                if nx is not None:
                    for t in range(2):
                        act.wait_ge(qkn_sb, at(nx, 2, t + 1))
                        nc.scalar.activation(stk[:, t, :, 0:HD], qk[:, t].rearrange("p (h d) -> p h d", d=HD),
                                             ACT.Copy).then_inc(qh_sb, 1)
                if mid is not None:
                    ex(mid, 5)
                    heads_out(mid, 1)
                if f2 is not None:
                    act.wait_ge(ms_sb, at(f2, 1, 1))
                    nc.scalar.activation(ln[:], ms[:], ACT.Ln, scale=RS * RS).then_inc(ln_sb, 1)
                    act.wait_ge(ln_sb, at(f2, 1, 1))
                    nc.scalar.activation(ry[:], ln[:], ACT.Exp, scale=-0.5).then_inc(ry_sb, 1)
                if mid is not None:
                    ex(mid, 6)
                    ex(mid, 7)
                    heads_out(mid, 2)
                    heads_out(mid, 3)
                if f2 is not None:
                    act.wait_ge(h_sb, at(f2, 3, 3))
                    nc.scalar.activation(hh[:], h[:], ACT.Copy).then_inc(hh_sb, 1)

            nc.scalar.preload_act_table_set("natural_log_exp_and_others")
            act.wait_ge(setup_pool, 4)
            slots(act, B, 2, body)

        @block.vector
        def _(dve):
            dve.wait_ge(setup_in, 48)
            nc.vector.tensor_scalar(gv[:, :, 0, :], gk[:, None, 0:1].broadcast_to([128, 2, H]), RS, None, ALU.mult)
            nc.vector.tensor_scalar(gv[:, :, 1, :], gk[:, None, 1:2].broadcast_to([128, 2, H]), RS * HEAD_NORM, None, ALU.mult)
            nc.vector.tensor_tensor(gk[:, 2:3], gk[:, 0:1], gk[:, 1:2], ALU.mult).then_inc(setup_dve, 1)
            dve.wait_ge(setup_dve, 1)
            nc.vector.tensor_scalar(gk[:, 3:4], gk[:, 2:3], -1.0, None, ALU.mult).then_inc(setup_dve, 1)
            dve.wait_ge(setup_dve, 2)
            nc.vector.tensor_scalar(gk[:, 2:3], gk[:, 3:4], gk[:, 2:3], -HEAD_NORM, ALU.max, ALU.mult).then_inc(setup_dve, 1)
            dve.wait_ge(setup_pool, 4)

            def qkv_out(nx, t):
                dve.wait_ge(qkv_mm, at(nx, 4, 2 * t + 1))
                a = rb[f"q{2 * t}"][:, 0:432]
                nc.vector.scalar_tensor_tensor(qk[:, t, 0:432], a, 1.0 / WS, bq[:, 0:432], ALU.mult, ALU.add).then_inc(qkv_sb, 1)
                dve.wait_ge(qkv_mm, at(nx, 4, 2 * t + 2))
                a = rb[f"q{2 * t + 1}"]
                nc.vector.scalar_tensor_tensor(qk[:, t, 432:576], a[:, 0:144], 1.0 / WS, bq[:, 432:576], ALU.mult, ALU.add)
                nc.vector.scalar_tensor_tensor(va[nx[1] % 2][:, t, :, 0:HD], a[:, 144:432].rearrange("p (h d) -> p h d", d=HD), 1.0 / WS,
                                               bq[:, 576:864].rearrange("p (h d) -> p h d", d=HD), ALU.mult, ALU.add).then_inc(qkv_sb, 1)

            def head_squares(nx, t):
                dve.wait_ge(qks_sb, at(nx, 2, t + 1))
                nc.vector.tensor_reduce(hss[:, 32 * t:32 * t + 32], qks[:, t].rearrange("p (h d) -> p h d", d=HD), AX.X, ALU.add).then_inc(hss_sb, 1)

            def body(batch, _centre):
                nx, f2, back = batch(1), batch(2), batch(-1)
                if back is not None:
                    dve.wait_ge(sums_in, at(back, 64, 64))
                    nc.vector.reciprocal(rsums[:], sums[:]).then_inc(rec_sb, 1)
                if nx is not None:
                    qkv_out(nx, 0)
                    head_squares(nx, 0)
                    qkv_out(nx, 1)
                    head_squares(nx, 1)
                    dve.wait_ge(hss_sb, at(nx, 2, 2))
                    nc.vector.tensor_scalar(hm[:], hss[:], GUARD, None, ALU.max).then_inc(hm_sb, 1)
                if back is not None:
                    for u in range(2):
                        dve.wait_ge(sb_mm, at(back, 2, u + 1))
                        nc.vector.tensor_tensor(OT2[:, 2 * u:2 * u + 2], rb[f"sb{u}"][:].rearrange("p (g t) -> p g t", g=2),
                                                OT[back[1] % 2][:, 2 * u:2 * u + 2], ALU.mult).then_inc(om_sb, 1)
                if nx is not None:
                    dve.wait_ge(hy_sb, at(nx, 1, 1))
                    dve.wait_ge(hm_sb, at(nx, 1, 1))
                    nc.vector.scalar_tensor_tensor(hu[:], hm[:], -0.5 * RS * RS, hy[:], ALU.mult, ALU.mult).then_inc(hnewton, 1)
                    dve.wait_ge(hnewton, at(nx, 3, 1))
                    nc.vector.tensor_tensor(hv[:], hu[:], hy[:], ALU.mult).then_inc(hnewton, 1)
                    dve.wait_ge(hnewton, at(nx, 3, 2))
                    nc.vector.scalar_tensor_tensor(hr[:], hv[:], 1.5, hy[:], ALU.add, ALU.mult).then_inc(hnewton, 1)
                    dve.wait_ge(hnewton, at(nx, 3, 3))
                    nc.vector.tensor_tensor(hr2[:], hr[:], gv[:].rearrange("p t a h -> p (t a h)"), ALU.mult).then_inc(hr_sb, 1)
                    dve.wait_ge(hr_sb, at(nx, 1, 1))
                    for t in range(2):
                        v = qk[:, t].rearrange("p (h d) -> p h d", d=HD)
                        nc.vector.tensor_tensor(v, v, hr2[:, 32 * t:32 * t + 32, None].broadcast_to([128, 32, HD]), ALU.mult).then_inc(qkn_sb, 1)
                if back is not None:
                    dve.wait_ge(oh_sb, at(back, 1, 1))
                    nc.vector.tensor_tensor(ol[:], OT2[:], oh[:], ALU.subtract).then_inc(ol_sb, 1)
                if f2 is not None:
                    p = f2[1] % 2
                    dve.wait_ge(x_in[p], uses(f2, 48, 48))
                    wait(dve, keep_in[p], uses(f2, 16, 0))
                    for k in range(KT):
                        dve.wait_ge(d_mm, at(f2, 3, k + 1))
                        nc.vector.tensor_tensor(x1[p][:, k], rb[f"d{k}"][0:R, 0:T], xs[p][:, k], ALU.add).then_inc(x1_sb, 1)
                if back is not None:
                    q = back[1] % 2
                    dve.wait_ge(gate_in[q], uses(back, 16, 16))
                    dve.wait_ge(keep_in[q], uses(back, 16, 16))
                    dve.wait_ge(x2_out[q], uses(back, 16, 16))
                    for k in range(KT):
                        dve.wait_ge(pj_mm, at(back, 3, k + 1))
                        nc.vector.scalar_tensor_tensor(x2s[q][:, k], rb[f"pj{k}"][0:R, 0:T], gate[q][:, k:k + 1], x1k[q][:, k],
                                                       ALU.mult, ALU.add).then_inc(x2_sb, 1)
                if f2 is not None:
                    dve.wait_ge(ss_mm, at(f2, 1, 1))
                    nc.vector.tensor_scalar(ms[:], rb["ss"][0:R, 0:T], GUARD, None, ALU.max).then_inc(ms_sb, 1)
                    dve.wait_ge(ry_sb, at(f2, 1, 1))
                    dve.wait_ge(ms_sb, at(f2, 1, 1))
                    nc.vector.scalar_tensor_tensor(ru[:], ms[:], -0.5 * RS * RS, ry[:], ALU.mult, ALU.mult).then_inc(newton, 1)
                    dve.wait_ge(newton, at(f2, 2, 1))
                    nc.vector.tensor_tensor(rv[:], ru[:], ry[:], ALU.mult).then_inc(newton, 1)
                    dve.wait_ge(newton, at(f2, 2, 2))
                    nc.vector.scalar_tensor_tensor(rs[:], rv[:], 1.5, ry[:], ALU.add, ALU.mult).then_inc(rs_sb, 1)
                if nx is not None:
                    for u in range(4):
                        dve.wait_ge(tr_mm, at(nx, 4, u + 1))
                        dst = (qT, kT)[u // 2]
                        nc.vector.tensor_copy(dst[:, 4 * (u % 2):4 * (u % 2) + 4].rearrange("p a t -> p (a t)"),
                                              rb[f"t{u}"][:].bitcast(F16)).then_inc(tr_sb, 1)
                if f2 is not None:
                    dve.wait_ge(t_sb, at(f2, 1, 1))
                    for k in range(KT):
                        nc.vector.tensor_scalar(h[:, k], h[:, k], ab[p][:, k:k + 1], ab[p][:, KT + k:KT + k + 1],
                                                ALU.mult, ALU.add).then_inc(h_sb, 1)
                    dve.wait_ge(hh_sb, at(f2, 1, 1))
                    nc.vector.tensor_tensor(hl[:], h[:], hh[:], ALU.subtract).then_inc(hl_sb, 1)

            slots(dve, B, 2, body)

        @block.tensor
        def _(pe):
            pe.wait_ge(setup_pool, 4)

            def take(use, centre):
                k, (i, c) = ORDER.index(use), centre
                while True:
                    k -= 3
                    if k < 0:
                        k, c = k + len(ORDER), c - 1
                    if i is None and c < -2:
                        return rb[use]
                    kind = ORDER[k].rstrip("0123456789")
                    reader, per, place = READER[kind]
                    m = valid((i, c + place), B)
                    if m is not None:
                        pe.wait_ge(reader, at(m, per, int(ORDER[k][len(kind):] or 0) + 1))
                        return rb[use]

            def scores(mid, hp):
                if hp == 0:
                    pe.wait_ge(tr_sb, at(mid, 4, 4))
                wait(pe, p_sb, at(mid, 8, hp - 1))
                for kt in range(2):
                    for e in range(2):
                        r = slice(64 * e, 64 * e + 64)
                        mm = nc.tensor.matmul(SP[hp % 2][:, e, kt * T:kt * T + T], kT[r, hp, kt * 128:kt * 128 + 128],
                                              qT[r, hp, :], start=True, stop=True)
                mm.then_inc(s_mm, 1)

            def values(mid, hp):
                pe.wait_ge(p_sb, at(mid, 8, hp + 1))
                if hp % 2 == 0:
                    wait(pe, ot_sb, at(mid, 4, hp // 2))
                for kt in range(2):
                    for e in range(2):
                        hd = 2 * hp + e
                        j = 32 * (hd % 4)
                        mm = nc.tensor.matmul(OP[j:j + 32, 0:T], va[mid[1] % 2][:, kt, hd, :], pt[hp % 4][:, e, kt, :],
                                              start=(kt == 0), stop=(kt == 1), skip_group_check=True)
                mm.then_inc(av_mm, 1)

            def body(batch, centre):
                mid, nx, f2, back = batch(0), batch(1), batch(2), batch(-1)

                def heads(v, s):
                    if mid is not None:
                        if v is not None:
                            values(mid, v)
                        if s is not None:
                            scores(mid, s)

                heads(None, 0)
                heads(None, 1)
                heads(0, 2)
                if nx is not None:
                    pe.wait_ge(hl_sb, at(nx, 1, 1))
                    for t in range(2):
                        for half in range(2):
                            o = take(f"q{2 * t + half}", centre)
                            c = slice(432 * half, 432 * half + 432)
                            terms = [(x, w, k) for k in range(KT) for x, w in ((hh, wqh), (hh, wql), (hl, wqh))]
                            for n, (x, w, k) in enumerate(terms):
                                mm = nc.tensor.matmul(o[:, 0:432], x[:, k, 128 * t:128 * t + 128], w[:, k, c],
                                                      start=(n == 0), stop=(n == 8))
                            mm.then_inc(qkv_mm, 1)
                heads(1, 3)
                if back is not None:
                    pe.wait_ge(recs_in, at(back, 64, 64))
                    for u in range(2):
                        o = take(f"sb{u}", centre)
                        nc.tensor.matmul(o[:], pick[:], recs[:, 2 * u:2 * u + 2].rearrange("p g t -> p (g t)"),
                                         start=True, stop=True).then_inc(sb_mm, 1)
                if f2 is not None:
                    p = f2[1] % 2
                    pe.wait_ge(x_in[p], uses(f2, 48, 48))
                    o = take("z", centre)
                    for k in range(KT):
                        mm = nc.tensor.matmul(o[0:R, 0:T], keep["U"][:, k], xs[p][:, k], start=(k == 0), stop=(k == 2))
                    mm.then_inc(z_mm, 1)
                heads(2, 4)
                if f2 is not None:
                    pe.wait_ge(z_sb, at(f2, 1, 1))
                    for m in range(KT):
                        o = take(f"d{m}", centre)
                        nc.tensor.matmul(o[0:R, 0:T], Gb[p][:, m * R:m * R + R], zT[:], start=True, stop=True).then_inc(d_mm, 1)
                if back is not None:
                    pe.wait_ge(ol_sb, at(back, 1, 1))
                    for m in range(KT):
                        o = take(f"pj{m}", centre)
                        c = slice(m * R, m * R + R)
                        terms = [(w, x, g) for g in range(4) for w, x in ((wph, oh), (wph, ol), (wpl, oh))]
                        for n, (w, x, g) in enumerate(terms):
                            mm = nc.tensor.matmul(o[0:R, 0:T], w[:, g, c], x[:, g], start=(n == 0), stop=(n == 11))
                        mm.then_inc(pj_mm, 1)
                heads(3, 5)
                if f2 is not None:
                    pe.wait_ge(sq_sb, at(f2, 1, 1))
                    o = take("ss", centre)
                    for k in range(KT):
                        mm = nc.tensor.matmul(o[0:R, 0:T], keep["ones"][:], sq[:, k], start=(k == 0), stop=(k == 2))
                    mm.then_inc(ss_mm, 1)
                heads(4, 6)
                heads(5, 7)
                if nx is not None:
                    pe.wait_ge(stk_sb, at(nx, 2, 2))
                    for u in range(4):
                        o = take(f"t{u}", centre)[:].bitcast(F16)
                        for n in range(4):
                            hd = H * (u // 2) + 8 * (u % 2) + 2 * n
                            for t in range(2):
                                mm = nc.tensor.transpose(o[:, n * T + 128 * t:n * T + 128 * t + 128],
                                                         stk[:, t, hd:hd + 2, :].rearrange("p h d -> p (h d)"), id16[:])
                        mm.then_inc(tr_mm, 1)
                heads(6, None)
                heads(7, None)

            slots(pe, B, 2, body)


def mlp(nc, io, dram, keep, out):
    W = 2 * T
    with ExitStack() as ctx:
        def sb(name, shape, dt=F32):
            return ctx.enter_context(nc.sbuf_tensor(name, shape, dt))

        def sem(name):
            return ctx.enter_context(nc.semaphore(name))

        xp = [sb(f"xp{p}", [R, KT, 2, T]) for p in range(2)]
        mb = [sb(f"mb{p}", [R, 2, AB]) for p in range(2)]
        gt = [sb(f"gt{p}", [R, 2, 2 * GT]) for p in range(2)]
        sq = sb("sqm", [R, KT, W])
        ms = sb("msm", [R, W])
        ln = sb("lnm", [R, W])
        ry = sb("rym", [R, W])
        ru = sb("rum", [R, W])
        rv = sb("rvm", [R, W])
        rs = sb("rsm", [R, W])
        h = sb("hm2", [R, KT, 2, T])
        hh = [sb(f"hh{p}", [R, KT, W], F16) for p in range(2)]
        hl = [sb(f"hl{p}", [R, KT, W], F16) for p in range(2)]
        b1 = sb("b1s", [128, MT])
        g = [sb(f"g{j}", [128, W]) for j in range(3)]
        gh = sb("gh", [128, MT, W], F16)
        gl = sb("gl", [128, MT, W], F16)
        yt = sb("yt", [R, KT, 2, T])
        ys = [sb(f"ys{p}", [R, KT, 2, T]) for p in range(2)]
        w1h = keep["w1h"][:].rearrange("p (k n) -> p k n", k=KT)
        w1l = keep["w1l"][:].rearrange("p (k n) -> p k n", k=KT)
        w2h = keep["w2h"][:].rearrange("p (j n) -> p j n", j=MT)
        w2l = keep["w2l"][:].rearrange("p (j n) -> p j n", j=MT)
        SS = ctx.enter_context(nc.psum_tensor("squares", [128, 512], F32))
        H1 = [ctx.enter_context(nc.psum_tensor(f"hidden{j}", [128, 512], F32)) for j in range(3)]
        Y = [ctx.enter_context(nc.psum_tensor(f"down{j}", [128, 512], F32)) for j in range(KT)]

        x_in = [sem("xp_in0"), sem("xp_in1")]
        b1_in = sem("b1_in")
        y_out = [sem("y_out0"), sem("y_out1")]
        ss_mm, fc1_mm, fc2_mm, down_mm = sem("ss_mm2"), sem("fc1_mm"), sem("fc2_mm"), sem("down_mm")
        sq_sb, ln_sb, ry_sb, hh_sb, g_sb, yt_sb = [sem(n + "_m") for n in ("sq_sb", "ln_sb", "ry_sb", "hh_sb", "g_sb", "yt_sb")]
        ms_sb, newton, rs_sb, h_sb, hl_sb, gh_sb, gl_sb = [sem(n + "_m") for n in ("ms_sb", "newton", "rs_sb", "h_sb", "hl_sb", "gh_sb", "gl_sb")]
        t_sb, y_sb = sem("t_sb_m"), sem("y_sb_m")

        block = ctx.enter_context(nc.Block())

        @block.sync
        def _(sp):
            sp.dma_start(b1[:], io["b1"]).then_inc(b1_in, 16)

            def load(m):
                p, s = m[1] % 2, bass.ds(number(m) * 2, 2)
                wait(sp, y_sb, at(m, 1, -1))
                sp.dma_start(xp[p][:], dram["x2"][s].rearrange("b r k t -> r k b t")).then_inc(x_in[p], 16)
                sp.dma_start(mb[p][:], dram["ab"][1][s].rearrange("b r c -> r b c")).then_inc(x_in[p], 16)
                sp.dma_start(gt[p][:, :, 0:GT], dram["gate"][1][s].rearrange("b r c -> r b c")).then_inc(x_in[p], 16)
                sp.dma_start(gt[p][:, :, GT:2 * GT], dram["gb"][s].rearrange("b r c -> r b c")).then_inc(x_in[p], 16)

            def body(batch, _centre):
                fr, mid, back = batch(1), batch(0), batch(-1)
                if fr is not None:
                    load(fr)
                if back is not None:
                    p, s = back[1] % 2, bass.ds(number(back) * 2, 2)
                    sp.wait_ge(y_sb, at(back, 1, 1))
                    sp.dma_start(out[s].rearrange("b r k t -> r k b t"), ys[p][:]).then_inc(y_out[p], 16)

            slots(sp, NP, 1, body)
            for p in range(2):
                sp.wait_ge(y_out[p], 16 * NP // 2)

        @block.gpsimd
        def _(pool):
            def body(batch, _centre):
                fr, mid, back = batch(1), batch(0), batch(-1)
                if fr is not None:
                    pool.wait_ge(rs_sb, at(fr, 1, 1))
                    nc.gpsimd.tensor_tensor(h[:].rearrange("r k b t -> r k (b t)"), xp[fr[1] % 2][:].rearrange("r k b t -> r k (b t)"),
                                            rs[:, None, :].broadcast_to([R, KT, W]), ALU.mult).then_inc(t_sb, 1)
                if mid is not None:
                    p = mid[1] % 2
                    pool.wait_ge(yt_sb, at(mid, 6, 6))
                    wait(pool, y_out[p], uses(mid, 16, 0))
                    nc.gpsimd.tensor_tensor(ys[p][:], yt[:], xp[p][:], ALU.add).then_inc(y_sb, 1)

            slots(pool, NP, 1, body)

        @block.scalar
        def _(act):
            def hidden(mid, j):
                act.wait_ge(fc1_mm, at(mid, MT, j + 1))
                wait(act, gl_sb, at(mid, MT, j - 2))
                nc.scalar.activation(g[j % 3][:], H1[j % 3][:], ACT.Gelu_apprx_tanh, bias=b1[:, j:j + 1],
                                     scale=1.0 / WS).then_inc(g_sb, 1)

            def body(batch, _centre):
                fr, mid, back = batch(1), batch(0), batch(-1)
                if mid is not None:
                    hidden(mid, 0)
                    hidden(mid, 1)
                    hidden(mid, 2)
                if fr is not None:
                    act.wait_ge(x_in[fr[1] % 2], uses(fr, 64, 64))
                    nc.scalar.activation(sq[:].rearrange("r k (b t) -> r k b t", b=2), xp[fr[1] % 2][:], ACT.Square).then_inc(sq_sb, 1)
                if mid is not None:
                    hidden(mid, 3)
                    hidden(mid, 4)
                if fr is not None:
                    act.wait_ge(ms_sb, at(fr, 1, 1))
                    nc.scalar.activation(ln[:], ms[:], ACT.Ln, scale=RS * RS).then_inc(ln_sb, 1)
                    act.wait_ge(ln_sb, at(fr, 1, 1))
                    nc.scalar.activation(ry[:], ln[:], ACT.Exp, scale=-0.5).then_inc(ry_sb, 1)
                if mid is not None:
                    hidden(mid, 5)
                    hidden(mid, 6)
                if fr is not None:
                    act.wait_ge(h_sb, at(fr, 6, 6))
                    nc.scalar.activation(hh[fr[1] % 2][:].rearrange("r k (b t) -> r k b t", b=2), h[:], ACT.Copy).then_inc(hh_sb, 1)
                if mid is not None:
                    hidden(mid, 7)
                    hidden(mid, 8)
                    p = mid[1] % 2
                    act.wait_ge(x_in[p], uses(mid, 64, 64))
                    wait(act, y_sb, at(mid, 1, 0))
                    for k in range(KT):
                        act.wait_ge(down_mm, at(mid, KT, k + 1))
                        for b in range(2):
                            nc.scalar.activation(yt[:, k, b], Y[k][0:R, b * T:b * T + T], ACT.Identity,
                                                 bias=gt[p][:, b, GT + k:GT + k + 1], scale=gt[p][:, b, k:k + 1]).then_inc(yt_sb, 1)

            act.wait_ge(b1_in, 16)
            slots(act, NP, 1, body)

        @block.vector
        def _(dve):
            def halves(mid, j):
                dve.wait_ge(g_sb, at(mid, MT, j + 1))
                nc.vector.tensor_copy(gh[:, j], g[j % 3][:]).then_inc(gh_sb, 1)
                dve.wait_ge(gh_sb, at(mid, MT, j + 1))
                nc.vector.tensor_tensor(gl[:, j], g[j % 3][:], gh[:, j], ALU.subtract).then_inc(gl_sb, 1)

            def body(batch, _centre):
                fr, mid, back = batch(1), batch(0), batch(-1)
                if mid is not None:
                    halves(mid, 0)
                    halves(mid, 1)
                    halves(mid, 2)
                    halves(mid, 3)
                if fr is not None:
                    dve.wait_ge(ss_mm, at(fr, 1, 1))
                    nc.vector.tensor_scalar(ms[:], SS[0:R], GUARD, None, ALU.max).then_inc(ms_sb, 1)
                if mid is not None:
                    halves(mid, 4)
                if fr is not None:
                    p = fr[1] % 2
                    dve.wait_ge(ry_sb, at(fr, 1, 1))
                    dve.wait_ge(ms_sb, at(fr, 1, 1))
                    nc.vector.scalar_tensor_tensor(ru[:], ms[:], -0.5 * RS * RS, ry[:], ALU.mult, ALU.mult).then_inc(newton, 1)
                    dve.wait_ge(newton, at(fr, 2, 1))
                    nc.vector.tensor_tensor(rv[:], ru[:], ry[:], ALU.mult).then_inc(newton, 1)
                    dve.wait_ge(newton, at(fr, 2, 2))
                    nc.vector.scalar_tensor_tensor(rs[:], rv[:], 1.5, ry[:], ALU.add, ALU.mult).then_inc(rs_sb, 1)
                if mid is not None:
                    halves(mid, 5)
                if fr is not None:
                    dve.wait_ge(x_in[p], uses(fr, 64, 64))
                    dve.wait_ge(t_sb, at(fr, 1, 1))
                    for k in range(KT):
                        for b in range(2):
                            nc.vector.tensor_scalar(h[:, k, b], h[:, k, b], mb[p][:, b, k:k + 1], mb[p][:, b, KT + k:KT + k + 1],
                                                    ALU.mult, ALU.add).then_inc(h_sb, 1)
                if mid is not None:
                    halves(mid, 6)
                if fr is not None:
                    dve.wait_ge(hh_sb, at(fr, 1, 1))
                    nc.vector.tensor_tensor(hl[p][:], h[:].rearrange("r k b t -> r k (b t)"), hh[p][:], ALU.subtract).then_inc(hl_sb, 1)
                if mid is not None:
                    halves(mid, 7)
                    halves(mid, 8)

            slots(dve, NP, 1, body)

        @block.tensor
        def _(pe):
            def up(mid, j):
                p = mid[1] % 2
                if j == 0:
                    pe.wait_ge(hl_sb, at(mid, 1, 1))
                wait(pe, g_sb, at(mid, MT, j - 2))
                c = slice(128 * j, 128 * j + 128)
                terms = [(w, x, k) for k in range(KT) for w, x in ((w1h, hh[p]), (w1h, hl[p]), (w1l, hh[p]))]
                for n, (w, x, k) in enumerate(terms):
                    mm = nc.tensor.matmul(H1[j % 3][:], w[:, k, c], x[:, k], start=(n == 0), stop=(n == 8))
                mm.then_inc(fc1_mm, 1)

            def down(mid, j):
                pe.wait_ge(gl_sb, at(mid, MT, j + 1))
                if j == 0:
                    wait(pe, yt_sb, at(mid, 6, 0))
                for k in range(KT):
                    c = slice(k * R, k * R + R)
                    for n, (w, x) in enumerate(((w2h, gh), (w2h, gl), (w2l, gh))):
                        mm = nc.tensor.matmul(Y[k][0:R], w[:, j, c], x[:, j], start=(j == 0 and n == 0), stop=(j == MT - 1 and n == 2))
                    if j == MT - 1:
                        mm.then_inc(down_mm, 1)

            def body(batch, _centre):
                fr, mid, back = batch(1), batch(0), batch(-1)
                if mid is not None:
                    up(mid, 0)
                    up(mid, 1)
                    up(mid, 2)
                    down(mid, 0)
                    up(mid, 3)
                    down(mid, 1)
                if fr is not None:
                    pe.wait_ge(sq_sb, at(fr, 1, 1))
                    wait(pe, ms_sb, at(fr, 1, 0))
                    for k in range(KT):
                        mm = nc.tensor.matmul(SS[0:R], keep["ones"][:], sq[:, k], start=(k == 0), stop=(k == 2))
                    mm.then_inc(ss_mm, 1)
                if mid is not None:
                    for j in range(4, MT):
                        up(mid, j)
                        down(mid, j - 2)
                    down(mid, MT - 2)
                    down(mid, MT - 1)

            slots(pe, NP, 1, body)


def build(nc, io, out):
    dram = {
        "A": nc.dram_tensor("skew_d", (B, D * D), F32, kind="Internal").ap(),
        "G": nc.dram_tensor("G_d", (B, D, N), F32, kind="Internal").ap(),
        "ab": [nc.dram_tensor(f"ab{p}_d", (B, R, AB), F32, kind="Internal").ap() for p in range(2)],
        "gate": [nc.dram_tensor(f"gate{p}_d", (B, R, GT), F32, kind="Internal").ap() for p in range(2)],
        "gb": nc.dram_tensor("gb_d", (B, R, GT), F32, kind="Internal").ap(),
        "x2": nc.dram_tensor("x2_d", (B, R, KT, T), F32, kind="Internal").ap(),
    }
    with ExitStack() as ctx:
        def sb(name, shape, dt=F32):
            return ctx.enter_context(nc.sbuf_tensor(name, shape, dt))

        keep = {"U": sb("U", [R, KT, R]), "ones": sb("ones", [R, R])}
        for name, parts, w in (("wq", R, KT * QKV), ("wp", 128, 4 * N), ("w1", R, KT * HID), ("w2", 128, MT * N)):
            keep[name + "h"] = sb(name + "h", [parts, w], F16)
            keep[name + "l"] = sb(name + "l", [parts, w], F16)
        prepare(nc, io, dram, keep)
        attention(nc, io, dram, keep)
        mlp(nc, io, dram, keep, out)


def kernel(**inputs):
    import numpy as np
    import concourse.bacc as bacc
    from concourse.bass_utils import run_bass_kernel_spmd

    a = {k: np.asarray(v) for k, v in inputs.items()}

    def rows(w):
        return np.ascontiguousarray(w.T.reshape(KT, R, -1).transpose(1, 0, 2))

    def grid(w):
        iu, ju = np.triu_indices(D, k=1)
        at = np.zeros((D, D), np.int64)
        at[iu, ju] = at[ju, iu] = np.arange(len(iu))
        return w[at.reshape(-1)]

    wp = np.zeros((4, 32, 4, N), np.float32)
    heads = a["L1_cond_proj_w"].T.reshape(4, 4, HD, N)
    wp[:, 0:HD] = heads.transpose(1, 2, 0, 3)
    wp[0, HD, 0] = a["L1_cond_proj_b"]
    arrays = {
        "x": np.ascontiguousarray(a["x"].reshape(B, T, KT, R).transpose(0, 3, 2, 1)),
        "condT": rows(a["cond_1152"]),
        "PT": np.ascontiguousarray(np.concatenate([a["L0_cond_P"].T] * 2)),
        "WT": rows(grid(a["L0_cond_W"])),
        "bfull": grid(a["L0_cond_b"])[None],
        "adaT": rows(a["L1_cond_ada_w"]),
        "adab": np.ascontiguousarray(a["L1_cond_ada_b"].reshape(MODS, R).T),
        "wqT": rows(a["L1_cond_qkv_w"]).reshape(R, -1),
        "bq": a["L1_cond_qkv_b"][None],
        "wpT": np.ascontiguousarray(wp.reshape(128, -1)),
        "w1T": rows(a["L1_cond_fc1_w"]).reshape(R, -1),
        "b1": np.ascontiguousarray(a["L1_cond_fc1_b"].reshape(MT, 128).T),
        "w2T": np.ascontiguousarray(a["L1_cond_fc2_w"].T.reshape(MT, 128, N).transpose(1, 0, 2)).reshape(128, -1),
        "b2": np.ascontiguousarray(a["L1_cond_fc2_b"].reshape(KT, R).T),
    }
    for n in ("g1", "g2", "qg", "kg"):
        arrays[n] = a["L1_cond_" + n][None]
    nc = bacc.Bacc("TRN2", target_bir_lowering=False, num_devices=1)
    io = {k: nc.dram_tensor(k + "_in", v.shape, F32, kind="ExternalInput").ap() for k, v in arrays.items()}
    out = nc.dram_tensor("y_out", (B, R, KT, T), F32, kind="ExternalOutput").ap()
    build(nc, io, out)
    r = run_bass_kernel_spmd(nc, [{k + "_in": v for k, v in arrays.items()}], core_ids=[0])
    y = r.results[0]["y_out"]
    return np.ascontiguousarray(y.transpose(0, 3, 2, 1)).reshape(B, T, N)
```

```python
from contextlib import ExitStack

import concourse.bass as bass
from concourse import mybir

F32 = mybir.dt.float32
F16 = mybir.dt.float16
ALU = mybir.AluOpType
ACT = mybir.ActivationFunctionType
AX = mybir.AxisListType

B, T, N, D = 32, 256, 288, 64
R, KT = 128, 3
REST = N - (KT - 1) * R
W = KT * R
CR = N // KT
H, HD = 16, 18
QKV = 3 * N
HID = 4 * N
MT = HID // 128
HP = H // 2
NP = B // 2
WS = 64.0
MODS = 6 * KT
AB, GT = 2 * KT, KT
DOUBLE = 13
RS = 256.0
GUARD = 1e-24
BIG_NORM = float(N) ** 0.5
HEAD_NORM = float(HD) ** 0.5
QR_PER = 4
ROUNDS = D // QR_PER
FIRST_PRODUCT = 3
CH = 4


def wait(eng, sem, value):
    if isinstance(value, int) and value <= 0:
        return
    eng.wait_ge(sem, value)


WIDTHS = {"wq": KT * QKV, "wp": 4 * W, "w1": KT * HID, "w2": MT * W}
WALL = sum(WIDTHS.values())
LOOPED = range(5, ROUNDS - 1)
PIECE = WALL // (len(LOOPED) * QR_PER)


def weights(keep, name):
    at = sum(list(WIDTHS.values())[:list(WIDTHS).index(name)])
    return [keep[half][:, at:at + WIDTHS[name]] for half in ("wh", "wl")]


class Count:

    def __init__(self, sem, base=0):
        self.sem, self.base, self.n = sem, base, 0

    def inc(self, ins):
        ins.then_inc(self.sem, 1)
        self.n += 1
        return self.base + self.n


def prepare(nc, io, dram, keep):
    with ExitStack() as ctx:
        def sb(name, shape, dt=F32):
            return ctx.enter_context(nc.sbuf_tensor(name, shape, dt))

        def sem(name):
            return ctx.enter_context(nc.semaphore(name))

        At = sb("At", [128, N + D])
        prod = sb("prod", [128, N])
        sqv = sb("sqv", [128, N])
        ident = sb("ident", [128, 128])
        identd = sb("identd", [128, D])
        gtm = sb("gtm", [128, D])
        lem = sb("lem", [128, D])
        sel = sb("sel", [128, 2, 128])
        dots = sb("dots", [128, 1])
        ssq = sb("ssq", [128, 1])
        sig = sb("sig", [128, 1])
        hs = sb("hs", [128, 1])
        a2 = sb("a2", [128, 1])
        t4 = sb("t4", [128, 1])
        am = sb("am", [128, 1])
        dm = sb("dm", [128, 1])
        tiny = sb("tiny", [128, 1])
        rsig = sb("rsig", [128, 1])
        sig2 = sb("sig2", [128, 1])
        nwt = sb("nwt", [128, 2])
        rt = sb("rt", [128, 1])
        wv = sb("wv", [128, 1])
        nw = sb("nw", [128, 1])
        stall = sb("stall", [128, 2, D])
        scol = sb("scol", [128, 2])
        junk = sb("junk", [128, D])
        rcol = sb("rcol", [128, 3])
        Vt = sb("Vt", [128, N])
        V = sb("V", [CR, KT, D])
        XY = sb("XY", [D, 2, 2 * D])
        XT = sb("XT", [D, 2, D])
        Yd = sb("Yd", [D, 2, D])
        UT = sb("UT", [128, W])
        cT = sb("cT", [CR, KT, B])
        cE = sb("cE", [CR, KT, B])
        cR = sb("cR", [CR, KT, B])
        sT = sb("sT", [CR, KT, B])
        bfull = sb("bfull", [B, D * D])
        wfull = sb("wfull", [CR, 2, KT, 512])
        vraw = sb("vraw", [B, 2, 512])
        vall = sb("vall", [B, D * D])
        Ald = sb("Ald", [128, 16, D])
        mask = sb("mask", [128, D])
        E = sb("E", [128, 16, 128])
        ET = sb("ET", [128, 16, 128])
        F = sb("F", [128, 16, 128])
        Q = sb("Q", [128, 16, 128])
        two = sb("two", [128, 128])
        half = sb("half", [128, 128])
        adaw = sb("adaw", [CR, KT, 6 * W])
        adab = sb("adab", [R, MODS])
        mod = sb("mod", [R, MODS, B])
        moda = keep["ab"][:].rearrange("r (b f c) -> r b f c", b=B, f=2)
        modg = keep["gate"][:].rearrange("r (b f c) -> r b f c", b=B, f=2)
        modb = keep["gb"][:].rearrange("r (b c) -> r b c", b=B)
        gs = sb("gs", [R, 2])
        b2 = sb("b2", [R, KT])
        ws = sb("ws", [128, 1])
        wraw = sb("wraw", [128, QR_PER, PIECE])
        ps = [ctx.enter_context(nc.psum_tensor(f"prep{i}", [128, 512], F32)) for i in range(8)]
        VA, VB = ps[0], ps[1]
        EP, TP, MP = ps[2:4], ps[4:6], ps[6:8]

        p_in = sem("p_in")
        c_in = sem("c_in")
        bias_in = sem("bias_in")
        wf_in = [sem("wf_in0"), sem("wf_in1")]
        ada_in = sem("ada_in")
        small_in = sem("small_in")
        a_in = sem("a_in")
        raw_in = [sem(f"raw_in{k}") for k in range(QR_PER)]
        masks = sem("masks")
        pool_step = sem("pool_step")
        dve_step = sem("dve_step")
        sel_ready = sem("sel_ready")
        row_bc = sem("row_bc")
        ssq_ready = sem("ssq_ready")
        sig_ready = sem("sig_ready")
        rcol_ready = sem("rcol_ready")
        at_updated = sem("at_updated")
        s_saved = sem("s_saved")
        exp_c = sem("exp_c")
        silu_ready = sem("silu_ready")
        v_mm = sem("v_mm")
        v_raw = sem("v_raw")
        v_ready = sem("v_ready")
        v_out = sem("v_out")
        a_ready = sem("a_ready")
        at_neg = sem("at_neg")
        taylor_sb = sem("taylor_sb")
        q_ready = sem("q_ready")
        prod_mm = sem("prod_mm")
        prod_sb = sem("prod_sb")
        tr_mm = sem("tr_mm")
        tr_sb = sem("tr_sb")
        f_ready = sem("f_ready")
        mod_mm = sem("mod_mm")
        mod_sb = sem("mod_sb")
        gate_t = sem("gate_t")
        mods_done = sem("mods_done")
        vt_ready = sem("vt_ready")
        wy_pe = sem("wy_pe")
        wy_sb = sem("wy_sb")
        g_mm = sem("g_mm")
        g_sb = sem("g_sb")
        w_scaled = sem("w_scaled")
        w_low = sem("w_low")
        w_high = sem("w_high")

        block = ctx.enter_context(nc.Block())
        NV = D * D // 512

        @block.sync
        def _(sp):
            sp.dma_start(At[:, 0:N], io["PT"]).then_inc(p_in, 16)
            sp.dma_start(cT[:], io["condT"]).then_inc(c_in, 16)
            for c in range(2):
                sp.dma_start(wfull[:, c], io["WT"][:, :, c * 512:(c + 1) * 512]).then_inc(wf_in[c], 16)
            sp.dma_start(bfull[:], io["bfull"].broadcast_to([B, D * D])).then_inc(bias_in, 16)
            sp.dma_start(adab[:], io["adab"]).then_inc(small_in, 16)
            sp.dma_start(b2[:], io["b2"]).then_inc(small_in, 16)
            sp.dma_start(gs[:, 0:1], io["g1"].broadcast_to([R, 1])).then_inc(small_in, 16)
            sp.dma_start(gs[:, 1:2], io["g2"].broadcast_to([R, 1])).then_inc(small_in, 16)

            def put_v(c):
                sp.wait_ge(v_ready, c + 1)
                at = slice(c * 512, (c + 1) * 512)
                sp.dma_start(dram["A"][:, at], vall[:, at]).then_inc(v_out, 16)

            for c in range(2, NV):
                sp.wait_ge(v_mm, c - 1)
                sp.dma_start(wfull[:, c % 2], io["WT"][:, :, c * 512:(c + 1) * 512]).then_inc(wf_in[c % 2], 16)
                put_v(c - 2)
            put_v(NV - 2)
            put_v(NV - 1)
            sp.wait_ge(v_out, 16 * NV)
            for p in range(2):
                sp.dma_start(Ald[64 * p:64 * p + 64], dram["A"].rearrange("(q p) (i j) -> p i q j", p=2, i=D)[p]).then_inc(a_in, 16)
            for k in range(QR_PER):
                sp.dma_start(wraw[:, k], io["weights"][:, k * PIECE:(k + 1) * PIECE]).then_inc(raw_in[k], 16)
            with sp.Fori(1, len(LOOPED)) as r:
                for k in range(QR_PER):
                    sp.wait_ge(w_low, r * QR_PER + (k + 1 - QR_PER))
                    sp.dma_start(wraw[:, k], io["weights"][:, bass.ds(r * (QR_PER * PIECE) + k * PIECE, PIECE)]).then_inc(raw_in[k], 16)

        @block.gpsimd
        def _(pool):
            pc = Count(pool_step)

            def link(ins):
                pool.wait_ge(pool_step, pc.inc(ins))

            nc.gpsimd.memset(ws[:], WS)
            for t, w in ((ident, 128), (two, 128), (half, 128), (identd, D)):
                ins = nc.gpsimd.memset(t[:], 0.0)
            for t in (gtm, lem, mask):
                ins = nc.gpsimd.memset(t[:], 0.0)
            link(ins)
            for t, v in ((ident, 1.0), (two, 2.0), (half, 0.5)):
                nc.gpsimd.affine_select(out=t[:], in_=t[:], compare_op=ALU.not_equal, fill=v, base=0,
                                        pattern=[[-1, 128]], channel_multiplier=1)
            for p in range(2):
                h = slice(64 * p, 64 * p + 64)
                sc = 2.0 ** -DOUBLE
                nc.gpsimd.affine_select(out=identd[h], in_=identd[h], compare_op=ALU.not_equal, fill=1.0, base=0,
                                        pattern=[[-1, D]], channel_multiplier=1)
                nc.gpsimd.affine_select(out=gtm[h], in_=gtm[h], compare_op=ALU.is_ge, fill=1.0, base=0,
                                        pattern=[[1, D]], channel_multiplier=-1)
                nc.gpsimd.affine_select(out=lem[h], in_=lem[h], compare_op=ALU.is_gt, fill=1.0, base=0,
                                        pattern=[[-1, D]], channel_multiplier=1)
                ins = nc.gpsimd.affine_select(out=mask[h], in_=mask[h], compare_op=ALU.is_ge, fill=sc, base=0,
                                              pattern=[[-1, D]], channel_multiplier=1)
                link(ins)
                ins = nc.gpsimd.affine_select(out=mask[h], in_=mask[h], compare_op=ALU.is_ge, fill=-sc, base=0,
                                        pattern=[[1, D]], channel_multiplier=-1)
            link(ins)
            nc.gpsimd.memset(E[:], 0.0).then_inc(masks, 1)

            def sel_step(j, s):
                if not (isinstance(j, int) and j < 2):
                    pool.wait_ge(row_bc, 2 * j - 2)
                nc.gpsimd.tensor_copy(sel[:, s % 2], ident[:, bass.ds(j, 1)].broadcast_to([128, 128])).then_inc(sel_ready, 1)

            sel_step(0, 0)

            def split(r, k):
                n = r * QR_PER + (k - LOOPED[0] * QR_PER)
                c = bass.ds(n * PIECE, PIECE)
                pool.wait_ge(w_high, n + 1)
                nc.gpsimd.tensor_tensor(wraw[:, k], wraw[:, k], ws[:].broadcast_to([128, PIECE]), ALU.mult).then_inc(w_scaled, 1)
                pool.wait_ge(w_scaled, n + 1)
                nc.gpsimd.tensor_tensor(keep["wl"][:, c], wraw[:, k], keep["wh"][:, c], ALU.subtract).then_inc(w_low, 1)

            def v_chunk(c):
                pool.wait_ge(v_raw, c + 1)
                if c == 0:
                    pool.wait_ge(bias_in, 16)
                nc.gpsimd.tensor_tensor(vall[:, c * 512:(c + 1) * 512], vraw[:, c % 2], bfull[:, c * 512:(c + 1) * 512],
                                        ALU.add).then_inc(v_ready, 1)

            def skew(p):
                pool.wait_ge(a_in, 32)
                pool.wait_ge(sel_ready, 2 * QR_PER + 4 + p)
                h = slice(64 * p, 64 * p + 64)
                nc.gpsimd.tensor_tensor(E[h, :, h], Ald[h], mask[h, None, :].broadcast_to([64, 16, D]), ALU.mult).then_inc(a_ready, 1)
                pool.wait_ge(a_ready, p + 1)

            def taylor(c):
                q = slice(CH * c, CH * c + CH)
                pool.wait_ge(taylor_sb, 2 + c)
                link(nc.gpsimd.tensor_tensor(Q[:, q], Q[:, q], E[:, q], ALU.add))
                nc.gpsimd.tensor_tensor(Q[:, q], Q[:, q], half[:, None, :].broadcast_to([128, CH, 128]), ALU.add).then_inc(q_ready, 1)

            def plus_two(c, k):
                q = slice(CH * c, CH * c + CH)
                pool.wait_ge(prod_sb, k + 1)
                nc.gpsimd.tensor_tensor(F[:, q], E[:, q], two[:, None, :].broadcast_to([128, CH, 128]),
                                        ALU.add).then_inc(f_ready, 1)

            def round_(r):
                for s in range(QR_PER):
                    j = QR_PER * r + s
                    if isinstance(r, int):
                        if j + 1 < D:
                            sel_step(j + 1, s + 1)
                        if r < 2:
                            v_chunk(j)
                        if r == 2 and s >= 2:
                            skew(s - 2)
                        if r == FIRST_PRODUCT:
                            taylor(s)
                        if r > FIRST_PRODUCT:
                            plus_two(s, (r - FIRST_PRODUCT) * CH + s)
                    else:
                        sel_step(r * QR_PER + s + 1, s + 1)
                        plus_two(s, r * CH + (s - FIRST_PRODUCT * CH))
                        split(r, s)

            for r in range(FIRST_PRODUCT + 2):
                round_(r)
            with pool.Fori(LOOPED[0], LOOPED[-1] + 1) as r:
                round_(r)
            round_(ROUNDS - 1)
            for c in range(CH):
                plus_two(c, (ROUNDS - FIRST_PRODUCT) * CH + c)
            pool.wait_ge(f_ready, DOUBLE * CH)
            pool.wait_ge(w_low, len(LOOPED) * QR_PER)
            views = [weights(keep, name)[half][:, WIDTHS[name] // KT * (KT - 1):] for name in ("wq", "w1") for half in (0, 1)]
            for hi, lo in (views[0:2], views[2:4]):
                link(nc.gpsimd.tensor_copy(hi[2 * REST:3 * REST], lo[2 * REST:3 * REST]))
            for hi in views[::2]:
                link(nc.gpsimd.memset(hi[3 * REST:], 0.0))
            pool.wait_ge(mod_sb, 2)
            pool.wait_ge(gate_t, 1)
            pool.wait_ge(small_in, 64)
            for ph, (sh, scl, gt) in enumerate(((0, 3, 6), (9, 12, 15))):
                v = mod[:, scl:scl + KT, :].rearrange("r c b -> r b c")
                link(nc.gpsimd.tensor_scalar(moda[:, :, ph, 0:KT], v, 1.0, BIG_NORM * RS, ALU.add, ALU.mult))
                link(nc.gpsimd.tensor_scalar(moda[:, :, ph, 0:KT], moda[:, :, ph, 0:KT], gs[:, ph:ph + 1], None, ALU.mult))
                link(nc.gpsimd.tensor_copy(moda[:, :, ph, KT:AB], mod[:, sh:sh + KT, :].rearrange("r c b -> r b c")))
                link(nc.gpsimd.tensor_scalar(modg[:, :, ph], mod[:, gt:gt + KT, :].rearrange("r c b -> r b c"),
                                             1.0 / WS, None, ALU.mult))
            nc.gpsimd.tensor_tensor(modb[:], mod[:, 15:18, :].rearrange("r c b -> r b c"),
                                    b2[:, None, :].broadcast_to([R, B, KT]), ALU.mult).then_inc(mods_done, 1)

        @block.scalar
        def _(act):
            act.dma_start(adaw[:], io["adaT"]).then_inc(ada_in, 16)
            act.wait_ge(c_in, 16)
            nc.scalar.activation(cE[:], cT[:], ACT.Exp, scale=-1.0).then_inc(exp_c, 1)

            act.wait_ge(dve_step, 1)

            def root(j):
                act.wait_ge(row_bc, 2 * j + 1)
                nc.scalar.activation(sqv[:], VA[:, 0:N], ACT.Square, accum_out=ssq[:]).then_inc(ssq_ready, 1)
                act.wait_ge(ssq_ready, j + 1)
                nc.scalar.activation(sig[:], ssq[:], ACT.Sqrt, bias=tiny[:]).then_inc(sig_ready, 1)

            def high(r, k):
                n = r * QR_PER + (k - LOOPED[0] * QR_PER)
                act.wait_ge(raw_in[k], r * 16 + (16 - LOOPED[0] * 16))
                nc.scalar.activation(keep["wh"][:, bass.ds(n * PIECE, PIECE)], wraw[:, k], ACT.Copy, scale=WS).then_inc(w_high, 1)

            def evac_product(c, k):
                act.wait_ge(prod_mm, k + 1)
                q = slice(CH * c, CH * c + CH)
                dst = F if isinstance(k, int) and k < 4 else E
                nc.scalar.activation(dst[:, q], EP[c % 2][:].rearrange("p (q n) -> p q n", q=CH), ACT.Copy).then_inc(prod_sb, 1)

            def evac_turned(c, k):
                act.wait_ge(tr_mm, k - 3)
                q = slice(CH * c, CH * c + CH)
                nc.scalar.activation(ET[:, q], TP[c % 2][:].rearrange("p (q n) -> p q n", q=CH), ACT.Copy).then_inc(tr_sb, 1)

            def round_(r):
                for s in range(QR_PER):
                    j = r * QR_PER + s
                    root(j)
                    if isinstance(r, int):
                        if r < 2:
                            act.wait_ge(v_mm, j + 1)
                            if j >= 2:
                                act.wait_ge(v_ready, j - 1)
                            nc.scalar.activation(vraw[:, j % 2], MP[j % 2][0:B, :], ACT.Copy).then_inc(v_raw, 1)
                        if r == 2 and s == 3:
                            act.wait_ge(a_ready, 2)
                            nc.scalar.activation(ET[:], E[:], ACT.Copy, scale=-1.0).then_inc(at_neg, 1)
                        if r == FIRST_PRODUCT and s == 0:
                            nc.scalar.activation(Q[:], E[:], ACT.Copy, scale=1.0 / 6).then_inc(taylor_sb, 1)
                        if r >= FIRST_PRODUCT:
                            k = (r - FIRST_PRODUCT) * CH + s
                            evac_product(s, k)
                            if r == FIRST_PRODUCT:
                                act.wait_ge(taylor_sb, 1)
                                nc.scalar.activation(E[:, CH * s:CH * s + CH], EP[s % 2][:].rearrange("p (q n) -> p q n", q=CH),
                                                     ACT.Copy, scale=1.0 / 24).then_inc(taylor_sb, 1)
                            if k >= 5:
                                evac_turned((s - 1) % 4, k - 1)
                    else:
                        evac_product(s, r * CH + (s - FIRST_PRODUCT * CH))
                        evac_turned((s - 1) % 4, r * CH + (s - 1 - FIRST_PRODUCT * CH))
                        high(r, s)

            for r in range(FIRST_PRODUCT + 2):
                round_(r)
            with act.Fori(LOOPED[0], LOOPED[-1] + 1) as r:
                round_(r)
            round_(ROUNDS - 1)
            act.wait_ge(rcol_ready, 1)
            nc.scalar.activation(rcol[:, 1:2], rcol[:, 0:1], ACT.Sqrt).then_inc(sig_ready, 1)
            for k in range((ROUNDS - FIRST_PRODUCT) * CH, (ROUNDS + 2 - FIRST_PRODUCT) * CH + 1):
                if k < (ROUNDS + 2 - FIRST_PRODUCT) * CH:
                    evac_product(k % 4, k)
                evac_turned((k - 1) % 4, k - 1)
            act.wait_ge(mod_sb, 2)
            nc.scalar.activation(mod[:, 6:9], mod[:, 6:9], ACT.Tanh)
            nc.scalar.activation(mod[:, 15:18], mod[:, 15:18], ACT.Tanh).then_inc(gate_t, 1)
            for q in range(16):
                act.wait_ge(g_mm, q + 1)
                nc.scalar.activation(keep["G"][:, q], MP[q % 2][:, 0:W], ACT.Copy).then_inc(g_sb, 1)

        @block.vector
        def _(dve):
            dc = Count(dve_step)

            def link(ins):
                dve.wait_ge(dve_step, dc.inc(ins))

            nc.vector.memset(keep["ones"][:], 1.0)
            nc.vector.memset(At[:, N:], 0.0)
            link(nc.vector.memset(tiny[:], 1e-30))
            dve.wait_ge(exp_c, 1)
            link(nc.vector.tensor_scalar(cE[:], cE[:], 1.0, None, ALU.add))
            link(nc.vector.reciprocal(cR[:], cE[:]))
            nc.vector.tensor_tensor(sT[:], cT[:], cR[:], ALU.mult).then_inc(silu_ready, 1)
            dve.wait_ge(masks, 1)
            dve.wait_ge(p_in, 16)

            def step(j):
                at, rest, alpha = bass.ds(j, 1), bass.ds(j, N), VB[:, 0:1]
                dve.wait_ge(row_bc, 2 * j + 2)
                wait(dve, s_saved, j)
                hs_at = dc.inc(nc.vector.tensor_scalar(hs[:], alpha, 0.0, 0.5, ALU.is_ge, ALU.subtract))
                dots_at = dc.inc(nc.vector.scalar_tensor_tensor(prod[:], At[:, rest], 1.0, VB[:, 0:N], ALU.mult, ALU.mult, accum_out=dots[:]))
                dve.wait_ge(sig_ready, j + 1)
                rsig_at = dc.inc(nc.vector.reciprocal(rsig[:], sig[:]))
                dve.wait_ge(dve_step, hs_at)
                nc.vector.tensor_scalar(a2[:], alpha, hs[:], 4.0, ALU.mult, ALU.mult)
                nc.vector.scalar_tensor_tensor(am[:], At[:, at], hs[:], gtm[:, at], ALU.mult, ALU.mult)
                dve.wait_ge(dve_step, rsig_at)
                sig2_at = dc.inc(nc.vector.scalar_tensor_tensor(sig2[:], ssq[:], rsig[:], sig[:], ALU.mult, ALU.add))
                dve.wait_ge(dve_step, dots_at)
                dm_at = dc.inc(nc.vector.tensor_tensor(dm[:], dots[:], gtm[:, at], ALU.mult))
                dve.wait_ge(dve_step, sig2_at)
                t_at = dc.inc(nc.vector.scalar_tensor_tensor(t4[:], sig2[:], a2[:], sig2[:], ALU.add, ALU.mult))
                dve.wait_ge(dve_step, dm_at)
                dc.inc(nc.vector.scalar_tensor_tensor(wv[:], am[:], sig2[:], dm[:], ALU.mult, ALU.add))
                dve.wait_ge(dve_step, t_at)
                link(nc.vector.reciprocal(rt[:], t4[:]))
                link(nc.vector.tensor_tensor(nw[:], wv[:], rt[:], ALU.mult))
                nc.vector.scalar_tensor_tensor(At[:, rest], VB[:, 0:N], nw[:], At[:, rest], ALU.mult, ALU.add).then_inc(at_updated, 1)
                nc.vector.tensor_tensor(stall[:, 0, at], hs[:], sig2[:], ALU.mult)
                nc.vector.tensor_scalar(stall[:, 1, at], t4[:], 1.0, None, ALU.mult).then_inc(s_saved, 1)

            link(nc.vector.tensor_scalar(gtm[:], gtm[:], -4.0, None, ALU.mult))

            def round_(r):
                for s in range(QR_PER):
                    step(r * QR_PER + s)

            for r in range(LOOPED[0] - 1):
                round_(r)
            before = dc.n
            round_(LOOPED[0] - 1)
            per_round = dc.n - before
            dve.wait_ge(mod_mm, 1)
            dve.wait_ge(small_in, 64)
            for c in range(2):
                nc.vector.tensor_tensor(mod[:, 9 * c:9 * c + 9], MP[c][0:R, 0:9 * B].rearrange("r (c b) -> r c b", b=B),
                                        adab[:, 9 * c:9 * c + 9, None].broadcast_to([R, 9, B]), ALU.add).then_inc(mod_sb, 1)
            start = dc.n
            with dve.Fori(LOOPED[0], ROUNDS) as r:
                dc.base, dc.n = r * per_round, start - LOOPED[0] * per_round
                round_(r)
            dc.base, dc.n = 0, start + (ROUNDS - LOOPED[0]) * per_round
            dve.wait_ge(s_saved, D)
            dve.wait_ge(at_updated, D)
            for k, scale in enumerate((1.0, 0.25)):
                link(nc.vector.tensor_tensor_reduce(junk[:], stall[:, k], identd[:], scale, 0.0, ALU.mult, ALU.add, scol[:, k:k + 1]))
            link(nc.vector.tensor_tensor(At[:, 0:D], At[:, 0:D], lem[:], ALU.mult))
            nc.vector.reciprocal(rcol[:, 0:1], scol[:, 1:2]).then_inc(rcol_ready, 1)
            dve.wait_ge(sig_ready, D + 1)
            link(nc.vector.tensor_tensor(nwt[:, 0:1], rcol[:, 1:2], rcol[:, 1:2], ALU.mult))
            link(nc.vector.scalar_tensor_tensor(nwt[:, 1:2], nwt[:, 0:1], -0.5, scol[:, 1:2], ALU.mult, ALU.mult))
            link(nc.vector.scalar_tensor_tensor(rcol[:, 2:3], nwt[:, 1:2], 1.5, rcol[:, 1:2], ALU.add, ALU.mult))
            link(nc.vector.scalar_tensor_tensor(At[:, 0:D], identd[:], scol[:, 0:1], At[:, 0:D], ALU.mult, ALU.add))
            nc.vector.tensor_scalar(Vt[:], At[:, 0:N], rcol[:, 2:3], None, ALU.mult).then_inc(vt_ready, 1)
            wy = Count(wy_sb)
            dve.wait_ge(wy_pe, 1)
            wy.inc(nc.vector.tensor_copy(V[:], VA[0:CR, 0:KT * D].rearrange("r (k d) -> r k d", k=KT)))
            dve.wait_ge(wy_pe, 2)
            link(nc.vector.tensor_tensor(junk[0:D], lem[0:D], identd[0:D], ALU.subtract))
            link(nc.vector.scalar_tensor_tensor(XY[:, 0, 0:D], VB[0:D, 0:D], -1.0, junk[0:D], ALU.mult, ALU.mult))
            link(nc.vector.scalar_tensor_tensor(XT[:, 0], VB[0:D, 0:D], 0.25, gtm[0:D], ALU.mult, ALU.mult))
            dve.wait_ge(vt_ready, 1)
            wy.inc(nc.vector.tensor_copy(XY[:, 0, D:2 * D], Vt[0:D, 0:D]))
            for k in range(6):
                a, b = k % 2, (k + 1) % 2
                dve.wait_ge(wy_pe, 3 + k)
                last = nc.vector.tensor_tensor(XY[:, b, D:2 * D], VA[0:D, D:2 * D], XY[:, a, D:2 * D], ALU.add)
                if k < 5:
                    nc.vector.tensor_copy(XY[:, b, 0:D], VA[0:D, 0:D])
                    last = nc.vector.tensor_copy(XT[:, b], VB[0:D, 0:D])
                wy.inc(last)
            dve.wait_ge(wy_sb, 8)
            wy.inc(nc.vector.tensor_copy(Yd[:], XY[:, 0, None, D:2 * D].broadcast_to([D, 2, D])))
            dve.wait_ge(wy_pe, 9)
            nc.vector.tensor_scalar(UT[:, D:2 * R], VA[:, D:2 * R], -1.0, None, ALU.mult)
            nc.vector.tensor_scalar(UT[:, 2 * R:].rearrange("p (a r) -> p a r", r=REST), VA[:, None, 2 * R:N].broadcast_to([128, R // REST, REST]),
                                    -1.0, None, ALU.mult)
            wy.inc(nc.vector.scalar_tensor_tensor(UT[:, 0:D], VA[:, 0:D], -1.0, identd[:], ALU.mult, ALU.add))
            dve.wait_ge(wy_pe, 10)
            nc.vector.memset(keep["U"][:], 0.0).then_inc(wy_sb, 1)
            dve.wait_ge(wy_sb, 11)
            nc.vector.tensor_copy(keep["U"][:, 0:2, D:2 * D], VB[:, 0:2 * D].rearrange("r (k d) -> r k d", k=2))
            wy.inc(nc.vector.tensor_copy(keep["U"][0:REST, 2, D:2 * D], VB[0:REST, 2 * D:3 * D]))
            dve.wait_ge(wy_sb, 12)

        @block.tensor
        def _(pe):
            pe.wait_ge(p_in, 16)
            pe.wait_ge(masks, 1)

            def bcast(j, s):
                pe.wait_ge(sel_ready, j + 1)
                if not (isinstance(j, int) and j == 0):
                    pe.wait_ge(at_updated, j)
                for t in (VA, VB):
                    nc.tensor.matmul(t[:, 0:N], sel[:, s % 2], At[:, bass.ds(j, N)], start=True, stop=True).then_inc(row_bc, 1)

            def product(c, k):
                if isinstance(k, int) and k < 4:
                    pe.wait_ge(at_neg, 1)
                elif isinstance(k, int) and k < 8:
                    pe.wait_ge(q_ready, k - 3)
                else:
                    pe.wait_ge(f_ready, k - 7)
                    pe.wait_ge(tr_sb, k - 7)
                if not (isinstance(k, int) and k < 2):
                    pe.wait_ge(prod_sb, k - 1)
                out = EP[c % 2]
                for n in range(CH):
                    q = CH * c + n
                    o = out[:, 128 * n:128 * n + 128]
                    if isinstance(k, int) and k < 4:
                        mm = nc.tensor.matmul(o, ET[:, q], E[:, q], start=True, stop=True)
                    elif isinstance(k, int) and k < 8:
                        nc.tensor.matmul(o, ET[:, q], ident[:], start=True, stop=False)
                        mm = nc.tensor.matmul(o, F[:, q], Q[:, q], start=False, stop=True)
                    else:
                        mm = nc.tensor.matmul(o, ET[:, q], F[:, q], start=True, stop=True)
                mm.then_inc(prod_mm, 1)

            def turn(c, k):
                pe.wait_ge(prod_sb, k + 1)
                if not (isinstance(k, int) and k < 6):
                    pe.wait_ge(tr_sb, k - 5)
                for n in range(CH):
                    mm = nc.tensor.transpose(TP[c % 2][:, 128 * n:128 * n + 128], E[:, CH * c + n], ident[:])
                mm.then_inc(tr_mm, 1)

            def round_(r):
                for s in range(QR_PER):
                    j = r * QR_PER + s
                    bcast(j, s)
                    if isinstance(r, int):
                        if r < 2:
                            if j == 0:
                                pe.wait_ge(silu_ready, 1)
                            pe.wait_ge(wf_in[j % 2], 16 * (j // 2 + 1))
                            if j >= 2:
                                pe.wait_ge(v_raw, j - 1)
                            for k in range(KT):
                                mm = nc.tensor.matmul(MP[j % 2][0:B, :], sT[:, k], wfull[:, j % 2, k], start=(k == 0), stop=(k == 2))
                            mm.then_inc(v_mm, 1)
                        if r == LOOPED[0] - 1:
                            if s == 0:
                                pe.wait_ge(ada_in, 16)
                                pe.wait_ge(v_raw, 8)
                            lo, hi = (0, 5, 9, 14, 18)[s], (0, 5, 9, 14, 18)[s + 1]
                            for c in range(lo, hi):
                                o = MP[c // 9][:, (c % 9) * B:(c % 9 + 1) * B]
                                for k in range(KT):
                                    mm = nc.tensor.matmul(o, adaw[:, k, c * R:(c + 1) * R], sT[:, k], start=(k == 0), stop=(k == 2))
                            if s == 3:
                                mm.then_inc(mod_mm, 1)
                        if r >= FIRST_PRODUCT:
                            k = (r - FIRST_PRODUCT) * CH + s
                            product(s, k)
                            if k >= 5:
                                turn((s - 1) % 4, k - 1)
                    else:
                        product(s, r * CH + (s - FIRST_PRODUCT * CH))
                        turn((s - 1) % 4, r * CH + (s - 1 - FIRST_PRODUCT * CH))

            for r in range(FIRST_PRODUCT + 2):
                round_(r)
            with pe.Fori(LOOPED[0], LOOPED[-1] + 1) as r:
                round_(r)
            round_(ROUNDS - 1)
            KEND = (ROUNDS + 2 - FIRST_PRODUCT) * CH

            def tail(k):
                if k < KEND:
                    product(k % 4, k)
                turn((k - 1) % 4, k - 1)

            wy = Count(wy_pe)
            kk = (ROUNDS - FIRST_PRODUCT) * CH
            tail(kk)
            pe.wait_ge(vt_ready, 1)
            for k in range(KT):
                mm = nc.tensor.transpose(VA[0:CR, D * k:D * k + D], Vt[0:D, CR * k:CR * k + CR], ident[0:D, 0:D])
            wy.inc(mm)
            tail(kk + 1)
            pe.wait_ge(wy_sb, 1)
            for k in range(KT):
                mm = nc.tensor.matmul(VB[0:D, 0:D], V[:, k], V[:, k], start=(k == 0), stop=(k == 2))
            wy.inc(mm)
            for k in range(6):
                if k < 6 and kk + 2 + k <= KEND:
                    tail(kk + 2 + k)
                pe.wait_ge(wy_sb, 2 + k)
                mm = nc.tensor.matmul(VA[0:D, 0:2 * D], XT[:, k % 2], XY[:, k % 2], start=True, stop=True)
                if k < 5:
                    mm = nc.tensor.matmul(VB[0:D, 0:D], XY[:, k % 2, 0:D], XT[:, k % 2], start=True, stop=True)
                wy.inc(mm)
            for k in range(kk + 8, KEND + 1):
                tail(k)
            pe.wait_ge(wy_sb, 9)
            wy.inc(nc.tensor.matmul(VA[:, 0:N], Yd[:].rearrange("p a d -> p (a d)"), Vt[0:D, :], start=True, stop=True))
            pe.wait_ge(wy_sb, 10)
            for k in range(KT):
                mm = nc.tensor.transpose(VB[0:R, D * k:D * k + D], UT[0:D, R * k:R * k + R], ident[0:D, 0:D])
            wy.inc(mm)
            pe.wait_ge(mod_sb, 2)
            pe.wait_ge(tr_sb, KEND - 4)
            for q in range(16):
                if q >= 2:
                    pe.wait_ge(g_sb, q - 1)
                nc.tensor.matmul(MP[q % 2][:, 0:W], ET[:, q], UT[:], start=True, stop=True).then_inc(g_mm, 1)


def at(m, per, k=0):
    i, c = m
    return per * c + k if i is None else i * (2 * per) + (per * c + k)


def number(m):
    return m[1] if m[0] is None else m[0] * 2 + m[1]


def vector(t, m, per, k):
    return t[:, bass.ds(number(m) * per + k, 1)]


def uses(m, per, k=0):
    i, c = m
    return per * (c // 2) + k if i is None else i * per + (per * (c // 2) + k)


def valid(m, last):
    return None if m[0] is None and not 0 <= m[1] < last else m


def slots(eng, last, ahead, body, early=0):
    def one(i, c):
        body(lambda d: valid((i, c + d), last), (i, c))

    for c in range(-ahead, 2):
        one(None, c)
    with eng.Fori(1, last // 2 - 1 - early) as i:
        one(i, 0)
        one(i, 1)
    for c in range(last - 2 - 2 * early, last + 1):
        one(None, c)


def attention(nc, io, dram, keep):
    with ExitStack() as ctx:
        def sb(name, shape, dt=F32):
            return ctx.enter_context(nc.sbuf_tensor(name, shape, dt))

        def sem(name):
            return ctx.enter_context(nc.semaphore(name))

        xs = [sb(f"xs{p}", [R, KT, T]) for p in range(2)]
        Gb = [sb(f"Gb{p}", [128, 1, W]) for p in range(2)]
        zT = sb("zT", [R, T])
        x1 = [sb(f"x1{p}", [R, KT, T]) for p in range(2)]
        x1k = [sb(f"x1k{p}", [R, KT, T]) for p in range(2)]
        x2s = keep["x2s"]
        sq = sb("sq", [R, KT, T])
        sqa = sb("sqa", [R, T])
        ms = sb("ms", [R, T])
        ln = sb("ln", [R, T])
        ry = sb("ry", [R, T])
        ru = sb("ru", [R, T])
        rv = sb("rv", [R, T])
        rs = sb("rs", [R, T])
        h = sb("h", [R, KT, T])
        hh = sb("hh", [R, KT, T], F16)
        hl = sb("hl", [R, KT - 1, T], F16)
        bq = sb("bq", [128, QKV])
        qk = sb("qk", [128, 2, 2 * N])
        qks = sb("qks", [128, 2, 2 * N])
        hss = sb("hss", [128, 2 * 32])
        hm = sb("hm", [128, 2 * 32])
        hr2 = sb("hr2", [128, 2 * 32])
        hln = sb("hln", [128, 2 * 32])
        hy = sb("hy", [128, 2 * 32])
        hu = sb("hu", [128, 2 * 32])
        hv = sb("hv", [128, 2 * 32])
        hr = sb("hr", [128, 2 * 32])
        gv = sb("gv", [128, 2, 2, H])
        gk = sb("gk", [128, 4])
        stk = sb("stk", [128, 2, 2 * H, 64], F16)
        va = [sb(f"va{p}", [128, 2, H, 32]) for p in range(2)]
        qT = sb("qT", [128, HP, T], F16)
        kT = sb("kT", [128, HP, T], F16)
        pt = [sb(f"pt{j}", [128, 2, 2, T]) for j in range(4)]
        OT = [sb(f"OT{p}", [128, 4, T]) for p in range(2)]
        sums = sb("sums", [128, 32])
        rsums = sb("rsums", [128, 32])
        recs = sb("recs", [128, 4, T])
        OT2 = sb("OT2", [128, 4, T])
        oh = sb("oh", [128, 4, T], F16)
        ol = sb("ol", [128, 4, T], F16)
        id16 = sb("id16", [128, 128], F16)
        pick = sb("pick", [128, 128])
        wqh, wql = [w.rearrange("p (k n) -> p k n", k=KT) for w in weights(keep, "wq")]
        wph, wpl = [w.rearrange("p (g n) -> p g n", g=4) for w in weights(keep, "wp")]

        SP = [ctx.enter_context(nc.psum_tensor(f"scores{j}", [128, 2, 512], F32)) for j in range(2)]
        OP = ctx.enter_context(nc.psum_tensor("heads_out", [128, 512], F32))
        RB = [ctx.enter_context(nc.psum_tensor(f"ring{j}", [128, 512], F32)) for j in range(3)]
        ORDER = ["z", "q0", "q1", "d0", "d1", "d2", "sb0", "sb1", "q2", "q3", "ss", "pj0", "pj1", "pj2",
                 "t0", "t1", "t2", "t3"]
        rb = {u: RB[k % 3] for k, u in enumerate(ORDER)}

        x_in = [sem("x_in0"), sem("x_in1")]
        keep_in = [sem("keep_in0"), sem("keep_in1")]
        x2_out = keep["x2_out"]
        setup_in = sem("setup_in")
        pair_in = sem("pair_in")
        setup_pool = sem("setup_pool")
        setup_dve = sem("setup_dve")
        names_pe = ("z_mm", "d_mm", "ss_mm", "qkv_mm", "tr_mm", "s_mm", "av_mm", "sb_mm", "pj_mm")
        (z_mm, d_mm, ss_mm, qkv_mm, tr_mm, s_mm, av_mm, sb_mm, pj_mm) = [sem(n) for n in names_pe]
        names_act = ("z_sb", "sq_sb", "ln_sb", "ry_sb", "hh_sb", "p_sb", "ot_sb", "oh_sb", "qks_sb", "hln_sb", "hy_sb", "qh_sb")
        (z_sb, sq_sb, ln_sb, ry_sb, hh_sb, p_sb, ot_sb, oh_sb, qks_sb, hln_sb, hy_sb, qh_sb) = [sem(n) for n in names_act]
        names_dve = ("rec_sb", "x1_sb", "ms_sb", "newton", "rs_sb", "h_sb", "ol_sb", "hl_sb", "x2_sb", "qkv_sb",
                     "hss_sb", "hm_sb", "hnewton", "hr_sb", "qkn_sb", "tr_sb")
        (rec_sb, x1_sb, ms_sb, newton, rs_sb, h_sb, ol_sb, hl_sb, x2_sb, qkv_sb,
         hss_sb, hm_sb, hnewton, hr_sb, qkn_sb, tr_sb) = [sem(n + "_a") for n in names_dve]
        om_sb = sem("om_sb")
        added = sem("added")
        sums_in = sem("sums_in")
        recs_in = sem("recs_in")
        READER = {"z": (z_sb, 1, 2), "sb": (om_sb, 2, -1), "d": (x1_sb, 3, 2), "ss": (ms_sb, 1, 2),
                  "pj": (x2_sb, 3, -1), "q": (qkv_sb, 4, 1), "t": (tr_sb, 4, 1)}
        t_sb, stk_sb, again_sb = sem("t_sb"), sem("stk_sb"), sem("again_sb")

        block = ctx.enter_context(nc.Block())

        @block.sync
        def _(sp):
            sp.dma_start(bq[:], io["bq"].broadcast_to([128, QKV])).then_inc(setup_in, 16)
            sp.dma_start(gk[:, 0:1], io["qg"].broadcast_to([128, 1])).then_inc(setup_in, 16)
            sp.dma_start(gk[:, 1:2], io["kg"].broadcast_to([128, 1])).then_inc(setup_in, 16)

            def load(m):
                p, s = m[1] % 2, bass.ds(number(m), 1)
                q = bass.ds(m[1] // 2 if m[0] is None else m[0] + m[1] // 2, 1)
                half = slice(D * p, D * p + D)
                wait(sp, x1_sb, at(m, 3, -3))
                sp.dma_start(Gb[p][half], keep["G"][half, q]).then_inc(x_in[p], 16)
                sp.dma_start(xs[p][:], io["x"][s].rearrange("o r k t -> (o r) k t")).then_inc(x_in[p], 16)

            load((None, 0))
            load((None, 1))
            for p in range(2):
                sp.sem_inc(x2_out[p], 16)

            def body(batch, centre):
                mid, back, f3 = batch(0), batch(-1), batch(3)
                if centre[0] is None and centre[1] == B - 1:
                    for p in range(2):
                        sp.wait_ge(x2_out[p], 32)
                    load_pair(sp, dram, (None, 0), keep["xp"], keep["xf"], pair_in)
                if mid is not None:
                    p = mid[1] % 2
                    sp.wait_ge(x1_sb, at(mid, 3, 3))
                    sp.dma_start(x1k[p][:], x1[p][:]).then_inc(keep_in[p], 16)
                if back is not None:
                    sp.wait_ge(ot_sb, at(back, 4, 4))
                    for j in range(4):
                        r = 32 * j + HD
                        sp.dma_start(sums[32 * j:32 * j + 32], OT[back[1] % 2][r:r + 1].rearrange("o g t -> o (g t)")
                                     .rearrange("o (r c) -> o r c", r=32)).then_inc(sums_in, 16)
                    sp.wait_ge(rec_sb, at(back, 1, 1))
                    for j in range(4):
                        r = 32 * j + HD
                        sp.dma_start(recs[r:r + 1].rearrange("o g t -> o (g t)").rearrange("o (r c) -> o r c", r=32),
                                     rsums[32 * j:32 * j + 32]).then_inc(recs_in, 16)
                if f3 is not None and not (f3[0] is None and f3[1] < 2):
                    load(f3)
                if back is not None:
                    p, s = back[1] % 2, bass.ds(number(back), 1)
                    sp.wait_ge(x2_sb, at(back, 3, 3))
                    sp.dma_start(dram["x2"][s].rearrange("o r k t -> (o r) k t"), x2s[p][:]).then_inc(x2_out[p], 16)

            sp.dma_start(keep["b1"][:], io["b1"]).then_inc(pair_in, 16)
            slots(sp, B, 2, body, early=1)
            sp.wait_ge(pair_in, 96)

        @block.gpsimd
        def _(pool):
            sc = Count(setup_pool)

            def link(ins):
                pool.wait_ge(setup_pool, sc.inc(ins))

            for p in range(2):
                link(nc.gpsimd.memset(Gb[p][D - D * p:2 * D - D * p], 0.0))
            nc.gpsimd.memset(id16[:], 0.0)
            nc.gpsimd.memset(pick[:], 0.0)
            nc.gpsimd.memset(stk[:], 0.0)
            nc.gpsimd.memset(va[0][:], 0.0)
            nc.gpsimd.memset(recs[:], 0.0)
            link(nc.gpsimd.memset(va[1][:], 0.0))

            def body(batch, _centre):
                nx, f2 = batch(1), batch(2)
                if f2 is not None:
                    pool.wait_ge(sq_sb, at(f2, 1, 1))
                    nc.gpsimd.tensor_tensor(sqa[:], sq[:, 0], sq[:, 1], ALU.add).then_inc(added, 1)
                    pool.wait_ge(added, at(f2, 2, 1))
                    nc.gpsimd.tensor_tensor(sqa[:], sqa[:], sq[:, 2], ALU.add).then_inc(added, 1)
                if nx is not None:
                    pool.wait_ge(qh_sb, at(nx, 2, 1))
                    v = qk[:, 0].rearrange("p (h d) -> p h d", d=HD)
                    nc.gpsimd.tensor_tensor(stk[:, 0, 0:H, HD:2 * HD], v[:, 0:H], stk[:, 0, 0:H, 0:HD], ALU.subtract)
                    nc.gpsimd.tensor_tensor(stk[:, 0, H:2 * H, 2 * HD:3 * HD], v[:, H:2 * H], stk[:, 0, H:2 * H, 0:HD],
                                            ALU.subtract).then_inc(stk_sb, 1)
                if f2 is not None:
                    if nx is not None:
                        pool.wait_ge(stk_sb, at(nx, 1, 1))
                    pool.wait_ge(rs_sb, at(f2, 1, 1))
                    nc.gpsimd.tensor_tensor(h[:], x1[f2[1] % 2][:], rs[:, None, :].broadcast_to([R, KT, T]), ALU.mult).then_inc(t_sb, 1)

            nc.gpsimd.affine_select(out=id16[:], in_=id16[:], compare_op=ALU.not_equal, fill=1.0, base=0,
                                    pattern=[[-1, 128]], channel_multiplier=1)
            nc.gpsimd.affine_select(out=pick[:].rearrange("p (j r) -> p j r", j=4), in_=pick[:].rearrange("p (j r) -> p j r", j=4),
                                    compare_op=ALU.not_equal, fill=1.0, base=-HD, pattern=[[-32, 4], [0, 32]],
                                    channel_multiplier=1)
            nc.gpsimd.memset(va[0][:, :, :, HD:HD + 1], 1.0)
            nc.gpsimd.memset(va[1][:, :, :, HD:HD + 1], 1.0)
            nc.gpsimd.memset(stk[:, :, 0:H, 3 * HD:3 * HD + 2], 1.0)
            pool.wait_ge(setup_dve, 3)
            nc.gpsimd.tensor_copy(stk[:, 0, H:2 * H, 3 * HD], gk[:, 2:3].broadcast_to([128, H]))
            link(nc.gpsimd.tensor_copy(stk[:, 1, H:2 * H, 3 * HD], gk[:, 2:3].broadcast_to([128, H])))
            for t in range(2):
                ins = nc.gpsimd.tensor_tensor(stk[:, t, H:2 * H, 3 * HD + 1], gk[:, 2:3].broadcast_to([128, H]),
                                              stk[:, t, H:2 * H, 3 * HD], ALU.subtract)
            link(ins)
            slots(pool, B, 2, body)

        @block.scalar
        def _(act):
            def ex(mid, hp):
                act.wait_ge(s_mm, at(mid, 8, hp + 1))
                wait(act, av_mm, at(mid, 8, hp - 3))
                nc.scalar.activation(pt[hp % 4][:].rearrange("p e k t -> p (e k t)"), SP[hp % 2][:].rearrange("p e n -> p (e n)"),
                                     ACT.Exp).then_inc(p_sb, 1)

            def heads_out(mid, g):
                act.wait_ge(av_mm, at(mid, 8, 2 * g + 2))
                wait(act, om_sb, at(mid, 2, -2))
                nc.scalar.activation(OT[mid[1] % 2][:, g], OP[:, 0:T], ACT.Copy).then_inc(ot_sb, 1)

            def squares(nx, t):
                act.wait_ge(qkv_sb, at(nx, 4, 2 * t + 2))
                nc.scalar.activation(qks[:, t], qk[:, t], ACT.Square).then_inc(qks_sb, 1)

            def head_roots(nx, t):
                c = slice(32 * t, 32 * t + 32)
                act.wait_ge(hm_sb, at(nx, 2, t + 1))
                nc.scalar.activation(hln[:, c], hm[:, c], ACT.Ln, scale=RS * RS).then_inc(hln_sb, 1)
                act.wait_ge(hln_sb, at(nx, 2, t + 1))
                nc.scalar.activation(hy[:, c], hln[:, c], ACT.Exp, scale=-0.5).then_inc(hy_sb, 1)

            def high_halves(nx, t):
                act.wait_ge(qkn_sb, at(nx, 2, t + 1))
                nc.scalar.activation(stk[:, t, :, 0:HD], qk[:, t].rearrange("p (h d) -> p h d", d=HD), ACT.Copy).then_inc(qh_sb, 1)

            def body(batch, centre):
                mid, nx, f2, back = batch(0), batch(1), batch(2), batch(-1)
                if centre[0] is None and centre[1] == -1:
                    act.wait_ge(setup_pool, 5)
                if mid is not None:
                    ex(mid, 0)
                if nx is not None:
                    act.wait_ge(h_sb, at(nx, 3, 3))
                    nc.scalar.activation(hh[:], h[:], ACT.Copy).then_inc(hh_sb, 1)
                if mid is not None:
                    ex(mid, 1)
                if f2 is not None:
                    act.wait_ge(z_mm, at(f2, 1, 1))
                    nc.scalar.activation(zT[:], rb["z"][:, 0:T], ACT.Copy).then_inc(z_sb, 1)
                if mid is not None:
                    ex(mid, 2)
                if nx is not None:
                    squares(nx, 0)
                if mid is not None:
                    heads_out(mid, 0)
                    ex(mid, 3)
                if nx is not None:
                    head_roots(nx, 0)
                if f2 is not None:
                    act.wait_ge(x1_sb, at(f2, 3, 3))
                    nc.scalar.activation(sq[:, 0:2], x1[f2[1] % 2][:, 0:2], ACT.Square)
                    nc.scalar.activation(sq[:, 2], x1[f2[1] % 2][:, 2], ACT.Square, scale=0.5).then_inc(sq_sb, 1)
                if mid is not None:
                    ex(mid, 4)
                if nx is not None:
                    high_halves(nx, 0)
                if back is not None:
                    act.wait_ge(om_sb, at(back, 2, 2))
                    nc.scalar.activation(oh[:], OT2[:], ACT.Copy).then_inc(oh_sb, 1)
                if nx is not None:
                    squares(nx, 1)
                if mid is not None:
                    heads_out(mid, 1)
                    ex(mid, 5)
                if nx is not None:
                    head_roots(nx, 1)
                    high_halves(nx, 1)
                if f2 is not None:
                    act.wait_ge(ms_sb, at(f2, 1, 1))
                    nc.scalar.activation(ln[:], ms[:], ACT.Ln, scale=RS * RS).then_inc(ln_sb, 1)
                    act.wait_ge(ln_sb, at(f2, 1, 1))
                    nc.scalar.activation(ry[:], ln[:], ACT.Exp, scale=-0.5).then_inc(ry_sb, 1)
                if mid is not None:
                    ex(mid, 6)
                    heads_out(mid, 2)
                    ex(mid, 7)
                    heads_out(mid, 3)

            nc.scalar.preload_act_table_set("natural_log_exp_and_others")
            slots(act, B, 2, body)

        @block.vector
        def _(dve):
            dve.wait_ge(setup_in, 48)
            nc.vector.tensor_scalar(gv[:, :, 0, :], gk[:, None, 0:1].broadcast_to([128, 2, H]), RS, None, ALU.mult)
            nc.vector.tensor_scalar(gv[:, :, 1, :], gk[:, None, 1:2].broadcast_to([128, 2, H]), RS * HEAD_NORM, None, ALU.mult)
            nc.vector.tensor_tensor(gk[:, 2:3], gk[:, 0:1], gk[:, 1:2], ALU.mult).then_inc(setup_dve, 1)
            dve.wait_ge(setup_dve, 1)
            nc.vector.tensor_scalar(gk[:, 3:4], gk[:, 2:3], -1.0, None, ALU.mult).then_inc(setup_dve, 1)
            dve.wait_ge(setup_dve, 2)
            nc.vector.tensor_scalar(gk[:, 2:3], gk[:, 3:4], gk[:, 2:3], -HEAD_NORM, ALU.max, ALU.mult).then_inc(setup_dve, 1)

            def qk_out(nx, t):
                dve.wait_ge(qkv_mm, at(nx, 4, 2 * t + 1))
                a = rb[f"q{2 * t}"][:, 0:432]
                nc.vector.scalar_tensor_tensor(qk[:, t, 0:432], a, 1.0 / WS, bq[:, 0:432], ALU.mult, ALU.add).then_inc(qkv_sb, 1)

            def kv_out(nx, t):
                dve.wait_ge(qkv_mm, at(nx, 4, 2 * t + 2))
                a = rb[f"q{2 * t + 1}"]
                nc.vector.scalar_tensor_tensor(qk[:, t, 432:576], a[:, 0:144], 1.0 / WS, bq[:, 432:576], ALU.mult, ALU.add)
                nc.vector.scalar_tensor_tensor(va[nx[1] % 2][:, t, :, 0:HD], a[:, 144:432].rearrange("p (h d) -> p h d", d=HD), 1.0 / WS,
                                               bq[:, 576:864].rearrange("p (h d) -> p h d", d=HD), ALU.mult, ALU.add).then_inc(qkv_sb, 1)

            def head_squares(nx, t):
                dve.wait_ge(qks_sb, at(nx, 2, t + 1))
                nc.vector.tensor_reduce(hss[:, 32 * t:32 * t + 32], qks[:, t].rearrange("p (h d) -> p h d", d=HD), AX.X, ALU.add).then_inc(hss_sb, 1)
                dve.wait_ge(hss_sb, at(nx, 2, t + 1))
                nc.vector.tensor_scalar(hm[:, 32 * t:32 * t + 32], hss[:, 32 * t:32 * t + 32], GUARD, None, ALU.max).then_inc(hm_sb, 1)

            def head_norm(nx, t):
                c = slice(32 * t, 32 * t + 32)
                dve.wait_ge(hy_sb, at(nx, 2, t + 1))
                dve.wait_ge(hm_sb, at(nx, 2, t + 1))
                nc.vector.scalar_tensor_tensor(hu[:, c], hm[:, c], -0.5 * RS * RS, hy[:, c], ALU.mult, ALU.mult).then_inc(hnewton, 1)
                dve.wait_ge(hnewton, at(nx, 6, 3 * t + 1))
                nc.vector.tensor_tensor(hv[:, c], hu[:, c], hy[:, c], ALU.mult).then_inc(hnewton, 1)
                dve.wait_ge(hnewton, at(nx, 6, 3 * t + 2))
                nc.vector.scalar_tensor_tensor(hr[:, c], hv[:, c], 1.5, hy[:, c], ALU.add, ALU.mult).then_inc(hnewton, 1)
                dve.wait_ge(hnewton, at(nx, 6, 3 * t + 3))
                nc.vector.tensor_tensor(hr2[:, c], hr[:, c], gv[:, t].rearrange("p a h -> p (a h)"), ALU.mult).then_inc(hr_sb, 1)
                dve.wait_ge(hr_sb, at(nx, 2, t + 1))
                v = qk[:, t].rearrange("p (h d) -> p h d", d=HD)
                nc.vector.tensor_tensor(v, v, hr2[:, c, None].broadcast_to([128, 32, HD]), ALU.mult).then_inc(qkn_sb, 1)

            def high_again(nx, t):
                dve.wait_ge(qkn_sb, at(nx, 2, t + 1))
                v = qk[:, t].rearrange("p (h d) -> p h d", d=HD)
                nc.vector.tensor_copy(stk[:, t, 0:H, 2 * HD:3 * HD], v[:, 0:H])
                nc.vector.tensor_copy(stk[:, t, H:2 * H, HD:2 * HD], v[:, H:2 * H]).then_inc(again_sb, 1)

            def normalised(back, u):
                dve.wait_ge(sb_mm, at(back, 2, u + 1))
                nc.vector.tensor_tensor(OT2[:, 2 * u:2 * u + 2], rb[f"sb{u}"][:].rearrange("p (g t) -> p g t", g=2),
                                        OT[back[1] % 2][:, 2 * u:2 * u + 2], ALU.mult).then_inc(om_sb, 1)

            def x2_tile(back, k):
                q = back[1] % 2
                if k == 0:
                    dve.wait_ge(keep_in[q], uses(back, 16, 16))
                    dve.wait_ge(x2_out[q], uses(back, 16, 16))
                dve.wait_ge(pj_mm, at(back, 3, k + 1))
                nc.vector.scalar_tensor_tensor(x2s[q][:, k], rb[f"pj{k}"][:, 0:T], vector(keep["gate"], back, 2 * GT, k), x1k[q][:, k],
                                               ALU.mult, ALU.add).then_inc(x2_sb, 1)

            def body(batch, centre):
                nx, f2, back = batch(1), batch(2), batch(-1)
                if centre[0] is None and centre[1] == -1:
                    dve.wait_ge(setup_pool, 5)
                if nx is not None:
                    dve.wait_ge(hh_sb, at(nx, 1, 1))
                    nc.vector.tensor_tensor(hl[:], h[:, 0:2], hh[:, 0:2], ALU.subtract)
                    low = slice(REST, 2 * REST)
                    nc.vector.tensor_tensor(hh[low, 2], h[low, 2], hh[low, 2], ALU.subtract).then_inc(hl_sb, 1)
                if back is not None:
                    dve.wait_ge(sums_in, at(back, 64, 64))
                    nc.vector.reciprocal(rsums[:], sums[:]).then_inc(rec_sb, 1)
                if nx is not None:
                    qk_out(nx, 0)
                    kv_out(nx, 0)
                    head_squares(nx, 0)
                if f2 is not None:
                    p = f2[1] % 2
                    dve.wait_ge(x_in[p], uses(f2, 32, 32))
                    wait(dve, keep_in[p], uses(f2, 16, 0))
                    for k in range(KT):
                        dve.wait_ge(d_mm, at(f2, 3, k + 1))
                        nc.vector.tensor_tensor(x1[p][:, k], rb[f"d{k}"][:, 0:T], xs[p][:, k], ALU.add).then_inc(x1_sb, 1)
                if nx is not None:
                    head_norm(nx, 0)
                if back is not None:
                    normalised(back, 0)
                    normalised(back, 1)
                if nx is not None:
                    high_again(nx, 0)
                if nx is not None:
                    qk_out(nx, 1)
                if back is not None:
                    dve.wait_ge(oh_sb, at(back, 1, 1))
                    nc.vector.tensor_tensor(ol[:], OT2[:], oh[:], ALU.subtract).then_inc(ol_sb, 1)
                if nx is not None:
                    kv_out(nx, 1)
                    head_squares(nx, 1)
                if f2 is not None:
                    dve.wait_ge(ss_mm, at(f2, 1, 1))
                    nc.vector.tensor_scalar(ms[:], rb["ss"][:, 0:T], GUARD, None, ALU.max).then_inc(ms_sb, 1)
                if back is not None:
                    x2_tile(back, 0)
                if nx is not None:
                    head_norm(nx, 1)
                    high_again(nx, 1)
                if back is not None:
                    x2_tile(back, 1)
                if nx is not None:
                    dve.wait_ge(qh_sb, at(nx, 2, 2))
                    v = qk[:, 1].rearrange("p (h d) -> p h d", d=HD)
                    nc.vector.tensor_tensor(stk[:, 1, 0:H, HD:2 * HD], v[:, 0:H], stk[:, 1, 0:H, 0:HD], ALU.subtract)
                    nc.vector.tensor_tensor(stk[:, 1, H:2 * H, 2 * HD:3 * HD], v[:, H:2 * H], stk[:, 1, H:2 * H, 0:HD],
                                            ALU.subtract).then_inc(again_sb, 1)
                if back is not None:
                    x2_tile(back, 2)
                def copy_turned(u):
                    if nx is not None:
                        dve.wait_ge(tr_mm, at(nx, 4, u + 1))
                        dst = (qT, kT)[u % 2]
                        nc.vector.tensor_copy(dst[:, 4 * (u // 2):4 * (u // 2) + 4].rearrange("p a t -> p (a t)"),
                                              rb[f"t{u}"][:].bitcast(F16)).then_inc(tr_sb, 1)

                if f2 is not None:
                    dve.wait_ge(ry_sb, at(f2, 1, 1))
                    dve.wait_ge(ms_sb, at(f2, 1, 1))
                    nc.vector.scalar_tensor_tensor(ru[:], ms[:], -0.5 * RS * RS, ry[:], ALU.mult, ALU.mult).then_inc(newton, 1)
                    dve.wait_ge(newton, at(f2, 2, 1))
                    nc.vector.tensor_tensor(rv[:], ru[:], ry[:], ALU.mult).then_inc(newton, 1)
                copy_turned(0)
                if f2 is not None:
                    dve.wait_ge(newton, at(f2, 2, 2))
                    nc.vector.scalar_tensor_tensor(rs[:], rv[:], 1.5, ry[:], ALU.add, ALU.mult).then_inc(rs_sb, 1)
                for u in range(1, 4):
                    copy_turned(u)
                if f2 is not None:
                    dve.wait_ge(t_sb, at(f2, 1, 1))
                    for k in range(KT):
                        nc.vector.tensor_scalar(h[:, k], h[:, k], vector(keep["ab"], f2, 2 * AB, k), vector(keep["ab"], f2, 2 * AB, KT + k),
                                                ALU.mult, ALU.add).then_inc(h_sb, 1)

            slots(dve, B, 2, body)

        @block.tensor
        def _(pe):
            pe.wait_ge(setup_pool, 2)

            def take(use, centre):
                k, (i, c) = ORDER.index(use), centre
                while True:
                    k -= 3
                    if k < 0:
                        k, c = k + len(ORDER), c - 1
                    if i is None and c < -2:
                        return rb[use]
                    kind = ORDER[k].rstrip("0123456789")
                    reader, per, place = READER[kind]
                    m = valid((i, c + place), B)
                    if m is not None:
                        pe.wait_ge(reader, at(m, per, int(ORDER[k][len(kind):] or 0) + 1))
                        return rb[use]

            def scores(mid, hp):
                if hp % 4 == 0:
                    pe.wait_ge(tr_sb, at(mid, 4, 2 + hp // 2))
                wait(pe, p_sb, at(mid, 8, hp - 1))
                for kt in range(2):
                    for e in range(2):
                        r = slice(64 * e, 64 * e + 64)
                        mm = nc.tensor.matmul(SP[hp % 2][:, e, kt * T:kt * T + T], kT[r, hp, kt * 128:kt * 128 + 128],
                                              qT[r, hp, :], start=True, stop=True)
                mm.then_inc(s_mm, 1)

            def values(mid, hp):
                pe.wait_ge(p_sb, at(mid, 8, hp + 1))
                if hp % 2 == 0:
                    wait(pe, ot_sb, at(mid, 4, hp // 2))
                for kt in range(2):
                    for e in range(2):
                        hd = 2 * hp + e
                        j = 32 * (hd % 4)
                        mm = nc.tensor.matmul(OP[j:j + 32, 0:T], va[mid[1] % 2][:, kt, hd, :], pt[hp % 4][:, e, kt, :],
                                              start=(kt == 0), stop=(kt == 1), skip_group_check=True)
                mm.then_inc(av_mm, 1)

            def body(batch, centre):
                mid, nx, f2, back = batch(0), batch(1), batch(2), batch(-1)
                if centre[0] is None and centre[1] == -1:
                    pe.wait_ge(setup_pool, 5)

                def heads(v, s):
                    if mid is not None:
                        if v is not None:
                            values(mid, v)
                        if s is not None:
                            scores(mid, s)

                def qkv(t):
                    for half in range(2):
                        o = take(f"q{2 * t + half}", centre)
                        c = slice(432 * half, 432 * half + 432)
                        terms = [(x, w, k) for k in range(2) for x, w in ((hh, wqh), (hh, wql), (hl, wqh))] + [(hh, wqh, 2)]
                        for n, (x, w, k) in enumerate(terms):
                            mm = nc.tensor.matmul(o[:, 0:432], x[:, k, 128 * t:128 * t + 128], w[:, k, c],
                                                  start=(n == 0), stop=(n == 6))
                        mm.then_inc(qkv_mm, 1)

                def project(m):
                    o = take(f"pj{m}", centre)
                    c = slice(m * R, m * R + R)
                    terms = [(w, x, g) for g in range(4) for w, x in ((wph, oh), (wph, ol), (wpl, oh))]
                    for n, (w, x, g) in enumerate(terms):
                        mm = nc.tensor.matmul(o[:, 0:T], w[:, g, c], x[:, g], start=(n == 0), stop=(n == 11))
                    mm.then_inc(pj_mm, 1)

                heads(None, 0)
                heads(None, 1)
                if f2 is not None:
                    p = f2[1] % 2
                    pe.wait_ge(x_in[p], uses(f2, 32, 32))
                    o = take("z", centre)
                    u = slice(D - D * p, 3 * D - D * p)
                    for k in range(KT):
                        mm = nc.tensor.matmul(o[:, 0:T], keep["U"][:, k, u], xs[p][:, k], start=(k == 0), stop=(k == 2))
                    mm.then_inc(z_mm, 1)
                heads(0, 2)
                if nx is not None:
                    pe.wait_ge(hl_sb, at(nx, 1, 1))
                    qkv(0)
                heads(1, 3)
                if f2 is not None:
                    pe.wait_ge(z_sb, at(f2, 1, 1))
                    for m in range(KT):
                        o = take(f"d{m}", centre)
                        nc.tensor.matmul(o[:, 0:T], Gb[p][:, 0, m * R:m * R + R], zT[:], start=True, stop=True).then_inc(d_mm, 1)
                heads(2, 4)
                if back is not None:
                    pe.wait_ge(recs_in, at(back, 64, 64))
                    for u in range(2):
                        o = take(f"sb{u}", centre)
                        nc.tensor.matmul(o[:], pick[:], recs[:, 2 * u:2 * u + 2].rearrange("p g t -> p (g t)"),
                                         start=True, stop=True).then_inc(sb_mm, 1)
                if nx is not None:
                    qkv(1)
                heads(3, 5)
                if f2 is not None:
                    pe.wait_ge(added, at(f2, 2, 2))
                    o = take("ss", centre)
                    nc.tensor.matmul(o[:, 0:T], keep["ones"][:], sqa[:], start=True, stop=True).then_inc(ss_mm, 1)
                if back is not None:
                    pe.wait_ge(ol_sb, at(back, 1, 1))
                    project(0)
                    project(1)
                    project(2)
                heads(4, 6)
                heads(5, 7)
                if nx is not None:
                    pe.wait_ge(stk_sb, at(nx, 1, 1))
                    pe.wait_ge(again_sb, at(nx, 3, 3))
                    for u in range(4):
                        o = take(f"t{u}", centre)[:].bitcast(F16)
                        for n in range(4):
                            hd = H * (u % 2) + 8 * (u // 2) + 2 * n
                            for t in range(2):
                                mm = nc.tensor.transpose(o[:, n * T + 128 * t:n * T + 128 * t + 128],
                                                         stk[:, t, hd:hd + 2, :].rearrange("p h d -> p (h d)"), id16[:])
                        mm.then_inc(tr_mm, 1)
                heads(6, None)
                heads(7, None)

            slots(pe, B, 2, body)


def load_pair(sp, dram, m, xp, xf, landed):
    sp.dma_start(xp[:], dram["x2"][bass.ds(number(m) * 2, 2)].rearrange("b r k t -> r k b t")).then_inc(landed, 16)
    QT = 2 * T // 4
    for q in range(4):
        b, rows = bass.ds(number(m) * 2 + q // 2, 1), slice(REST * q, REST * (q + 1))
        sp.dma_start(xf[rows], dram["x2"][b, rows, 2, (q % 2) * QT:(q % 2 + 1) * QT].rearrange("b r t -> (b r) t")).then_inc(landed, 16)


def mlp(nc, io, dram, keep, out):
    T2 = 2 * T
    QT = T2 // 4
    with ExitStack() as ctx:
        def sb(name, shape, dt=F32):
            return ctx.enter_context(nc.sbuf_tensor(name, shape, dt))

        def sem(name):
            return ctx.enter_context(nc.semaphore(name))

        xp = [keep["xp"], sb("xp1", [R, KT, 2, T])]
        sq = sb("sqm", [R, KT, T2])
        sqa = sb("sqam", [R, T2])
        ms = sb("msm", [R, T2])
        ln = sb("lnm", [R, T2])
        ry = sb("rym", [R, T2])
        ru = sb("rum", [R, T2])
        rv = sb("rvm", [R, T2])
        rs = sb("rsm", [R, T2])
        h = sb("hm2", [R, KT, 2, T])
        hh = [sb(f"hh{p}", [R, KT, T2], F16) for p in range(2)]
        hl = [sb(f"hl{p}", [R, KT - 1, T2], F16) for p in range(2)]
        b1 = keep["b1"]
        g = [sb(f"g{j}", [128, T2]) for j in range(3)]
        gh = sb("gh", [128, MT, T2], F16)
        gl = sb("gl", [128, MT, T2], F16)
        yt = sb("yt", [R, 2, 2, T])
        yf = sb("yf", [R, QT])
        ys = [sb(f"ys{p}", [R, 2, 2, T]) for p in range(2)]
        ysf = [sb(f"ysf{p}", [R, QT]) for p in range(2)]
        xf = [keep["xf"], sb("xf1", [R, QT])]
        w1h, w1l = [w.rearrange("p (k n) -> p k n", k=KT) for w in weights(keep, "w1")]
        w2h, w2l = [w.rearrange("p (j n) -> p j n", j=MT) for w in weights(keep, "w2")]
        SS = ctx.enter_context(nc.psum_tensor("squares", [128, 512], F32))
        H1 = [ctx.enter_context(nc.psum_tensor(f"hidden{j}", [128, 512], F32)) for j in range(3)]
        Y = [ctx.enter_context(nc.psum_tensor(f"down{j}", [128, 512], F32)) for j in range(KT)]

        x_in = [sem("xp_in0"), sem("xp_in1")]
        y_out = [sem("y_out0"), sem("y_out1")]
        ss_mm, fc1_mm, down_mm = sem("ss_mm2"), sem("fc1_mm"), sem("down_mm")
        sq_sb, ln_sb, ry_sb, hh_sb, g_sb, yt_sb = [sem(n + "_m") for n in ("sq_sb", "ln_sb", "ry_sb", "hh_sb", "g_sb", "yt_sb")]
        ms_sb, newton, rs_sb, h_sb, hl_sb, gh_sb, gl_sb = [sem(n + "_m") for n in ("ms_sb", "newton", "rs_sb", "h_sb", "hl_sb", "gh_sb", "gl_sb")]
        t_sb, y_sb, added = sem("t_sb_m"), sem("y_sb_m"), sem("added_m")

        def pair_vector(name, m, b, per, k):
            return vector(keep[name], m, 2 * per, b * per + k)

        block = ctx.enter_context(nc.Block())

        @block.sync
        def _(sp):
            sp.sem_inc(x_in[0], 80)
            for p in range(2):
                sp.wait_ge(keep["x2_out"][p], 16 * NP + 16)

            def load(m):
                p = m[1] % 2
                wait(sp, y_sb, at(m, 1, -1))
                load_pair(sp, dram, m, xp[p], xf[p], x_in[p])

            def body(batch, _centre):
                fr, back = batch(1), batch(-1)
                if fr is not None and not (fr[0] is None and fr[1] == 0):
                    load(fr)
                if back is not None:
                    p, s = back[1] % 2, bass.ds(number(back) * 2, 2)
                    sp.wait_ge(y_sb, at(back, 1, 1))
                    for k in range(2):
                        sp.dma_start(out[s, k * R:(k + 1) * R].rearrange("b r t -> r b t"), ys[p][:, k]).then_inc(y_out[p], 16)
                    for q in range(4):
                        b = bass.ds(number(back) * 2 + q // 2, 1)
                        sp.dma_start(out[b, 2 * R:, (q % 2) * QT:(q % 2 + 1) * QT].rearrange("b r t -> (b r) t"),
                                     ysf[p][REST * q:REST * (q + 1)]).then_inc(y_out[p], 16)

            slots(sp, NP, 1, body)
            for p in range(2):
                sp.wait_ge(y_out[p], 96 * NP // 2)

        @block.gpsimd
        def _(pool):
            def body(batch, _centre):
                fr, mid = batch(1), batch(0)
                if fr is not None:
                    pool.wait_ge(sq_sb, at(fr, 1, 1))
                    nc.gpsimd.tensor_tensor(sqa[:], sq[:, 0], sq[:, 1], ALU.add).then_inc(added, 1)
                    pool.wait_ge(added, at(fr, 2, 1))
                    nc.gpsimd.tensor_tensor(sqa[:], sqa[:], sq[:, 2], ALU.add).then_inc(added, 1)
                    pool.wait_ge(rs_sb, at(fr, 1, 1))
                    nc.gpsimd.tensor_tensor(h[:].rearrange("r k b t -> r k (b t)"), xp[fr[1] % 2][:].rearrange("r k b t -> r k (b t)"),
                                            rs[:, None, :].broadcast_to([R, KT, T2]), ALU.mult).then_inc(t_sb, 1)
                if mid is not None:
                    p = mid[1] % 2
                    wait(pool, y_out[p], uses(mid, 96, 0))
                    pool.wait_ge(x_in[p], uses(mid, 80, 80))
                    for k in range(2):
                        pool.wait_ge(yt_sb, at(mid, 6, 2 * k + 2))
                        nc.gpsimd.tensor_tensor(ys[p][:, k], yt[:, k], xp[p][:, k], ALU.add)
                    pool.wait_ge(yt_sb, at(mid, 6, 6))
                    nc.gpsimd.tensor_tensor(ysf[p][:], yf[:], xf[p][:], ALU.add).then_inc(y_sb, 1)

            slots(pool, NP, 1, body)

        @block.scalar
        def _(act):
            def hidden(mid, j):
                act.wait_ge(fc1_mm, at(mid, MT, j + 1))
                wait(act, gl_sb, at(mid, MT, j - 2))
                nc.scalar.activation(g[j % 3][:], H1[j % 3][:], ACT.Gelu_apprx_tanh, bias=b1[:, j:j + 1],
                                     scale=1.0 / WS).then_inc(g_sb, 1)

            def body(batch, _centre):
                fr, mid = batch(1), batch(0)
                if mid is not None:
                    hidden(mid, 0)
                    hidden(mid, 1)
                    hidden(mid, 2)
                if fr is not None:
                    act.wait_ge(x_in[fr[1] % 2], uses(fr, 80, 80))
                    x = xp[fr[1] % 2][:].rearrange("r k b t -> r k (b t)")
                    nc.scalar.activation(sq[:, 0:2], x[:, 0:2], ACT.Square)
                    nc.scalar.activation(sq[:, 2], x[:, 2], ACT.Square, scale=0.5).then_inc(sq_sb, 1)
                if mid is not None:
                    hidden(mid, 3)
                    hidden(mid, 4)
                if fr is not None:
                    nc.scalar.preload_act_table_set("natural_log_exp_and_others")
                    act.wait_ge(ms_sb, at(fr, 1, 1))
                    nc.scalar.activation(ln[:], ms[:], ACT.Ln, scale=RS * RS).then_inc(ln_sb, 1)
                    act.wait_ge(ln_sb, at(fr, 1, 1))
                    nc.scalar.activation(ry[:], ln[:], ACT.Exp, scale=-0.5).then_inc(ry_sb, 1)
                if mid is not None:
                    hidden(mid, 5)
                    hidden(mid, 6)
                    hidden(mid, 7)
                if fr is not None:
                    act.wait_ge(h_sb, at(fr, 6, 6))
                    nc.scalar.activation(hh[fr[1] % 2][:].rearrange("r k (b t) -> r k b t", b=2), h[:], ACT.Copy).then_inc(hh_sb, 1)
                if mid is not None:
                    hidden(mid, 8)
                    p = mid[1] % 2
                    wait(act, y_sb, at(mid, 1, 0))
                    for k in range(2):
                        act.wait_ge(down_mm, at(mid, KT, k + 1))
                        for b in range(2):
                            nc.scalar.activation(yt[:, k, b], Y[k][:, b * T:b * T + T], ACT.Identity,
                                                 bias=pair_vector("gb", mid, b, GT, k), scale=pair_vector("gate", mid, b, 2 * GT, GT + k)).then_inc(yt_sb, 1)
                    act.wait_ge(down_mm, at(mid, KT, KT))
                    for b in range(2):
                        half = slice(64 * b, 64 * b + 64)
                        nc.scalar.activation(yf[half], Y[2][half, 0:QT], ACT.Identity,
                                             bias=pair_vector("gb", mid, b, GT, 2)[half],
                                             scale=pair_vector("gate", mid, b, 2 * GT, GT + 2)[half]).then_inc(yt_sb, 1)

            slots(act, NP, 1, body)

        @block.vector
        def _(dve):
            def modulate(fr, parts):
                dve.wait_ge(t_sb, at(fr, 1, 1))
                for n in parts:
                    k, b = n // 2, n % 2
                    nc.vector.tensor_scalar(h[:, k, b], h[:, k, b], pair_vector("ab", fr, b, 2 * AB, AB + k),
                                            pair_vector("ab", fr, b, 2 * AB, AB + KT + k), ALU.mult, ALU.add).then_inc(h_sb, 1)

            def halves(mid, j):
                dve.wait_ge(g_sb, at(mid, MT, j + 1))
                nc.vector.tensor_copy(gh[:, j], g[j % 3][:]).then_inc(gh_sb, 1)
                dve.wait_ge(gh_sb, at(mid, MT, j + 1))
                nc.vector.tensor_tensor(gl[:, j], g[j % 3][:], gh[:, j], ALU.subtract).then_inc(gl_sb, 1)

            def body(batch, _centre):
                fr, mid = batch(1), batch(0)
                if mid is not None:
                    halves(mid, 0)
                    halves(mid, 1)
                    halves(mid, 2)
                    halves(mid, 3)
                if fr is not None:
                    dve.wait_ge(ss_mm, at(fr, 1, 1))
                    nc.vector.tensor_scalar(ms[:], SS[:], GUARD, None, ALU.max).then_inc(ms_sb, 1)
                if mid is not None:
                    halves(mid, 4)
                if fr is not None:
                    p = fr[1] % 2
                    dve.wait_ge(ry_sb, at(fr, 1, 1))
                    dve.wait_ge(ms_sb, at(fr, 1, 1))
                    nc.vector.scalar_tensor_tensor(ru[:], ms[:], -0.5 * RS * RS, ry[:], ALU.mult, ALU.mult).then_inc(newton, 1)
                    dve.wait_ge(newton, at(fr, 2, 1))
                    nc.vector.tensor_tensor(rv[:], ru[:], ry[:], ALU.mult).then_inc(newton, 1)
                    dve.wait_ge(newton, at(fr, 2, 2))
                    nc.vector.scalar_tensor_tensor(rs[:], rv[:], 1.5, ry[:], ALU.add, ALU.mult).then_inc(rs_sb, 1)
                if mid is not None:
                    halves(mid, 5)
                if fr is not None:
                    modulate(fr, (0, 1, 2))
                if mid is not None:
                    halves(mid, 6)
                if fr is not None:
                    modulate(fr, (3, 4, 5))
                if mid is not None:
                    halves(mid, 7)
                    halves(mid, 8)
                if fr is not None:
                    dve.wait_ge(hh_sb, at(fr, 1, 1))
                    v, low = h[:].rearrange("r k b t -> r k (b t)"), slice(REST, 2 * REST)
                    nc.vector.tensor_tensor(hl[p][:], v[:, 0:2], hh[p][:, 0:2], ALU.subtract)
                    nc.vector.tensor_tensor(hh[p][low, 2], v[low, 2], hh[p][low, 2], ALU.subtract).then_inc(hl_sb, 1)

            slots(dve, NP, 1, body)

        @block.tensor
        def _(pe):
            def up(mid, j):
                p = mid[1] % 2
                if j == 0:
                    pe.wait_ge(hl_sb, at(mid, 1, 1))
                wait(pe, g_sb, at(mid, MT, j - 2))
                c = slice(128 * j, 128 * j + 128)
                terms = [(w, x, k) for k in range(2) for w, x in ((w1h, hh[p]), (w1h, hl[p]), (w1l, hh[p]))] + [(w1h, hh[p], 2)]
                for n, (w, x, k) in enumerate(terms):
                    mm = nc.tensor.matmul(H1[j % 3][:], w[:, k, c], x[:, k], start=(n == 0), stop=(n == 6))
                mm.then_inc(fc1_mm, 1)

            def down(mid, j):
                pe.wait_ge(gl_sb, at(mid, MT, j + 1))
                if j == 0:
                    wait(pe, yt_sb, at(mid, 6, 0))
                terms = ((w2h, gh), (w2h, gl), (w2l, gh))
                for k in range(2):
                    c = slice(k * R, k * R + R)
                    for n, (w, x) in enumerate(terms):
                        mm = nc.tensor.matmul(Y[k][:], w[:, j, c], x[:, j], start=(j == 0 and n == 0), stop=(j == MT - 1 and n == 2))
                    if j == MT - 1:
                        mm.then_inc(down_mm, 1)
                c = slice(2 * R, 2 * R + REST)
                for n, (w, x) in enumerate(terms):
                    for q in range(4):
                        mm = nc.tensor.matmul(Y[2][REST * q:REST * (q + 1), 0:QT], w[:, j, c], x[:, j, q * QT:(q + 1) * QT],
                                              start=(j == 0 and n == 0), stop=(j == MT - 1 and n == 2), skip_group_check=True)
                if j == MT - 1:
                    mm.then_inc(down_mm, 1)

            def body(batch, _centre):
                fr, mid = batch(1), batch(0)
                if mid is not None:
                    up(mid, 0)
                    up(mid, 1)
                    up(mid, 2)
                    down(mid, 0)
                    up(mid, 3)
                    down(mid, 1)
                    up(mid, 4)
                    down(mid, 2)
                if fr is not None:
                    pe.wait_ge(added, at(fr, 2, 2))
                    wait(pe, ms_sb, at(fr, 1, 0))
                    nc.tensor.matmul(SS[:], keep["ones"][:], sqa[:], start=True, stop=True).then_inc(ss_mm, 1)
                if mid is not None:
                    for j in range(5, MT):
                        up(mid, j)
                        down(mid, j - 2)
                    down(mid, MT - 2)
                    down(mid, MT - 1)

            slots(pe, NP, 1, body)


def build(nc, io, out):
    dram = {
        "A": nc.dram_tensor("skew_d", (B, D * D), F32, kind="Internal").ap(),
        "x2": nc.dram_tensor("x2_d", (B, R, KT, T), F32, kind="Internal").ap(),
    }
    with ExitStack() as ctx:
        def sb(name, shape, dt=F32):
            return ctx.enter_context(nc.sbuf_tensor(name, shape, dt))

        keep = {"U": sb("U", [R, KT, 3 * D]), "G": sb("G", [128, NP, W]), "ones": sb("ones", [R, R]), "wh": sb("wh", [128, WALL], F16), "wl": sb("wl", [128, WALL], F16)}
        keep |= {"ab": sb("ab", [R, B * 2 * AB]), "gate": sb("gate", [R, B * 2 * GT]), "gb": sb("gb", [R, B * GT])}
        prepare(nc, io, dram, keep)
        keep |= {"xp": sb("xp0", [R, KT, 2, T]), "xf": sb("xf0", [R, T // 2]), "b1": sb("b1s", [128, MT])}
        keep |= {"x2s": [sb(f"x2s{p}", [R, KT, T]) for p in range(2)],
                 "x2_out": [ctx.enter_context(nc.semaphore(f"x2_out{p}")) for p in range(2)]}
        attention(nc, io, dram, keep)
        mlp(nc, io, dram, keep, out)


def kernel(**inputs):
    import numpy as np
    import concourse.bacc as bacc
    from concourse.bass_utils import run_bass_kernel_spmd

    a = {k: np.asarray(v) for k, v in inputs.items()}

    def rows(w):
        return np.ascontiguousarray(w.T.reshape(KT, CR, -1).transpose(1, 0, 2))

    place = np.concatenate([np.arange(2 * R), np.tile(np.arange(2 * R, N), R // REST)])

    def tiles(w):
        return w[..., place, :].reshape(w.shape[:-2] + (KT, R, -1)).swapaxes(-2, -3)

    def grid(w):
        iu, ju = np.triu_indices(D, k=1)
        at = np.zeros((D, D), np.int64)
        at[iu, ju] = at[ju, iu] = np.arange(len(iu))
        return w[at.reshape(-1)]

    wp = np.zeros((4, 32, 4, W), np.float32)
    heads = a["L1_cond_proj_w"].T.reshape(4, 4, HD, N)
    wp[:, 0:HD] = heads.transpose(1, 2, 0, 3)[..., place]
    wp[0, HD, 0] = a["L1_cond_proj_b"][place]
    w2 = a["L1_cond_fc2_w"].T[:, place].reshape(MT, 128, W).transpose(1, 0, 2)
    parts = (tiles(a["L1_cond_qkv_w"].T), wp, tiles(a["L1_cond_fc1_w"].T), w2)
    modulation = (np.arange(6)[:, None] * N + place).reshape(-1)
    arrays = {
        "x": np.ascontiguousarray(tiles(a["x"].swapaxes(1, 2))),
        "condT": rows(a["cond_1152"]),
        "PT": np.ascontiguousarray(np.concatenate([a["L0_cond_P"].T] * 2)),
        "WT": rows(grid(a["L0_cond_W"])),
        "bfull": grid(a["L0_cond_b"])[None],
        "adaT": rows(a["L1_cond_ada_w"][modulation]),
        "adab": np.ascontiguousarray(a["L1_cond_ada_b"][modulation].reshape(MODS, R).T),
        "weights": np.ascontiguousarray(np.concatenate([w.reshape(128, -1) for w in parts], axis=1)),
        "bq": a["L1_cond_qkv_b"][None],
        "b1": np.ascontiguousarray(a["L1_cond_fc1_b"].reshape(MT, 128).T),
        "b2": np.ascontiguousarray(a["L1_cond_fc2_b"][place].reshape(KT, R).T),
    }
    for n in ("g1", "g2", "qg", "kg"):
        arrays[n] = a["L1_cond_" + n][None]
    nc = bacc.Bacc("TRN2", target_bir_lowering=False, num_devices=1)
    io = {k: nc.dram_tensor(k + "_in", v.shape, F32, kind="ExternalInput").ap() for k, v in arrays.items()}
    out = nc.dram_tensor("y_out", (B, N, T), F32, kind="ExternalOutput").ap()
    build(nc, io, out)
    r = run_bass_kernel_spmd(nc, [{k + "_in": v for k, v in arrays.items()}], core_ids=[0])
    y = r.results[0]["y_out"]
    return np.ascontiguousarray(y.swapaxes(1, 2))
```
